# Optimizing a Trainium2 kernel written in Bass

```python
import numpy as np
import jax
import jax.numpy as jnp

def _softmax(x, axis=-1):
    return jax.nn.softmax(x, axis=axis)

def _gelu(x):
    return jax.nn.gelu(x, approximate=True)

def _silu(x):
    return jax.nn.silu(x)

def _sigmoid(x):
    return jax.nn.sigmoid(x)

def _layernorm(x, axis=-1, eps=1e-05):
    m = jnp.mean(x, axis=axis, keepdims=True)
    v = jnp.var(x, axis=axis, keepdims=True)
    return (x - m) / jnp.sqrt(v + eps)

def _scatter_add(tgt, idx, src, axis=0):
    return tgt.at[idx].add(src)

def _segment_sum(src, seg, n):
    return jax.ops.segment_sum(src, seg, n)
kernel_name = 'mk_xattn_seq_d2_seqx_r4_074207'

def setup_inputs(seed: int=0):
    np.random.seed(seed)
    _w = jnp.asarray

    def _rec_inputs():
        import jax
        import jax.numpy as jnp
        _rk = jax.random.key(seed)
        x = 0.0002279 + 0.9999 * jax.random.normal(jax.random.fold_in(_rk, 1), (2, 512, 1024), jnp.float32)
        _lenS = 512 - jax.random.randint(jax.random.fold_in(_rk, 7), (2,), 0, max(1, 512 // 4) + 1, jnp.int32)
        _lenS2 = 1024 - jax.random.randint(jax.random.fold_in(_rk, 8), (2,), 0, max(1, 1024 // 4) + 1, jnp.int32)
        _ctx_4096P = jax.random.normal(jax.random.fold_in(_rk, 11), (2, 16, 1024), jnp.float32)
        _ctx_4096c = jax.random.dirichlet(jax.random.fold_in(_rk, 511), 0.3 * jnp.ones((16,), jnp.float32), (2, 1024))
        _ctx_4096t = jnp.einsum('bsk,bkd->bsd', _ctx_4096c, _ctx_4096P)
        _ctx_4096t = _ctx_4096t * jax.lax.rsqrt(jnp.mean(jnp.square(_ctx_4096t)) + 1e-12) * 0.953939
        ctx_4096 = -0.000702761 + 1.00443 * (_ctx_4096t + 0.3 * jax.random.normal(jax.random.fold_in(_rk, 611), (2, 1024, 1024), jnp.float32))
        fside_BxSxS_0 = -0.000132966 + 0.0502041 * jax.random.normal(jax.random.fold_in(_rk, 12), (2, 512, 512), jnp.float32)
        return (x, ctx_4096, fside_BxSxS_0)
    x, ctx_4096, fside_BxSxS_0 = _rec_inputs()

    def _L0_xattn_setup():
        import jax, jax.numpy as jnp
        import numpy as np
        K = 8
        NUM_BLOCKS = 4
        SLOPE = 0.01

        def _lrelu(x):
            return jnp.where(x >= 0, x, SLOPE * x)

        def _knn_indices(xyz, k):
            sq = jnp.sum(xyz * xyz, axis=1)
            d2 = sq[:, :, None] + sq[:, None, :] - 2.0 * jnp.einsum('bdn,bdm->bnm', xyz, xyz)
            _, idx = jax.lax.top_k(-d2, k)
            return idx

        def _group_point(p, idx_t):
            return jnp.take_along_axis(p[:, :, None, :], idx_t, axis=3)
        key = jax.random.key(seed)
        k1, k2, k3, k4 = jax.random.split(key, 4)
        b, n, d = (4, 1024, 64)
        xyz = jax.random.normal(k1, (b, 3, n), dtype=jnp.float32)
        points = jax.random.normal(k2, (b, d, n), dtype=jnp.float32)
        w_center = jax.random.normal(k3, (NUM_BLOCKS, d, d), dtype=jnp.float32) * 0.05
        w_neighbor = jax.random.normal(k4, (NUM_BLOCKS, d, d), dtype=jnp.float32) * 0.05
        return {'xyz': xyz, 'points': points, 'w_center': w_center, 'w_neighbor': w_neighbor}
    _L0_xattn_all = _L0_xattn_setup()
    _L0_xattn_in = {k: v for k, v in _L0_xattn_all.items() if k in ()}
    del _L0_xattn_all

    def _L1_xattn_setup():
        import jax, jax.numpy as jnp
        import numpy as np
        B, N, C, K = (8, 1024, 64, 30)
        EPS_BN = 1e-05
        TINY = 1e-20

        def _knn(p, k):
            xx = jnp.sum(p * p, axis=1)
            pd = 2.0 * jnp.einsum('bdn,bdm->bnm', p, p) - xx[:, :, None] - xx[:, None, :]
            return jax.lax.top_k(pd, k)[1]

        def _bn(h, g, b):
            mu = jnp.mean(h, axis=(0, 1, 2), keepdims=True)
            var = jnp.var(h, axis=(0, 1, 2), keepdims=True)
            return (h - mu) * jax.lax.rsqrt(var + EPS_BN) * g + b

        def _forward(x_loc, x, W1, g1, b1, W2, g2, b2, W3, g3, b3, k):
            Bsz = x.shape[0]
            idx = _knn(x_loc, k)
            bidx = jnp.arange(Bsz)[:, None, None]
            pts = x_loc.transpose(0, 2, 1)
            rel = pts[bidx, idx] - pts[:, :, None, :]
            xr, yr, zr = (rel[..., 0], rel[..., 1], rel[..., 2])
            sxy2 = xr * xr + yr * yr
            r2 = sxy2 + zr * zr
            rho = jnp.sqrt(jnp.maximum(r2, TINY))
            sxy = jnp.sqrt(jnp.maximum(sxy2, TINY))
            deg_r = r2 < TINY
            deg_p = sxy2 < TINY
            theta = jnp.arctan2(jnp.where(deg_r, 0.0, zr), jnp.where(deg_r, 1.0, sxy))
            phi = jnp.arctan2(jnp.where(deg_p, 0.0, yr), jnp.where(deg_p, 1.0, xr))
            sph = jnp.stack([rho, theta, phi], axis=-1)
            feat = jnp.concatenate([sph, sph - jnp.mean(sph, axis=-1, keepdims=True)], axis=-1)
            lrelu = lambda h: jax.nn.leaky_relu(h, 0.2)
            h = lrelu(_bn(feat @ W1.T, g1, b1))
            h = lrelu(_bn(h @ W2.T, g2, b2))
            h = lrelu(_bn(h @ W3.T, g3, b3))
            att = jax.nn.softmax(h[..., 0], axis=-1)
            xk = x.transpose(0, 2, 1)[bidx, idx]
            agg = jnp.einsum('bnkc,bnk->bnc', xk, att)
            return x + agg.transpose(0, 2, 1)
        key = jax.random.key(seed)
        ks = jax.random.split(key, 12)
        return {'x_loc': jax.random.normal(ks[0], (B, 3, N), jnp.float32), 'x': jax.random.normal(ks[1], (B, C, N), jnp.float32), 'W1': jax.random.normal(ks[2], (6, 6), jnp.float32) * 0.4, 'g1': 1.0 + 0.1 * jax.random.normal(ks[3], (6,), jnp.float32), 'b1': 0.1 * jax.random.normal(ks[4], (6,), jnp.float32), 'W2': jax.random.normal(ks[5], (3, 6), jnp.float32) * 0.4, 'g2': 1.0 + 0.1 * jax.random.normal(ks[6], (3,), jnp.float32), 'b2': 0.1 * jax.random.normal(ks[7], (3,), jnp.float32), 'W3': jax.random.normal(ks[8], (1, 3), jnp.float32) * 0.4, 'g3': 1.0 + 0.1 * jax.random.normal(ks[9], (1,), jnp.float32), 'b3': 0.1 * jax.random.normal(ks[10], (1,), jnp.float32), 'k': K}
    _L1_xattn_all = _L1_xattn_setup()
    _L1_xattn_in = {k: v for k, v in _L1_xattn_all.items() if k in ('W1', 'g1', 'b1', 'W2', 'g2', 'b2', 'W3', 'g3', 'b3')}
    del _L1_xattn_all
    return {'x': x, 'ctx_4096': ctx_4096, 'fside_BxSxS_0': fside_BxSxS_0, 'L1_xattn_W1': _L1_xattn_in['W1'], 'L1_xattn_g1': _L1_xattn_in['g1'], 'L1_xattn_b1': _L1_xattn_in['b1'], 'L1_xattn_W2': _L1_xattn_in['W2'], 'L1_xattn_g2': _L1_xattn_in['g2'], 'L1_xattn_b2': _L1_xattn_in['b2'], 'L1_xattn_W3': _L1_xattn_in['W3'], 'L1_xattn_g3': _L1_xattn_in['g3'], 'L1_xattn_b3': _L1_xattn_in['b3']}

def reference(x, ctx_4096, fside_BxSxS_0, L1_xattn_W1, L1_xattn_g1, L1_xattn_b1, L1_xattn_W2, L1_xattn_g2, L1_xattn_b2, L1_xattn_W3, L1_xattn_g3, L1_xattn_b3):
    import jax
    import jax.numpy as jnp

    def _L0_xattn_ref(xyz, points, w_center, w_neighbor):
        import jax, jax.numpy as jnp
        import numpy as np
        K = 8
        NUM_BLOCKS = 4
        SLOPE = 0.01

        def _lrelu(x):
            return jnp.where(x >= 0, x, SLOPE * x)

        def _knn_indices(xyz, k):
            sq = jnp.sum(xyz * xyz, axis=1)
            d2 = sq[:, :, None] + sq[:, None, :] - 2.0 * jnp.einsum('bdn,bdm->bnm', xyz, xyz)
            _, idx = jax.lax.top_k(-d2, k)
            return idx

        def _group_point(p, idx_t):
            return jnp.take_along_axis(p[:, :, None, :], idx_t, axis=3)
        idx = _knn_indices(xyz, K)
        idx_t = jnp.transpose(idx, (0, 2, 1))[:, None, :, :]
        for i in range(NUM_BLOCKS):
            shortcut = points
            p = _lrelu(points)
            g = _group_point(p, idx_t)
            c = jnp.einsum('oi,bin->bon', w_center[i], p)
            gn = jnp.einsum('oi,bikn->bokn', w_neighbor[i], g)
            points = (c + gn.sum(axis=2)) / (K + 1.0) + shortcut
        return points

    def _L1_xattn_ref(x_loc, x, W1, g1, b1, W2, g2, b2, W3, g3, b3, k):
        import jax, jax.numpy as jnp
        import numpy as np
        B, N, C, K = (8, 1024, 64, 30)
        EPS_BN = 1e-05
        TINY = 1e-20

        def _knn(p, k):
            xx = jnp.sum(p * p, axis=1)
            pd = 2.0 * jnp.einsum('bdn,bdm->bnm', p, p) - xx[:, :, None] - xx[:, None, :]
            return jax.lax.top_k(pd, k)[1]

        def _bn(h, g, b):
            mu = jnp.mean(h, axis=(0, 1, 2), keepdims=True)
            var = jnp.var(h, axis=(0, 1, 2), keepdims=True)
            return (h - mu) * jax.lax.rsqrt(var + EPS_BN) * g + b

        def _forward(x_loc, x, W1, g1, b1, W2, g2, b2, W3, g3, b3, k):
            Bsz = x.shape[0]
            idx = _knn(x_loc, k)
            bidx = jnp.arange(Bsz)[:, None, None]
            pts = x_loc.transpose(0, 2, 1)
            rel = pts[bidx, idx] - pts[:, :, None, :]
            xr, yr, zr = (rel[..., 0], rel[..., 1], rel[..., 2])
            sxy2 = xr * xr + yr * yr
            r2 = sxy2 + zr * zr
            rho = jnp.sqrt(jnp.maximum(r2, TINY))
            sxy = jnp.sqrt(jnp.maximum(sxy2, TINY))
            deg_r = r2 < TINY
            deg_p = sxy2 < TINY
            theta = jnp.arctan2(jnp.where(deg_r, 0.0, zr), jnp.where(deg_r, 1.0, sxy))
            phi = jnp.arctan2(jnp.where(deg_p, 0.0, yr), jnp.where(deg_p, 1.0, xr))
            sph = jnp.stack([rho, theta, phi], axis=-1)
            feat = jnp.concatenate([sph, sph - jnp.mean(sph, axis=-1, keepdims=True)], axis=-1)
            lrelu = lambda h: jax.nn.leaky_relu(h, 0.2)
            h = lrelu(_bn(feat @ W1.T, g1, b1))
            h = lrelu(_bn(h @ W2.T, g2, b2))
            h = lrelu(_bn(h @ W3.T, g3, b3))
            att = jax.nn.softmax(h[..., 0], axis=-1)
            xk = x.transpose(0, 2, 1)[bidx, idx]
            agg = jnp.einsum('bnkc,bnk->bnc', xk, att)
            return x + agg.transpose(0, 2, 1)
        return _forward(x_loc, x, W1, g1, b1, W2, g2, b2, W3, g3, b3, k)
    x = _L0_xattn_ref(ctx_4096, x, fside_BxSxS_0, fside_BxSxS_0)
    x = _L1_xattn_ref(ctx_4096, x, L1_xattn_W1, L1_xattn_g1, L1_xattn_b1, L1_xattn_W2, L1_xattn_g2, L1_xattn_b2, L1_xattn_W3, L1_xattn_g3, L1_xattn_b3, 30)
    return x

_drawn_inputs = setup_inputs


def setup_inputs(seed=0):
    import zlib

    import numpy as np

    out = dict(_drawn_inputs(seed))
    spreads = {}
    factors = {}
    for name, (base, spread) in spreads.items():
        noise = np.random.default_rng([zlib.crc32(name.encode()), seed]).standard_normal(out[name].shape)
        drawn = base * np.exp(spread * noise) if base else spread * noise
        out[name] = jnp.asarray(drawn.astype(out[name].dtype))
    for name, factor in factors.items():
        out[name] = (out[name] * factor).astype(out[name].dtype)
    return out
```

```python
from contextlib import ExitStack

import numpy as np
import concourse.bass as bass
from concourse import mybir

F32 = mybir.dt.float32
F32R = mybir.dt.float32r
BF16 = mybir.dt.bfloat16
U32 = mybir.dt.uint32
ALU = mybir.AluOpType
ACT = mybir.ActivationFunctionType
AX_X = mybir.AxisListType.X

P = 128
HALF = 512
K0 = 8
K1 = 30
KP = 32
BLOCKS = 4
SLOPE0 = 0.01
SLOPE1 = 0.2
EPS_BN = 1e-5
TINY = 1e-20
REMOVED = -3.0e38
PI = float(np.pi)


def build(nc, x, ctx, fside, W1, g1, b1, W2, g2, b2, W3, g3, b3, out):
    B, C, N = x.shape
    D = ctx.shape[1]
    CT = C // P
    KT = D // P
    NT = N // P
    TILES = B * NT
    NH = N // HALF
    AB = N // P
    CH = 4
    CHUNKS = TILES // CH
    ITS = B * BLOCKS
    GN = 8
    NG = P // GN
    NS = 6
    U = TILES * K1

    with ExitStack() as st:
        def sb(name, shape, dt):
            return st.enter_context(nc.sbuf_tensor(name, shape, dt))

        def sem(name):
            return st.enter_context(nc.semaphore(name))

        pts_h = sb("pts_h", [P, KT, N], F32R)
        pts_l = sb("pts_l", [P, KT, N], F32R)
        nbr = sb("nbr", [P, B, NT, N], F32R)
        X = sb("X", [P, B, CT, N], F32)
        wT = sb("wT", [P, 2, CT, C], F32R)
        scratch = sb("scratch", [P, 11 * U + 2 * HALF], F32)
        ident = sb("ident", [P, P], F32)
        ident_b = sb("ident_b", [P, P], BF16)
        neg_half = sb("neg_half", [P, P], F32)
        mean_mat = sb("mean_mat", [P, P], F32)
        iota_r = sb("iota_r", [P, KP], F32)
        part = sb("part", [P, 1], F32)
        slot_t = sb("slot_t", [P, 1], F32)
        att_h12 = sb("att_h12", [P, P], F32R)
        vals = sb("vals", [P, 2, KP], F32)
        idx = sb("idx", [P, TILES, KP], U32)
        own = sb("own", [P, 3, TILES], F32)
        tab = sb("tab", [P, B, 3, AB], F32)
        tab_rest = sb("tab_rest", [P, B, 3, AB], F32)
        tab_p = sb("tab_p", [P, 3, B, 3, AB], BF16)
        a_row = sb("a_row", [P, P], BF16)
        prm = sb("prm", [P, 77], F32)
        w_eff = sb("w_eff", [P, 6, 3], F32)
        stat = sb("stat", [P, 64], F32)
        small = sb("small", [P, 64], F32)

        a_rows = nc.dram_tensor("a_rows", [CHUNKS, P, P], BF16, kind="Internal").ap()
        att_d = nc.dram_tensor("att_d", [CHUNKS, P, NG * HALF], F32, kind="Internal").ap()
        w1_keep = nc.dram_tensor("w1_keep", [P, 2 * CT * C], F32, kind="Internal").ap()

        bank = [st.enter_context(nc.psum_tensor(f"bank{i}", [P, HALF], F32)) for i in range(8)]

        x_flat = X[:].rearrange("p b c n -> p (b c n)")
        stage = x_flat[:, 0:NS * N].rearrange("p (s n) -> p s n", s=NS)
        sq_half = [x_flat[:, (NS + b) * N:(NS + b + 1) * N] for b in range(B)]
        score = scratch[:, 0:2 * N].rearrange("p (s n) -> p s n", s=2)
        adj = scratch[:, 2 * N:3 * N].bitcast(BF16).rearrange("p (s n) -> p s n", s=2)
        w_raw = [scratch[:, 4096:6144].rearrange("p (t c) -> p t c", t=CT),
                 scratch[:, 2048:4096].rearrange("p (t c) -> p t c", t=CT)]
        p_h, p_l = pts_h[:, 0:CT, :], pts_h[:, CT:2 * CT, :]
        y_h = pts_l[:, 0:CT, :].rearrange("p c n -> p (c n)").rearrange("p (m o) -> p m o", m=NT)
        y_l = pts_l[:, CT:2 * CT, :].rearrange("p c n -> p (c n)").rearrange("p (m o) -> p m o", m=NT)
        NB = 3
        KH = K1 // 2
        near = scratch[:, 0:3 * U].rearrange("p (j t k) -> p j t k", j=3, t=TILES)
        oh_r = scratch[:, 1440:1500].bitcast(BF16).rearrange("p (k r) -> p k r", k=KH)
        r_all = scratch[:, 1500:1756].bitcast(BF16).rearrange("p (t k) -> p t k", t=TILES)
        i_u = scratch[:, 1756:1884].bitcast(U32)
        a_f = scratch[:, 1884:2012]
        pick = scratch[:, 2012:2372].rearrange("p (k j r) -> p k j r", k=KH, j=3)
        bc = scratch[:, 2372:5252].bitcast(BF16).rearrange("p (s f) -> p s f", s=NB)
        att32 = scratch[:, 2400:2912].rearrange("p (t k) -> p t k", t=TILES)
        a_all = scratch[:, 2912:3424]
        r4_all = scratch[:, 3424:3936]
        i_all = scratch[:, 3936:4448].bitcast(U32)
        l_tmp = scratch[:, 4864:4992]
        aT = scratch[:, 0:256].bitcast(BF16)
        rT = scratch[:, 256:512].bitcast(BF16)
        att_q = scratch[:, 512:1536].bitcast(BF16).rearrange("p (i h n) -> p i h n", i=2, h=2)
        oa = [scratch[:, 1536 + 512 * i:2048 + 512 * i].bitcast(BF16).rearrange("p (a n) -> p a n", n=GN)
              for i in range(2)]
        eq = [scratch[:, 2560 + 128 * i:2688 + 128 * i].bitcast(BF16).rearrange("p (r n) -> p r n", n=GN)
              for i in range(2)]
        mv = [scratch[:, 2816 + 512 * i:3328 + 512 * i].bitcast(BF16)
              .rearrange("p (i h r n) -> p i h r n", n=GN, i=2, h=2) for i in range(2)]
        iota_a8 = idx[:].rearrange("p t k -> p (t k)").bitcast(BF16).rearrange("p (a n) -> p a n", n=GN)
        iota_r8 = scratch[:, 4992:5120].bitcast(BF16).rearrange("p (r n) -> p r n", n=GN)
        spread_s = [scratch[:, 3840 + 512 * i:4352 + 512 * i] for i in range(2)]
        w_flat = wT[:].rearrange("p h t c -> p (h t c)")
        att_flat = [nbr[:, i].rearrange("p m n -> p (m n)") for i in range(2)]
        att_T = [a.rearrange("p (q h r x) -> p h r q x", q=NG, h=2, r=AB) for a in att_flat]
        xT = [t[:].rearrange("p k n -> p (k n)").rearrange("p (h r c) -> p h r c", h=2, r=AB)
              for t in (pts_h, pts_l)]

        def p32(n):
            return scratch[:, 11 * U + (n % 2) * HALF:11 * U + (n % 2 + 1) * HALF]

        def slots(a, n=1):
            return scratch[:, a * U:(a + n) * U]

        s_w = sem("w_loaded")
        s_stage = [sem(f"stage_loaded{i}") for i in range(NS)]
        s_prm = sem("params_loaded")
        s_const = sem("consts_ready")
        s_wps = sem("w_transposed")
        s_wh = sem("w_high_ready")
        s_wl = sem("w_low_ready")
        s_wkeep = sem("w1_kept")
        s_wback = sem("w1_back")
        s_ph = sem("pts_high_ready")
        s_pl0 = sem("pts0_low_ready")
        s_pl1 = sem("pts1_low_ready")
        s_sq = sem("squares_ready")
        s_sqmm = sem("squares_used")
        s_nsq = sem("sq_half_ready")
        s_kdone = sem("pts_tile_used")
        s_g = sem("gram_ready")
        s_gc = sem("gram_copied")
        s_v = sem("scores_ready")
        s_top = sem("topk_step")
        s_adj = sem("adj_ready")
        s_adjT = sem("adj_transposed")
        s_nbr = sem("nbr_ready")
        s_x = [sem(f"x{b}_loaded") for b in range(B)]
        s_p32 = sem("p_ready")
        s_p0 = sem("p_high_ready")
        s_p1 = sem("p_low_ready")
        s_wm = sem("wp_done")
        s_yh = sem("y_high_ready")
        s_yl = sem("y_low_ready")
        s_m = sem("agg_done")
        s_xu = sem("x_updated")
        s_link = sem("dve_link")
        s_af = sem("a_index_ready")
        s_aT = sem("a_index_transposed")
        s_ar = sem("a_row_ready")
        s_arow = sem("a_rows_stored")
        s_bc = [sem(f"a_broadcast{i}") for i in range(NB)]
        s_oh = sem("onehot_ready")
        s_look = sem("lookup_done")
        s_pick = sem("lookup_read")
        s_tab = sem("table_ready")
        s_mlp = sem("mlp_to_act")
        s_act = sem("act_to_mlp")
        s_bnin = sem("bn_partial_ready")
        s_bnps = sem("bn_summed")
        s_att = sem("att_ready")
        s_scT = sem("att_transposed")
        s_sct = sem("att_columns_copied")
        s_h12 = sem("att_high_rounded")
        s_attq = sem("att_parts_ready")
        s_st = [sem(f"spread_stored{i}") for i in range(2)]
        s_back = sem("attention_loaded")
        s_oa = sem("a_onehot_ready")
        s_eq = sem("r_onehot_ready")
        s_mv = [sem(f"weighted_onehot{i}_ready") for i in range(2)]
        s_iota = sem("repeated_iotas_ready")
        s_sc = sem("spread_done")
        s_scc = sem("spread_copied")
        s_xT = sem("xT_done")
        s_xTh = sem("xT_high_ready")
        s_xTl = sem("xT_low_ready")
        s_f = sem("attended")
        s_fo = sem("result_ready")
        s_out = sem("out_stored")

        TOPSTEPS = 12

        MLP = {e: n + 1 for n, e in enumerate(
            ("sqrt", "atan", "bn1s", "bn1a", "bn2s", "bn2a", "bn3s", "bn3a", "exp"))}
        DONE = {"sqrt": 1, "atan": 2, "bn1s": 3, "bn1a": 9, "bn2s": 10, "bn2a": 13, "bn3s": 14, "bn3a": 15,
                "exp": 16}
        G0 = 12
        R0 = 6
        M0 = G0 + 2 * TILES + 3
        T0 = M0 + 50
        S0 = T0 + 3
        S_END = 16 * ITS - S0
        TAIL = 4

        QUARTER = NG // 4
        FREE_AT = [13, S_END + 1, S_END + 4 * TAIL + 2, S_END + 8 * TAIL + 1]
        LOAD_AT = {}
        for c in range(CHUNKS):
            for j in range(4):
                q = max(NG * c + QUARTER * (j + 1) + 1, FREE_AT[c] + 2 * j)
                LOAD_AT.setdefault(min(q, CHUNKS * NG - 1), []).append((c, j))

        block = st.enter_context(nc.Block())

        def tail_groups(i):
            return range(min(S_END + TAIL * i, CHUNKS * NG), min(S_END + TAIL * (i + 1), CHUNKS * NG))

        def w_bank(n):
            return bank[(6, 7, 4, 5)[n % 4]][:]

        def weigh(engine, q, i):
            n0 = (q // NG) * P + (q % NG) * GN
            engine.tensor_tensor(mv[q % 2][:, i],
                                 eq[q % 2].unsqueeze(1).to_broadcast([P, 2, KP, GN]),
                                 att_q[:, i, :, n0:n0 + GN].unsqueeze(2).to_broadcast([P, 2, KP, GN]),
                                 ALU.mult).then_inc(s_mv[i], 1)

        @block.sync
        def _(sp):
            def load_stage(n):
                e = n - NS
                if 0 <= e < 2 * KT:
                    sp.wait_ge(s_sqmm, e + 1)
                if 0 <= e < KT:
                    sp.wait_ge(s_pl0, e + 1)
                if e >= 2 * KT:
                    sp.wait_ge(s_pl1, e - 2 * KT + 1)
                b, k = (0 if n < KT else 1), n % KT
                sp.dma_start(stage[:, n % NS, :], ctx[b, k * P:(k + 1) * P, :]).then_inc(s_stage[n % NS], 16)

            for n in range(KT):
                load_stage(n)
            for i in (1, 0):
                sp.dma_start(w_raw[i], fside[i].rearrange("(t p) c -> p t c", p=P)).then_inc(s_w, 16)
            for n in range(KT, KT + NS):
                load_stage(n)
            off = 0
            for w in (W1, g1, b1, W2, g2, b2, W3, g3, b3):
                n = int(np.prod(w.shape))
                flat = w.rearrange("a b -> (a b)") if len(w.shape) == 2 else w
                sp.dma_start(prm[:, off:off + n], flat.unsqueeze(0).to_broadcast([P, n])).then_inc(s_prm, 16)
                off += n
            for b in range(B):
                for j in range(3):
                    sp.dma_start(tab[:, b, j, :], ctx[b, 2 - j, :].rearrange("(a r) -> a r", r=AB)) \
                        .then_inc(s_prm, 16)
                    sp.dma_start(own[:, j, b * NT:(b + 1) * NT],
                                 ctx[b, 2 - j, :].rearrange("(t p) -> p t", p=P),
                                 allow_slow_non_contiguous=True).then_inc(s_prm, 16)
            sp.wait_ge(s_wh, CT)
            sp.wait_ge(s_wl, CT)
            sp.dma_start(w1_keep, w_flat.bitcast(F32)).then_inc(s_wkeep, 16)
            for n in range(KT + NS, 3 * KT):
                load_stage(n)
            sp.wait_ge(s_pl1, KT)
            sp.dma_start(X[:, 0], x[0].rearrange("(t p) n -> p t n", p=P)).then_inc(s_x[0], 16)
            sp.wait_ge(s_v, TILES)
            sp.dma_start(X[:, 1], x[1].rearrange("(t p) n -> p t n", p=P)).then_inc(s_x[1], 16)
            sp.wait_ge(s_adjT, TILES)
            for c in range(CHUNKS):
                sp.wait_ge(s_ar, c + 1)
                sp.dma_start(a_rows[c], a_row[:]).then_inc(s_arow, 16)
                sp.wait_ge(s_arow, 16 * (c + 1))
                for t in range(2 * CH):
                    u = 2 * CH * c + t
                    if u >= NB:
                        sp.wait_ge(s_look, u - NB + 1)
                    k = (t // 2) * KP + (t % 2) * KH
                    sp.dma_start(bc[:, u % NB, :],
                                 a_rows[c, k:k + KH, :].rearrange("k n -> (k n)").unsqueeze(0)
                                 .to_broadcast([P, KH * P])).then_inc(s_bc[u % NB], 16)

            def load_attention(c, j):
                for i in range(2):
                    sp.wait_ge(s_st[i], 16 * (NG * c + QUARTER * (j + 1)) // 2)
                if c < 2:
                    sp.wait_ge(s_m, 2 * CT * (ITS - 1 + c))
                else:
                    sp.wait_ge(s_f, CT * (c - 1))
                cols = slice(QUARTER * HALF * j, QUARTER * HALF * (j + 1))
                sp.dma_start(att_flat[c % 2][:, cols].bitcast(F32), att_d[c][:, cols]).then_inc(s_back, 16)

            for q in range(CHUNKS * NG):
                sp.wait_ge(s_scc, q + 1)
                sp.dma_start(att_d[q // NG, :, (q % NG) * HALF:(q % NG + 1) * HALF],
                             spread_s[q % 2]).then_inc(s_st[q % 2], 16)
                for c, j in LOAD_AT.get(q, []):
                    load_attention(c, j)
            for c in range(CHUNKS):
                b, hf = c // NH, c % NH
                for t in range(CT):
                    sp.wait_ge(s_fo, CT * c + t + 1)
                    sp.dma_start(out[b, t * P:(t + 1) * P, hf * HALF:(hf + 1) * HALF],
                                 X[:, b, t, hf * HALF:(hf + 1) * HALF]).then_inc(s_out, 16)
            sp.wait_ge(s_out, 16 * CHUNKS * CT)

        @block.gpsimd
        def _(pool):
            pool.memset(ident[:], 0.0).then_inc(s_const, 1)
            pool.memset(neg_half[:], -0.5).then_inc(s_const, 1)
            pool.memset(mean_mat[:], 1.0 / P).then_inc(s_const, 1)
            pool.wait_ge(s_const, 3)
            pool.affine_select(out=ident[:], in_=ident[:], compare_op=ALU.not_equal, fill=1.0, base=0,
                               pattern=[[-1, P]], channel_multiplier=1).then_inc(s_const, 1)
            pool.iota(iota_r[:], pattern=[[1, KP]], base=0, channel_multiplier=0,
                      allow_small_or_imprecise_dtypes=True).then_inc(s_const, 1)
            pool.iota(part[:], pattern=[[0, 1]], base=0, channel_multiplier=1,
                      allow_small_or_imprecise_dtypes=True).then_inc(s_const, 1)
            for t in range(CH):
                pool.wait_ge(s_const, 6 + t)
                pool.memset(slot_t[t * KP:(t + 1) * KP, :], float(t)).then_inc(s_const, 1)
            pool.wait_ge(s_const, 6 + CH)
            pool.tensor_copy(ident_b[:], ident[:]).then_inc(s_const, 1)

            def low_part(k):
                n = 2 * KT + k
                pool.wait_ge(s_stage[n % NS], 16 * (n // NS + 1))
                pool.wait_ge(s_ph, KT + k + 1)
                pool.tensor_tensor(pts_l[:, k, :], stage[:, n % NS, :], pts_h[:, k, :].bitcast(F32),
                                   ALU.subtract).then_inc(s_pl1, 1)

            def add_norm(T):
                pool.wait_ge(s_nsq, 2 * (T // NT + 1))
                pool.wait_ge(s_gc, 2 * (T + 1))
                pool.tensor_tensor(score[:, T % 2, :], score[:, T % 2, :], sq_half[T // NT],
                                   ALU.add).then_inc(s_v, 1)

            for T in range(NT - 1):
                add_norm(T)
            for k in range(3):
                low_part(k)
            add_norm(NT - 1)
            for k in range(3, KT):
                low_part(k)
            for T in range(NT, TILES):
                add_norm(T)

            def p_low(n):
                hf, t = (n % (2 * CT)) // CT, n % CT
                pool.wait_ge(s_p0, n + 1)
                pool.tensor_tensor(p_l[:, t, hf * HALF:(hf + 1) * HALF], p32(n),
                                   p_h[:, t, hf * HALF:(hf + 1) * HALF].bitcast(F32),
                                   ALU.subtract).then_inc(s_p1, 1)

            def weight(q):
                c = q // NG
                pool.wait_ge(s_eq, q + 1)
                if q % NG == 0:
                    pool.wait_ge(s_attq, c + 1)
                if q >= 2:
                    pool.wait_ge(s_sc, q - 1)
                weigh(pool, q, 1)

            for n in range(2 * CT):
                p_low(n)
            for it in range(ITS):
                for s_ in range(16):
                    g = 16 * it + s_
                    if g == T0:
                        pool.wait_ge(s_att, 1)
                        pool.iota(iota_a8, pattern=[[1, P], [0, GN]], base=0, channel_multiplier=0,
                                  allow_small_or_imprecise_dtypes=True).then_inc(s_iota, 1)
                        pool.iota(iota_r8, pattern=[[1, KP], [0, GN]], base=0, channel_multiplier=0,
                                  allow_small_or_imprecise_dtypes=True).then_inc(s_iota, 1)
                    if g >= S0:
                        weight(g - S0)
                    if s_ >= NT and it + 1 < ITS:
                        p_low(2 * CT * (it + 1) + s_ - NT)
            for q in range(S_END, CHUNKS * NG):
                weight(q)

        @block.scalar
        def _(act):
            def w_high(n):
                t = n % CT
                act.wait_ge(s_wps, n + 1)
                if n == CT:
                    act.wait_ge(s_wkeep, 16)
                act.copy(wT[:, 0, t, :], w_bank(n)).then_inc(s_wh, 1)

            def high_part(m):
                k, n = m % KT, m if m < KT else m + KT
                act.wait_ge(s_stage[n % NS], 16 * (n // NS + 1))
                if m >= KT:
                    act.wait_ge(s_kdone, k + 1)
                act.copy(pts_h[:, k, :], stage[:, n % NS, :]).then_inc(s_ph, 1)

            def square(n):
                if n < KT:
                    act.wait_ge(s_pl0, n + 1)
                else:
                    act.wait_ge(s_stage[n % NS], 16 * (n // NS + 1))
                act.activation(stage[:, n % NS, :], stage[:, n % NS, :], ACT.Square).then_inc(s_sq, 1)

            def norm_out(b):
                act.wait_ge(s_sqmm, KT * (b + 1))
                for hf in range(NH):
                    act.copy(sq_half[b][:, hf * HALF:(hf + 1) * HALF], bank[4 + hf][:]).then_inc(s_nsq, 1)

            def gram_out(T):
                if T == NT - 1:
                    act.wait_ge(s_kdone, KT)
                else:
                    act.wait_ge(s_g, T + 1 if T < NT else T)
                if T >= 2:
                    act.wait_ge(s_top, TOPSTEPS * (T - 1))
                for hf in range(NH):
                    act.copy(score[:, T % 2, hf * HALF:(hf + 1) * HALF], bank[2 * (T % 2) + hf][:]) \
                        .then_inc(s_gc, 1)

            def nbr_out(T):
                act.wait_ge(s_adjT, T + 1)
                act.copy(nbr[:, T // NT, :, (T % NT) * P:(T % NT + 1) * P],
                         bank[6 + T % 2][:].bitcast(BF16).rearrange("p (m n) -> p m n", m=NT)) \
                    .then_inc(s_nbr, 1)

            high_part(0)
            for n in range(1, KT):
                high_part(n)
                square(n - 1)
            square(KT - 1)
            norm_out(0)
            gram_out(0)
            for n in range(CT):
                w_high(n)
            for T in range(1, NT - 1):
                gram_out(T)
                nbr_out(T - 1)
                if T == 3:
                    for n in range(CT, 2 * CT):
                        w_high(n)
                if T in (4, 5):
                    for n in range(KT + 4 * (T - 4), KT + 4 * (T - 3)):
                        square(n)
                if T == 6:
                    norm_out(1)
            for k in range(3):
                high_part(KT + k)
            gram_out(NT - 1)
            for k in range(3, KT):
                high_part(KT + k)
            nbr_out(NT - 2)
            for T in range(NT, TILES):
                gram_out(T)
                nbr_out(T - 1)

            def p_high(n):
                hf, t = (n % (2 * CT)) // CT, n % CT
                act.wait_ge(s_p32, n + 1)
                act.copy(p_h[:, t, hf * HALF:(hf + 1) * HALF], p32(n)).then_inc(s_p0, 1)

            def y_high(g):
                it, m = g // NT, g % NT
                act.wait_ge(s_wm, g + 1)
                if m == 0 and it:
                    act.wait_ge(s_m, 2 * CT * it)
                act.copy(y_h[:, m, :], bank[g % 3][:]).then_inc(s_yh, 1)

            def a_row_out(c):
                act.wait_ge(s_aT, c + 1)
                if c:
                    act.wait_ge(s_arow, 16 * c)
                act.copy(a_row[:], bank[6][:, 384:HALF]).then_inc(s_ar, 1)

            def bn_sqrt(ev, n):
                act.wait_ge(s_mlp, MLP[ev])
                act.activation(stat[:, 40:40 + n], stat[:, 34:34 + n], ACT.Sqrt).then_inc(s_act, 1)

            def bn_apply(ev, first, n):
                act.wait_ge(s_mlp, MLP[ev])
                for c in range(n):
                    act.activation(slots(first + c), slots(first + c), ACT.Identity, bias=stat[:, 58 + c:59 + c],
                                   scale=stat[:, 52 + c:53 + c]).then_inc(s_act, 1)

            def side(g):
                if g == 0:
                    nbr_out(TILES - 1)
                if (g - R0) % 8 == 2 and 0 <= (g - R0) // 8 < CHUNKS:
                    a_row_out((g - R0) // 8)
                if g == 16 + NT:
                    act.wait_ge(s_wm, 2 * NT)
                    act.dma_start(w_flat.bitcast(F32), w1_keep).then_inc(s_wback, 16)
                m = g - M0
                if m == 4:
                    act.wait_ge(s_mlp, MLP["sqrt"])
                    act.activation(slots(6, 2), slots(4, 2), ACT.Sqrt).then_inc(s_act, 1)
                if m == 10:
                    act.wait_ge(s_mlp, MLP["atan"])
                    act.activation(slots(6, 2), slots(8, 2), ACT.Arctan).then_inc(s_act, 1)
                if m == 25:
                    bn_sqrt("bn1s", 6)
                if m == 26:
                    bn_apply("bn1a", 0, 6)
                if m == 38:
                    bn_sqrt("bn2s", 3)
                if m == 39:
                    bn_apply("bn2a", 6, 3)
                if m == 45:
                    bn_sqrt("bn3s", 1)
                if m == 46:
                    bn_apply("bn3a", 0, 1)
                if m == 47:
                    act.wait_ge(s_mlp, MLP["exp"])
                    act.activation(slots(1), slots(0), ACT.Exp).then_inc(s_act, 1)
                if g == T0 + 1:
                    columns()
                if g in (T0 + 2, T0 + 3):
                    round_high(2 * (g - T0 - 2))
                if g >= S0:
                    spread_out(g - S0)
                if g >= 16 * ITS - AB:
                    xT_high(g - 16 * ITS + AB)

            def columns():
                act.wait_ge(s_scT, 1)
                act.copy(aT, bank[6][:]).then_inc(s_sct, 1)
                act.wait_ge(s_scT, 2)
                act.activation(rT, bank[7][:], ACT.Identity, bias=slot_t[:, 0:1]).then_inc(s_sct, 1)

            def round_high(c0):
                act.wait_ge(s_scT, 3)
                for c in (c0, c0 + 1):
                    if c:
                        act.wait_ge(s_attq, c)
                    act.copy(att_h12[:], bank[6][:, c * P:(c + 1) * P]).then_inc(s_h12, 1)

            def spread_out(q):
                act.wait_ge(s_sc, q + 1)
                if q >= 2:
                    act.wait_ge(s_st[q % 2], 16 * (q // 2))
                act.copy(spread_s[q % 2].rearrange("p (x n) -> p n x", n=GN),
                         bank[6 + q % 2][:].rearrange("p (n x) -> p n x", n=GN)).then_inc(s_scc, 1)

            def xT_high(n):
                act.wait_ge(s_xT, n + 1)
                act.copy(xT[n // AB][:, 0, n % AB, :], bank[n % 2][:]).then_inc(s_xTh, 1)

            for j in range(2 * CT):
                p_high(j)
            for it in range(ITS):
                for m in range(NT):
                    y_high(NT * it + m)
                    side(16 * it + m)
                for j in range(2 * CT):
                    if it + 1 < ITS:
                        p_high(2 * CT * (it + 1) + j)
                    side(16 * it + NT + j)

            for i in range(CHUNKS * CT):
                for n, q in enumerate(tail_groups(i)):
                    if n == 2 and i < AB:
                        xT_high(AB + i)
                    spread_out(q)

        @block.vector
        def _(dve):
            chain = [0]

            def link(ins):
                chain[0] += 1
                ins.then_inc(s_link, 1)
                dve.wait_ge(s_link, chain[0])

            def w_low(n):
                t = n % CT
                dve.wait_ge(s_wh, n + 1)
                dve.tensor_tensor(wT[:, 1, t, :], w_bank(n), wT[:, 0, t, :].bitcast(F32),
                                  ALU.subtract).then_inc(s_wl, 1)

            def pts_low(k):
                dve.wait_ge(s_ph, k + 1)
                dve.tensor_tensor(pts_l[:, k, :], stage[:, k % NS, :], pts_h[:, k, :].bitcast(F32),
                                  ALU.subtract).then_inc(s_pl0, 1)

            def select(T, rounds=range(KP // 8)):
                b, t, v = T // NT, T % NT, score[:, T % 2, :]
                step = [TOPSTEPS * T + (4 + 3 * (rounds[0] - 1) if rounds[0] else 0)]

                def done(ins):
                    step[0] += 1
                    ins.then_inc(s_top, 1)
                    if T < TILES - 2:
                        dve.wait_ge(s_top, step[0])
                    else:
                        count[0] += 1
                        dve.wait_ge(s_top, count[0])

                dve.wait_ge(s_v, T + 1)
                for r in rounds:
                    top = vals[:, T % 2, 8 * r:8 * r + 8]
                    done(dve.max(top, v))
                    done(dve.max_index(idx[:, T, 8 * r:8 * r + 8], top, v))
                    if r == KP // 8 - 1:
                        break
                    done(dve.match_replace(v, top, v, REMOVED))
                    if r == 0:
                        if T == 0:
                            dve.wait_ge(s_wps, CT)
                        if T >= 2:
                            dve.wait_ge(s_adjT, T - 1)
                        done(dve.tensor_scalar(adj[:, T % 2, :], v, REMOVED / 2, None, ALU.is_le))
                        diag = adj[:, T % 2, t * P:(t + 1) * P]
                        dve.tensor_tensor(diag, diag, ident_b[:], ALU.add).then_inc(s_adj, 1)

            count = [TOPSTEPS * (TILES - 2)]
            dve.wait_ge(s_const, 7 + CH)
            for k in range(KT):
                pts_low(k)
            for T in range(TILES - 2):
                select(T)
                if T in (0, 2):
                    for n in range(2 * T, 2 * T + CT):
                        w_low(n)
                if T == 4:
                    dve.wait_ge(s_prm, 16 * (9 + 6 * B))
                    link(dve.tensor_copy(tab_p[:, 0], tab[:]))
                    link(dve.tensor_tensor(tab_rest[:], tab[:], tab_p[:, 0], ALU.subtract))
                    link(dve.tensor_copy(tab_p[:, 1], tab_rest[:]))
                    link(dve.tensor_tensor(tab_rest[:], tab_rest[:], tab_p[:, 1], ALU.subtract))
                    dve.tensor_copy(tab_p[:, 2], tab_rest[:]).then_inc(s_tab, 1)
            for T in (TILES - 2, TILES - 1):
                select(T, range(1))

            def p_make(n):
                it = n // (2 * CT)
                b, hf, t = it % B, (n % (2 * CT)) // CT, n % CT
                if it < B:
                    dve.wait_ge(s_x[b], 16)
                else:
                    dve.wait_ge(s_xu, 2 * CT * (it - 1))
                if it and n % (2 * CT) == 0:
                    dve.wait_ge(s_wm, NT * it)
                if n >= 2:
                    dve.wait_ge(s_p1, n - 1)
                src = X[:, b, t, hf * HALF:(hf + 1) * HALF]
                dve.scalar_tensor_tensor(p32(n), src, SLOPE0, src, ALU.mult, ALU.max).then_inc(s_p32, 1)

            def y_low(g):
                m = g % NT
                dve.wait_ge(s_yh, g + 1)
                dve.tensor_tensor(y_l[:, m, :], bank[g % 3][:], y_h[:, m, :].bitcast(F32),
                                  ALU.subtract).then_inc(s_yl, 1)

            def x_update(g):
                it, j = g // (2 * CT), g % (2 * CT)
                b, hf, t = it % B, j // CT, j % CT
                dst = X[:, b, t, hf * HALF:(hf + 1) * HALF]
                dve.wait_ge(s_m, g + 1)
                dve.scalar_tensor_tensor(dst, bank[3 + g % 3][:], 1.0 / (K0 + 1.0), dst,
                                         ALU.mult, ALU.add).then_inc(s_xu, 1)

            def index_rows(c):
                if c == 0:
                    dve.wait_ge(s_adjT, TILES)
                src = idx[:, CH * c:CH * (c + 1), :].rearrange("p t k -> p (t k)")
                if c:
                    dve.wait_ge(s_aT, c)
                link(dve.tensor_scalar(i_u, src, 3, None, ALU.logical_shift_right))
                link(dve.tensor_copy(a_f, i_u))
                link(dve.tensor_scalar(i_u, src, AB - 1, None, ALU.bitwise_and))
                dve.tensor_copy(r_all[:, CH * c:CH * (c + 1), :].rearrange("p t k -> p (t k)"), i_u) \
                    .then_inc(s_af, 1)

            def onehot_a(u):
                dve.wait_ge(s_bc[u % NB], 16 * (u // NB + 1))
                dve.tensor_scalar(bc[:, u % NB, :], bc[:, u % NB, :], part[:, 0:1], None, ALU.is_equal) \
                    .then_inc(s_oh, 1)

            def pick_r(u):
                T, k0 = u // 2, (u % 2) * KH
                dve.wait_ge(s_af, T // CH + 1)
                link(dve.tensor_tensor(oh_r, r_all[:, T, k0:k0 + KH].unsqueeze(2).to_broadcast([P, KH, AB]),
                                       iota_r[:, 0:AB].unsqueeze(1).to_broadcast([P, KH, AB]), ALU.is_equal))
                dve.wait_ge(s_look, u + 1)
                dve.tensor_tensor(pick, bank[6 + u % 2][:, 0:3 * KH * AB]
                                  .rearrange("p (k j r) -> p k j r", k=KH, j=3),
                                  oh_r.unsqueeze(2).to_broadcast([P, KH, 3, AB]), ALU.mult).then_inc(s_pick, 1)
                dve.wait_ge(s_pick, u + 1)
                link(dve.tensor_reduce(near[:, :, T, k0:k0 + KH], pick.rearrange("p k j r -> p j k r"),
                                       AX_X, ALU.add))

            def tt(o, a, b_, op):
                link(dve.tensor_tensor(o, a, b_, op))

            def ts(o, a, s1, op0, s2=None, op1=None):
                if op1 is None:
                    link(dve.tensor_scalar(o, a, s1, None, op0))
                else:
                    link(dve.tensor_scalar(o, a, s1, s2, op0, op1))

            def stt(o, a, s_, b_, op0, op1):
                link(dve.scalar_tensor_tensor(o, a, s_, b_, op0, op1))

            def mix(first, src, ws, fresh=True):
                for j, a in enumerate(src):
                    for c, w in enumerate(ws(j)):
                        if j == 0 and fresh:
                            ts(slots(first + c), slots(a), w, ALU.mult)
                        else:
                            stt(slots(first + c), slots(a), w, slots(first + c), ALU.mult, ALU.add)

            def bn_partial(first, n, some, last):
                for c in some:
                    link(dve.bn_stats(small[:, 6 * c:6 * c + 6], slots(first + c)))
                for c in some:
                    link(dve.bn_aggr(small[:, 40 + 2 * c:42 + 2 * c], small[:, 6 * c:6 * c + 6]))
                if not last:
                    return
                pair = small[:, 40:40 + 2 * n].rearrange("p (c s) -> p s c", s=2)
                ts(stat[:, 0:n], pair[:, 0], 1.0, ALU.mult)
                tt(stat[:, n:2 * n], pair[:, 0], pair[:, 0], ALU.mult)
                dve.tensor_tensor(stat[:, n:2 * n], stat[:, n:2 * n], pair[:, 1], ALU.add).then_inc(s_bnin, 1)

            def bn_variance(layer, n, ev):
                dve.wait_ge(s_bnps, layer)
                ts(stat[:, 16:16 + 2 * n], bank[7][:, 480:480 + 2 * n], 1.0, ALU.mult)
                tt(stat[:, 28:28 + n], stat[:, 16:16 + n], stat[:, 16:16 + n], ALU.mult)
                tt(stat[:, 34:34 + n], stat[:, 16 + n:16 + 2 * n], stat[:, 28:28 + n], ALU.subtract)
                dve.tensor_scalar(stat[:, 34:34 + n], stat[:, 34:34 + n], EPS_BN, None,
                                  ALU.add).then_inc(s_mlp, 1)

            def bn_coefficients(n, gain, bias, ev):
                y, t, v = stat[:, 46:46 + n], stat[:, 28:28 + n], stat[:, 34:34 + n]
                dve.wait_ge(s_act, DONE[ev])
                link(dve.reciprocal(y, stat[:, 40:40 + n]))
                tt(t, y, y, ALU.mult)
                tt(t, t, v, ALU.mult)
                ts(t, t, -0.5, ALU.mult, 1.5, ALU.add)
                tt(y, y, t, ALU.mult)
                tt(stat[:, 52:52 + n], y, prm[:, gain:gain + n], ALU.mult)
                tt(t, stat[:, 16:16 + n], stat[:, 52:52 + n], ALU.mult)
                dve.tensor_tensor(stat[:, 58:58 + n], prm[:, bias:bias + n], t,
                                  ALU.subtract).then_inc(s_mlp, 1)

            def leaky(first, n, ev):
                dve.wait_ge(s_act, DONE[ev])
                h = slots(first, n)
                stt(h, h, SLOPE1, h, ALU.mult, ALU.max)

            own_k = own[:].unsqueeze(3).to_broadcast([P, 3, TILES, K1])

            def grid(a):
                return slots(a).rearrange("p (t k) -> p t k", t=TILES)

            def network(n):
                Y, Xa, S, R = slots(0, 2), slots(2, 2), slots(4), slots(5)
                A, T_ = slots(6, 2), slots(8, 2)
                if n == 0:
                    tt(grid(0), grid(0), own_k[:, 0], ALU.subtract)
                    tt(grid(1), grid(1), own_k[:, 1], ALU.subtract)
                    tt(grid(3), grid(2), own_k[:, 2], ALU.subtract)
                if n == 1:
                    tt(S, slots(3), slots(3), ALU.mult)
                    tt(R, slots(1), slots(1), ALU.mult)
                    tt(S, S, R, ALU.add)
                if n == 2:
                    tt(R, slots(0), slots(0), ALU.mult)
                    tt(R, S, R, ALU.add)
                    stt(slots(0), R, TINY, slots(0), ALU.is_ge, ALU.mult)
                if n == 3:
                    stt(slots(1), S, TINY, slots(1), ALU.is_ge, ALU.mult)
                    stt(slots(3), S, TINY, slots(3), ALU.is_ge, ALU.mult)
                if n == 4:
                    stt(slots(3), S, TINY, slots(3), ALU.is_lt, ALU.add)
                    dve.tensor_scalar(slots(4, 2), slots(4, 2), TINY, None, ALU.max).then_inc(s_mlp, 1)
                if n == 5:
                    dve.wait_ge(s_act, DONE["sqrt"])
                    link(dve.reciprocal(T_, A))
                    tt(T_, T_, slots(4, 2), ALU.mult)
                if n == 6:
                    tt(T_, T_, A, ALU.add)
                    ts(slots(2), slots(8), 0.5, ALU.mult)
                    ts(slots(10), slots(9), 0.5, ALU.mult)
                if n == 7:
                    stt(slots(4, 2), Y, -1.0, Y, ALU.mult, ALU.max)
                    stt(A, Xa, -1.0, Xa, ALU.mult, ALU.max)
                if n == 8:
                    tt(T_, slots(4, 2), A, ALU.min)
                    tt(A, slots(4, 2), A, ALU.max)
                if n == 9:
                    tt(slots(4, 2), slots(4, 2), A, ALU.is_ge)
                    link(dve.reciprocal(A, A))
                if n == 10:
                    dve.tensor_tensor(T_, T_, A, ALU.mult).then_inc(s_mlp, 1)
                    w = prm[:, 0:36].rearrange("p (c j) -> p c j", c=6)
                    link(dve.tensor_reduce(small[:, 0:6], w[:, :, 3:6], AX_X, ALU.add))
                    ts(small[:, 0:6], small[:, 0:6], -1.0 / 3.0, ALU.mult)
                    tt(w_eff[:], w[:, :, 0:3], w[:, :, 3:6], ALU.add)
                    tt(w_eff[:], w_eff[:], small[:, 0:6].unsqueeze(2).to_broadcast([P, 6, 3]), ALU.add)
                if n == 11:
                    dve.wait_ge(s_act, DONE["atan"])
                    ts(T_, A, -2.0, ALU.mult, PI / 2, ALU.add)
                    tt(T_, T_, slots(4, 2), ALU.mult)
                if n == 12:
                    tt(A, A, T_, ALU.add)
                    ts(T_, A, -2.0, ALU.mult, PI, ALU.add)
                if n == 13:
                    stt(T_, Xa, 0.0, T_, ALU.is_lt, ALU.mult)
                    tt(A, A, T_, ALU.add)
                if n == 14:
                    ts(T_, Y, 0.0, ALU.is_ge, 2.0, ALU.mult)
                    stt(A, T_, -1.0, A, ALU.add, ALU.mult)
                if 15 <= n < 21:
                    c = n - 15
                    mix(c, (10, 6, 7), lambda j: [w_eff[:, c, j:j + 1]])
                if n == 21:
                    bn_partial(0, 6, range(3), False)
                if n == 22:
                    bn_partial(0, 6, range(3, 6), True)
                if n == 25:
                    bn_variance(1, 6, "bn1s")
                if n == 26:
                    bn_coefficients(6, 36, 42, "bn1s")
                if n == 27:
                    leaky(0, 3, "bn1a")
                if n == 28:
                    leaky(3, 3, "bn1a")
                if 29 <= n < 35:
                    c, hf = (n - 29) // 2, (n - 29) % 2
                    mix(6 + c, range(3 * hf, 3 * hf + 3),
                        lambda j: [prm[:, 48 + 6 * c + 3 * hf + j:49 + 6 * c + 3 * hf + j]], hf == 0)
                if n == 35:
                    bn_partial(6, 3, range(3), True)
                if n == 38:
                    bn_variance(2, 3, "bn2s")
                if n == 39:
                    bn_coefficients(3, 66, 69, "bn2s")
                if n == 40:
                    leaky(6, 3, "bn2a")
                if n == 41:
                    mix(0, (6, 7, 8), lambda j: [prm[:, 72 + j:73 + j]])
                if n == 42:
                    bn_partial(0, 1, range(1), True)
                if n == 45:
                    bn_variance(3, 1, "bn3s")
                if n == 46:
                    bn_coefficients(1, 75, 76, "bn3s")
                if n == 47:
                    leaky(0, 1, "bn3a")
                    link(dve.tensor_reduce(small[:, 0:TILES], grid(0), AX_X, ALU.max))
                    dve.tensor_tensor(grid(0), grid(0), small[:, 0:TILES].unsqueeze(2)
                                      .to_broadcast([P, TILES, K1]), ALU.subtract).then_inc(s_mlp, 1)
                if n == 48:
                    dve.wait_ge(s_act, DONE["exp"])
                    link(dve.tensor_reduce(small[:, 16:16 + TILES], grid(1), AX_X, ALU.add))
                    link(dve.reciprocal(small[:, 32:32 + TILES], small[:, 16:16 + TILES]))
                    link(dve.memset(att32[:, :, K1:KP], 0.0))
                    tt(att32[:, :, 0:K1], grid(1), small[:, 32:32 + TILES].unsqueeze(2)
                       .to_broadcast([P, TILES, K1]), ALU.mult)

            def index_columns():
                src = idx[:].rearrange("p t k -> p (t k)")
                link(dve.tensor_scalar(i_all, src, 3, None, ALU.logical_shift_right))
                link(dve.tensor_copy(a_all, i_all))
                link(dve.tensor_scalar(i_all, src, AB - 1, None, ALU.bitwise_and))
                dve.tensor_scalar(r4_all, i_all, float(CH), None, ALU.mult).then_inc(s_att, 1)

            def att_parts(c):
                cols = slice(c * P, (c + 1) * P)
                dve.wait_ge(s_h12, c + 1)
                h = att_h12[:].bitcast(F32)
                link(dve.tensor_copy(att_q[:, 0, 0, cols], h))
                link(dve.tensor_tensor(att_q[:, 1, 0, cols], h, att_q[:, 0, 0, cols], ALU.subtract))
                link(dve.tensor_tensor(l_tmp, bank[6][:, cols], h, ALU.subtract))
                link(dve.tensor_copy(att_q[:, 0, 1, cols], l_tmp))
                dve.tensor_tensor(att_q[:, 1, 1, cols], l_tmp, att_q[:, 0, 1, cols],
                                  ALU.subtract).then_inc(s_attq, 1)

            def onehots(q):
                n0 = (q // NG) * P + (q % NG) * GN
                if q == 0:
                    dve.wait_ge(s_sct, 2)
                    dve.wait_ge(s_iota, 2)
                    dve.wait_ge(s_attq, CHUNKS)
                if q >= 2:
                    dve.wait_ge(s_sc, q - 1)
                    dve.wait_ge(s_mv[1], q - 1)
                dve.tensor_tensor(eq[q % 2], rT[:, n0:n0 + GN].unsqueeze(1).to_broadcast([P, KP, GN]),
                                  iota_r8, ALU.is_equal).then_inc(s_eq, 1)
                dve.tensor_tensor(oa[q % 2], aT[:, n0:n0 + GN].unsqueeze(1).to_broadcast([P, P, GN]),
                                  iota_a8, ALU.is_equal).then_inc(s_oa, 1)
                dve.wait_ge(s_eq, q + 1)
                weigh(dve, q, 0)

            def xT_low(n):
                dve.wait_ge(s_xTh, n + 1)
                dve.tensor_tensor(xT[n // AB][:, 1, n % AB, :], bank[n % 2][:],
                                  xT[n // AB][:, 0, n % AB, :].bitcast(F32), ALU.subtract).then_inc(s_xTl, 1)

            def side(g):
                if g < 6:
                    select(TILES - 2 + g // 3, range(1 + g % 3, 2 + g % 3))
                if (g - R0) % 8 == 0 and 0 <= (g - R0) // 8 < CHUNKS:
                    index_rows((g - R0) // 8)
                if G0 <= g < G0 + 2 * TILES:
                    onehot_a(g - G0)
                if G0 + 2 <= g < G0 + 2 + 2 * TILES:
                    pick_r(g - G0 - 2)
                if M0 <= g < M0 + 49:
                    network(g - M0)
                if g == M0 + 49:
                    index_columns()
                if g == T0 + 2:
                    att_parts(0)
                    att_parts(1)
                if g == T0 + 3:
                    att_parts(2)
                    att_parts(3)
                if g >= S0:
                    onehots(g - S0)
                if g > 16 * ITS - AB:
                    xT_low(g - 16 * ITS + AB - 1)

            for j in range(2 * CT):
                p_make(j)
            for it in range(ITS):
                for m in range(NT):
                    side(16 * it + m)
                    y_low(NT * it + m)
                for j in range(2 * CT):
                    side(16 * it + NT + j)
                    x_update(2 * CT * it + j)
                    if it + 1 < ITS:
                        p_make(2 * CT * (it + 1) + j)

            def result(i):
                c, t = i // CT, i % CT
                b, hf = c // NH, c % NH
                dve.wait_ge(s_f, i + 1)
                dst = X[:, b, t, hf * HALF:(hf + 1) * HALF].rearrange("p (t q n) -> p q t n", t=CH, n=GN)
                dve.tensor_tensor(dst, bank[4 + t % 2][:].rearrange("p (q t n) -> p q t n", q=NG, t=CH),
                                  dst, ALU.add).then_inc(s_fo, 1)

            xT_low(AB - 1)
            for i in range(CHUNKS * CT):
                for n, q in enumerate(tail_groups(i)):
                    onehots(q)
                    if n == 1 and i:
                        result(i - 1)
                    if n == 3 and i < AB:
                        xT_low(AB + i)
                if i and not tail_groups(i):
                    result(i - 1)
            result(CHUNKS * CT - 1)

        @block.tensor
        def _(pe):
            def w_turn(n):
                i, t = 1 - n // CT, n % CT
                pe.wait_ge(s_w, 32)
                if n == CT:
                    pe.wait_ge(s_wl, CT)
                    pe.wait_ge(s_nbr, 3)
                if n == 2:
                    pe.wait_ge(s_nsq, 2)
                for o in range(CT):
                    mm = pe.transpose(w_bank(n)[:, o * P:(o + 1) * P],
                                      w_raw[i][:, o, t * P:(t + 1) * P], ident[:])
                mm.then_inc(s_wps, 1)

            def norms(n):
                pe.wait_ge(s_sq, n + 1)
                if n == KT:
                    pe.wait_ge(s_wl, 2 * CT)
                k = n % KT
                for hf in range(NH):
                    mm = pe.matmul(bank[4 + hf][:], neg_half[:], stage[:, n % NS, hf * HALF:(hf + 1) * HALF],
                                   start=(k == 0), stop=(k == KT - 1))
                mm.then_inc(s_sqmm, 1)

            def gram(T):
                b, t = T // NT, T % NT
                if T >= 2:
                    pe.wait_ge(s_gc, 2 * (T - 1))
                for k in range(KT):
                    if t == 0:
                        pe.wait_ge((s_pl0, s_pl1)[b], k + 1)
                    rows = slice(t * P, (t + 1) * P)
                    for hf in range(NH):
                        cols = slice(hf * HALF, (hf + 1) * HALF)
                        o = bank[2 * (T % 2) + hf][:]
                        pe.matmul(o, pts_h[:, k, rows], pts_h[:, k, cols], start=(k == 0), stop=False)
                        pe.matmul(o, pts_h[:, k, rows], pts_l[:, k, cols], start=False, stop=False)
                        mm = pe.matmul(o, pts_l[:, k, rows], pts_h[:, k, cols], start=False,
                                       stop=(k == KT - 1))
                    if T == NT - 1:
                        mm.then_inc(s_kdone, 1)
                    if T == 0 and k:
                        norms(k - 1)
                if T != NT - 1:
                    mm.then_inc(s_g, 1)

            def adj_turn(T):
                pe.wait_ge(s_adj, T + 1)
                if T in (0, 3):
                    pe.wait_ge(s_wl, CT if T == 0 else 2 * CT)
                if T >= 2:
                    pe.wait_ge(s_nbr, T - 1)
                for m in range(NT):
                    mm = pe.transpose(bank[6 + T % 2][:].bitcast(BF16)[:, m * P:(m + 1) * P],
                                      adj[:, T % 2, m * P:(m + 1) * P], ident_b[:])
                mm.then_inc(s_adjT, 1)

            pe.wait_ge(s_const, 7 + CH)
            gram(0)
            norms(KT - 1)
            for n in range(CT):
                w_turn(n)
            for T in range(1, NT):
                gram(T)
                if T == 4:
                    for n in range(CT, 2 * CT):
                        w_turn(n)
                adj_turn(T - 1)
                if T in (5, 6):
                    for n in range(KT + 4 * (T - 5), KT + 4 * (T - 4)):
                        norms(n)
            for T in range(NT, TILES):
                gram(T)
                adj_turn(T - 1)

            def wp(g):
                it, m = g // NT, g % NT
                if m in (0, NT // 2):
                    pe.wait_ge(s_p1, 2 * CT * it + (CT if m == 0 else 2 * CT))
                if g == 2 * NT:
                    pe.wait_ge(s_wback, 16)
                if g >= 3:
                    pe.wait_ge(s_yl, g - 2)
                elif g == 0:
                    pe.wait_ge(s_gc, 2 * TILES)
                cols = slice(m * P, (m + 1) * P)
                for t in range(CT):
                    pe.matmul(bank[g % 3][:], p_h[:, t, cols], wT[:, 0, t, :], start=(t == 0), stop=False)
                    pe.matmul(bank[g % 3][:], p_h[:, t, cols], wT[:, 1, t, :], start=False, stop=False)
                    mm = pe.matmul(bank[g % 3][:], p_l[:, t, cols], wT[:, 0, t, :], start=False,
                                   stop=(t == CT - 1))
                mm.then_inc(s_wm, 1)

            def aggregate(g):
                it, j = g // (2 * CT), g % (2 * CT)
                b, hf, t = it % B, j // CT, j % CT
                if it < B and j == 0:
                    pe.wait_ge(s_nbr, NT * (it + 1))
                if g >= 3:
                    pe.wait_ge(s_xu, g - 2)
                for m in range(NT):
                    if j == 0:
                        pe.wait_ge(s_yl, NT * it + m + 1)
                    for part_, y in enumerate((y_h, y_l)):
                        mm = pe.matmul(bank[3 + g % 3][:], y[:, m, t * P:(t + 1) * P],
                                       nbr[:, b, m, hf * HALF:(hf + 1) * HALF],
                                       start=(m == 0 and part_ == 0), stop=(m == NT - 1 and part_ == 1))
                mm.then_inc(s_m, 1)

            def turn_a(c):
                pe.wait_ge(s_af, c + 1)
                if c:
                    pe.wait_ge(s_ar, c)
                    pe.wait_ge(s_pick, 8 * c + R0 - G0 + 1)
                else:
                    pe.wait_ge(s_nbr, TILES)
                pe.transpose(bank[6][:, 384:HALF], a_f, ident[:]).then_inc(s_aT, 1)

            def lookup(u):
                pe.wait_ge(s_oh, u + 1)
                if u >= 2:
                    pe.wait_ge(s_pick, u - 1)
                pe.wait_ge(s_ar, min((u + G0 - R0 - 2) // 8 + 1, CHUNKS))
                b = u // (2 * NT)
                for k in range(KH):
                    for i in range(3):
                        mm = pe.matmul(bank[6 + u % 2][:, k * 3 * AB:(k + 1) * 3 * AB],
                                       bc[:, u % NB, k * P:(k + 1) * P],
                                       tab_p[:, i, b].rearrange("p j r -> p (j r)"),
                                       start=(i == 0), stop=(i == 2))
                mm.then_inc(s_look, 1)

            def bn_sum(layer, n):
                pe.wait_ge(s_bnin, layer)
                pe.matmul(bank[7][:, 480:480 + 2 * n], mean_mat[:], stat[:, 0:2 * n],
                          start=True, stop=True).then_inc(s_bnps, 1)

            def side(g):
                if g == 0:
                    adj_turn(TILES - 1)
                if G0 < g <= G0 + 2 * TILES:
                    lookup(g - G0 - 1)
                if (g - R0) % 8 == 2 and 0 <= (g - R0) // 8 < CHUNKS:
                    turn_a((g - R0) // 8)
                m = g - M0
                if m == 24:
                    bn_sum(1, 6)
                if m == 37:
                    bn_sum(2, 3)
                if m == 44:
                    bn_sum(3, 1)
                if g == T0 + 1:
                    turn_att()
                if g > S0:
                    spread(g - S0 - 1)
                if g == 16 * ITS - 1:
                    spread(g - S0)
                if g >= 16 * ITS - AB:
                    turn_x(g - 16 * ITS + AB)

            def turn_att():
                pe.wait_ge(s_att, 1)
                for c in range(CHUNKS):
                    mm = pe.transpose(bank[6][:, c * P:(c + 1) * P], a_all[:, c * P:(c + 1) * P], ident[:])
                mm.then_inc(s_scT, 1)
                for c in range(CHUNKS):
                    mm = pe.transpose(bank[7][:, c * P:(c + 1) * P], r4_all[:, c * P:(c + 1) * P], ident[:])
                mm.then_inc(s_scT, 1)
                pe.wait_ge(s_sct, 1)
                for c in range(CHUNKS):
                    mm = pe.transpose(bank[6][:, c * P:(c + 1) * P],
                                      att32[:, CH * c:CH * (c + 1), :].rearrange("p t k -> p (t k)"), ident[:])
                mm.then_inc(s_scT, 1)

            def spread(q):
                pe.wait_ge(s_oa, q + 1)
                pe.wait_ge(s_mv[0], q + 1)
                pe.wait_ge(s_mv[1], q + 1)
                if q == 0:
                    pe.wait_ge(s_attq, CHUNKS)
                if q >= 2:
                    pe.wait_ge(s_scc, q - 1)
                for n in range(GN):
                    for i in range(2):
                        mm = pe.matmul(bank[6 + q % 2][:, n * 2 * KP:(n + 1) * 2 * KP], oa[q % 2][:, :, n],
                                       mv[q % 2][:, i, :, :, n].rearrange("p h r -> p (h r)"),
                                       start=(i == 0), stop=(i == 1))
                mm.then_inc(s_sc, 1)

            def turn_x(n):
                if n == 0:
                    pe.wait_ge(s_yl, NT * ITS)
                    pe.wait_ge(s_xu, 2 * CT * (ITS - 1))
                if n == AB:
                    pe.wait_ge(s_xu, 2 * CT * ITS)
                if n >= 2:
                    pe.wait_ge(s_xTl, n - 1)
                b, r = n // AB, n % AB
                for t in range(CT):
                    mm = pe.transpose(bank[n % 2][:, t * P:(t + 1) * P], X[:, b, t, r:N:AB], ident[:])
                mm.then_inc(s_xT, 1)

            for it in range(ITS):
                for m in range(NT):
                    wp(NT * it + m)
                    side(16 * it + m)
                for j in range(2 * CT):
                    aggregate(2 * CT * it + j)
                    side(16 * it + NT + j)

            def attend(i):
                c, t = i // CT, i % CT
                b = c // NH
                if t == 0:
                    pe.wait_ge(s_back, 16 * 4 * (c + 1))
                    pe.wait_ge(s_xTl, AB * (b + 1))
                if i >= 2:
                    pe.wait_ge(s_fo, i - 1)
                else:
                    pe.wait_ge(s_xu, 2 * CT * ITS)
                beside = list(tail_groups(i))
                for r in range(AB):
                    if r % 2 and r // 2 < len(beside):
                        spread(beside[r // 2])
                    if r == 3 and i < AB:
                        turn_x(AB + i)
                    o = bank[4 + t % 2][:]
                    lhs = [xT[b][:, h, r, t * P:(t + 1) * P] for h in range(2)]
                    rhs = [att_T[c % 2][:, h, r] for h in range(2)]
                    pe.matmul(o, lhs[0], rhs[0], start=(r == 0), stop=False)
                    pe.matmul(o, lhs[0], rhs[1], start=False, stop=False)
                    mm = pe.matmul(o, lhs[1], rhs[0], start=False, stop=(r == AB - 1))
                mm.then_inc(s_f, 1)

            for i in range(CHUNKS * CT):
                attend(i)



_INS = ["x", "ctx_4096", "fside_BxSxS_0", "L1_xattn_W1", "L1_xattn_g1", "L1_xattn_b1", "L1_xattn_W2",
        "L1_xattn_g2", "L1_xattn_b2", "L1_xattn_W3", "L1_xattn_g3", "L1_xattn_b3"]


def kernel(**inputs):
    import concourse.bacc as bacc
    from concourse.bass_utils import run_bass_kernel_spmd

    nc = bacc.Bacc("TRN2", target_bir_lowering=False, num_devices=1)
    arrays, args = {}, []
    for name in _INS:
        a = np.ascontiguousarray(inputs[name])
        arrays[f"in_{name}"] = a
        args.append(nc.dram_tensor(f"in_{name}", a.shape, mybir.dt.from_np(a.dtype), kind="ExternalInput").ap())
    shape = arrays["in_x"].shape
    out = nc.dram_tensor("out_dram", shape, F32, kind="ExternalOutput").ap()
    build(nc, *args, out)
    r = run_bass_kernel_spmd(nc, [arrays], core_ids=[0])
    return r.results[0]["out_dram"]
```

```python
from contextlib import ExitStack

import numpy as np
import concourse.bass as bass
from concourse import mybir

F32 = mybir.dt.float32
F32R = mybir.dt.float32r
BF16 = mybir.dt.bfloat16
U32 = mybir.dt.uint32
ALU = mybir.AluOpType
ACT = mybir.ActivationFunctionType
AX_X = mybir.AxisListType.X

P = 128
HALF = 512
K0 = 8
K1 = 30
KP = 32
BLOCKS = 4
SLOPE0 = 0.01
SLOPE1 = 0.2
EPS_BN = 1e-5
TINY = 1e-20
REMOVED = -1.0e38
PI = float(np.pi)


def build(nc, x, ctx, fside, W1, g1, b1, W2, g2, b2, W3, g3, b3, out):
    B, C, N = x.shape
    D = ctx.shape[1]
    CT = C // P
    KT = D // P
    NT = N // P
    TILES = B * NT
    NH = N // HALF
    AB = N // P
    CH = 4
    CHUNKS = TILES // CH
    ITS = B * BLOCKS
    GN = 8
    NG = P // GN
    NS = 6
    U = TILES * K1

    with ExitStack() as st:
        def sb(name, shape, dt):
            return st.enter_context(nc.sbuf_tensor(name, shape, dt))

        def sem(name):
            return st.enter_context(nc.semaphore(name))

        pts_h = sb("pts_h", [P, KT, N], F32R)
        pts_l = sb("pts_l", [P, KT, N], F32R)
        nbr = sb("nbr", [P, B, NT, N], F32R)
        X = sb("X", [P, B, CT, N], F32)
        wT = sb("wT", [P, 2, CT, C], F32R)
        scratch = sb("scratch", [P, 11 * U + 2 * HALF], F32)
        ident = sb("ident", [P, P], F32)
        ident_b = sb("ident_b", [P, P], BF16)
        neg_half = sb("neg_half", [P, P], F32)
        mean_mat = sb("mean_mat", [P, P], F32)
        iota_r = sb("iota_r", [P, KP], F32)
        part = sb("part", [P, 1], F32)
        minus_one = sb("minus_one", [P, 1], F32)
        slot_t = sb("slot_t", [P, 1], F32)
        att_h12 = sb("att_h12", [P, P], F32R)
        vals = sb("vals", [P, 2, KP], F32)
        idx = sb("idx", [P, TILES, KP], U32)
        own = sb("own", [P, 3, TILES], F32)
        tab = sb("tab", [P, B, 3, AB], F32)
        tab_rest = sb("tab_rest", [P, B, 3, AB], F32)
        tab_p = sb("tab_p", [P, 3, B, 3, AB], BF16)
        a_row = sb("a_row", [P, P], BF16)
        prm = sb("prm", [P, 77], F32)
        w_eff = sb("w_eff", [P, 6, 3], F32)
        stat = sb("stat", [P, 64], F32)
        small = sb("small", [P, 64], F32)

        a_rows = nc.dram_tensor("a_rows", [CHUNKS, P, P], BF16, kind="Internal").ap()
        att_d = nc.dram_tensor("att_d", [CHUNKS, P, NG * HALF], F32, kind="Internal").ap()
        w1_keep = nc.dram_tensor("w1_keep", [P, 2 * CT * C], F32, kind="Internal").ap()

        bank = [st.enter_context(nc.psum_tensor(f"bank{i}", [P, HALF], F32)) for i in range(8)]

        x_flat = X[:].rearrange("p b c n -> p (b c n)")
        stage = x_flat[:, 0:NS * N].rearrange("p (s n) -> p s n", s=NS)
        sq_half = [x_flat[:, (NS + b) * N:(NS + b + 1) * N] for b in range(B)]
        SC = 4
        score = scratch[:, 0:SC * N].rearrange("p (s n) -> p s n", s=SC)
        adj = scratch[:, SC * N:(SC + 1) * N].bitcast(BF16).rearrange("p (s n) -> p s n", s=2)
        acc = [scratch[:, (SC + 1) * N:(SC + 2) * N], sq_half[1]]
        w_raw = [x_flat[:, 2 * N:4 * N].rearrange("p (t c) -> p t c", t=CT),
                 scratch[:, 2 * N:4 * N].rearrange("p (t c) -> p t c", t=CT)]
        p_h, p_l = pts_h[:, 0:CT, :], pts_h[:, CT:2 * CT, :]
        y_h = pts_l[:, 0:CT, :].rearrange("p c n -> p (c n)").rearrange("p (m o) -> p m o", m=NT)
        y_l = pts_l[:, CT:2 * CT, :].rearrange("p c n -> p (c n)").rearrange("p (m o) -> p m o", m=NT)
        NB = 3
        KH = K1 // 2
        near = scratch[:, 0:3 * U].rearrange("p (j t k) -> p j t k", j=3, t=TILES)
        oh_r = scratch[:, 1440:1500].bitcast(BF16).rearrange("p (k r) -> p k r", k=KH)
        r_all = scratch[:, 1500:1756].bitcast(BF16).rearrange("p (t k) -> p t k", t=TILES)
        i_u = scratch[:, 1756:1884].bitcast(U32)
        a_f = scratch[:, 1884:2012]
        pick = scratch[:, 2012:2372].rearrange("p (k j r) -> p k j r", k=KH, j=3)
        bc = scratch[:, 2372:5252].bitcast(BF16).rearrange("p (s f) -> p s f", s=NB)
        att32 = scratch[:, 2400:2912].rearrange("p (t k) -> p t k", t=TILES)
        a_all = scratch[:, 2912:3424]
        r4_all = scratch[:, 3424:3936]
        i_all = scratch[:, 3936:4448].bitcast(U32)
        l_tmp = scratch[:, 4864:4992]
        aT = scratch[:, 0:256].bitcast(BF16)
        rT = scratch[:, 256:512].bitcast(BF16)
        att_q = scratch[:, 512:1536].bitcast(BF16).rearrange("p (i h n) -> p i h n", i=2, h=2)
        oa = [scratch[:, 1536 + 512 * i:2048 + 512 * i].bitcast(BF16).rearrange("p (a n) -> p a n", n=GN)
              for i in range(2)]
        eq = [scratch[:, 2560 + 128 * i:2688 + 128 * i].bitcast(BF16).rearrange("p (r n) -> p r n", n=GN)
              for i in range(2)]
        mv = [scratch[:, 2816 + 512 * i:3328 + 512 * i].bitcast(BF16)
              .rearrange("p (i h r n) -> p i h r n", n=GN, i=2, h=2) for i in range(2)]
        iota_a8 = idx[:].rearrange("p t k -> p (t k)").bitcast(BF16).rearrange("p (a n) -> p a n", n=GN)
        iota_r8 = scratch[:, 4992:5120].bitcast(BF16).rearrange("p (r n) -> p r n", n=GN)
        spread_s = [scratch[:, 3840 + 512 * i:4352 + 512 * i] for i in range(2)]
        w_flat = wT[:].rearrange("p h t c -> p (h t c)")
        att_flat = [nbr[:, i].rearrange("p m n -> p (m n)") for i in range(2)]
        att_T = [a.rearrange("p (q h r x) -> p h r q x", q=NG, h=2, r=AB) for a in att_flat]
        xT = [t[:].rearrange("p k n -> p (k n)").rearrange("p (h r c) -> p h r c", h=2, r=AB)
              for t in (pts_h, pts_l)]

        def p32(n):
            return scratch[:, 11 * U + (n % 2) * HALF:11 * U + (n % 2 + 1) * HALF]

        def slots(a, n=1):
            return scratch[:, a * U:(a + n) * U]

        s_w = sem("w_loaded")
        s_stage = [sem(f"stage_loaded{i}") for i in range(NS)]
        s_prm = sem("params_loaded")
        s_const = sem("consts_ready")
        s_wps = sem("w_transposed")
        s_wh = sem("w_high_ready")
        s_wl = sem("w_low_ready")
        s_wkeep = sem("w1_kept")
        s_wback = sem("w1_back")
        s_ph = sem("pts_high_ready")
        s_pl0 = sem("pts0_low_ready")
        s_pl1 = sem("pts1_low_ready")
        s_sq = sem("squares_ready")
        s_sqmm = sem("squares_used")
        s_nsq = sem("sq_half_ready")
        s_kdone = sem("pts_tile_used")
        s_g = sem("gram_ready")
        s_gc = sem("gram_copied")
        s_v = sem("scores_ready")
        s_add = [sem(f"squares_added{i}") for i in range(2)]
        s_top = sem("topk_step")
        s_near = sem("nearest_removed")
        s_sel = sem("selection_done")
        s_adj = sem("adj_ready")
        s_diag = sem("adj_diagonal_ready")
        s_adjT = sem("adj_transposed")
        s_nbr = sem("nbr_ready")
        s_x = [sem(f"x{b}_loaded") for b in range(B)]
        s_p32 = sem("p_ready")
        s_p0 = sem("p_high_ready")
        s_p1 = sem("p_low_ready")
        s_wm = sem("wp_done")
        s_yh = sem("y_high_ready")
        s_yl = sem("y_low_ready")
        s_m = sem("agg_done")
        s_xu = sem("x_updated")
        s_link = sem("dve_link")
        s_af = sem("a_index_ready")
        s_aT = sem("a_index_transposed")
        s_ar = sem("a_row_ready")
        s_arow = sem("a_rows_stored")
        s_bc = [sem(f"a_broadcast{i}") for i in range(NB)]
        s_oh = sem("onehot_ready")
        s_look = sem("lookup_done")
        s_pick = sem("lookup_read")
        s_tab = sem("table_ready")
        s_mlp = sem("mlp_to_act")
        s_act = sem("act_to_mlp")
        s_bnin = sem("bn_partial_ready")
        s_bnps = sem("bn_summed")
        s_att = sem("att_ready")
        s_scT = sem("att_transposed")
        s_sct = sem("att_columns_copied")
        s_h12 = sem("att_high_rounded")
        s_attq = sem("att_parts_ready")
        s_st = [sem(f"spread_stored{i}") for i in range(2)]
        s_back = sem("attention_loaded")
        s_oa = sem("a_onehot_ready")
        s_eq = sem("r_onehot_ready")
        s_mv = [sem(f"weighted_onehot{i}_ready") for i in range(2)]
        s_iota = sem("repeated_iotas_ready")
        s_sc = sem("spread_done")
        s_scc = sem("spread_copied")
        s_xT = sem("xT_done")
        s_xTh = sem("xT_high_ready")
        s_xTl = sem("xT_low_ready")
        s_f = sem("attended")
        s_fo = sem("result_ready")
        s_out = sem("out_stored")

        MLP = {e: n + 1 for n, e in enumerate(
            ("sqrt", "atan", "bn1s", "bn1a", "bn2s", "bn2a", "bn3s", "bn3a", "exp"))}
        DONE = {"sqrt": 1, "atan": 2, "bn1s": 3, "bn1a": 9, "bn2s": 10, "bn2a": 13, "bn3s": 14, "bn3a": 15,
                "exp": 16}
        G0 = 12
        R0 = 6
        M0 = G0 + 2 * TILES + 3
        T0 = M0 + 50
        S0 = T0 + 3
        S_END = 16 * ITS - S0
        TAIL = 4

        QUARTER = NG // 4
        FREE_AT = [13, S_END + 1, S_END + 4 * TAIL + 2, S_END + 8 * TAIL + 1]
        LOAD_AT = {}
        for c in range(CHUNKS):
            for j in range(4):
                q = max(NG * c + QUARTER * (j + 1) + 1, FREE_AT[c] + 2 * j)
                LOAD_AT.setdefault(min(q, CHUNKS * NG - 1), []).append((c, j))

        block = st.enter_context(nc.Block())

        def tail_groups(i):
            return range(min(S_END + TAIL * i, CHUNKS * NG), min(S_END + TAIL * (i + 1), CHUNKS * NG))

        def w_bank(n):
            return bank[(6, 7, 4, 5)[n % 4]][:]

        def weigh(engine, q, i):
            n0 = (q // NG) * P + (q % NG) * GN
            engine.tensor_tensor(mv[q % 2][:, i],
                                 eq[q % 2].unsqueeze(1).to_broadcast([P, 2, KP, GN]),
                                 att_q[:, i, :, n0:n0 + GN].unsqueeze(2).to_broadcast([P, 2, KP, GN]),
                                 ALU.mult).then_inc(s_mv[i], 1)

        @block.sync
        def _(sp):
            def load_stage(n):
                e = n - NS
                if e in (0, 1, KT):
                    sp.wait_ge(s_sq, e + 1)
                elif 0 <= e < KT:
                    sp.wait_ge(s_add[e % 2], e // 2)
                elif KT < e < 2 * KT:
                    sp.wait_ge(s_add[0], KT // 2 - 1 + e - KT)
                if 0 <= e < KT:
                    sp.wait_ge(s_pl0, e + 1)
                if e >= 2 * KT:
                    sp.wait_ge(s_pl1, e - 2 * KT + 1)
                b, k = (0 if n < KT else 1), n % KT
                sp.dma_start(stage[:, n % NS, :], ctx[b, k * P:(k + 1) * P, :]).then_inc(s_stage[n % NS], 16)

            for n in range(KT):
                load_stage(n)
            sp.dma_start(w_raw[1], fside[1].rearrange("(t p) c -> p t c", p=P)).then_inc(s_w, 16)
            for n in range(KT, KT + NS):
                load_stage(n)
            off = 0
            for w in (W1, g1, b1, W2, g2, b2, W3, g3, b3):
                n = int(np.prod(w.shape))
                flat = w.rearrange("a b -> (a b)") if len(w.shape) == 2 else w
                sp.dma_start(prm[:, off:off + n], flat.unsqueeze(0).to_broadcast([P, n])).then_inc(s_prm, 16)
                off += n
            for b in range(B):
                for j in range(3):
                    sp.dma_start(tab[:, b, j, :], ctx[b, 2 - j, :].rearrange("(a r) -> a r", r=AB)) \
                        .then_inc(s_prm, 16)
                    sp.dma_start(own[:, j, b * NT:(b + 1) * NT],
                                 ctx[b, 2 - j, :].rearrange("(t p) -> p t", p=P),
                                 allow_slow_non_contiguous=True).then_inc(s_prm, 16)
            sp.wait_ge(s_wh, CT)
            sp.wait_ge(s_wl, CT)
            sp.dma_start(w1_keep, w_flat.bitcast(F32)).then_inc(s_wkeep, 16)
            for n in range(KT + NS, 3 * NS + 2):
                load_stage(n)
            sp.wait_ge(s_add[0], KT // 2 - 1 + KT - 1)
            sp.dma_start(w_raw[0], fside[0].rearrange("(t p) c -> p t c", p=P)).then_inc(s_w, 16)
            sp.wait_ge(s_wps, 2 * CT)
            for n in range(3 * NS + 2, 3 * KT):
                load_stage(n)
            sp.wait_ge(s_pl1, KT)
            sp.dma_start(X[:, 0], x[0].rearrange("(t p) n -> p t n", p=P)).then_inc(s_x[0], 16)
            sp.wait_ge(s_v, TILES)
            sp.dma_start(X[:, 1], x[1].rearrange("(t p) n -> p t n", p=P)).then_inc(s_x[1], 16)
            sp.wait_ge(s_adjT, TILES)
            sp.wait_ge(s_sel, TILES)
            for c in range(CHUNKS):
                sp.wait_ge(s_ar, c + 1)
                sp.dma_start(a_rows[c], a_row[:]).then_inc(s_arow, 16)
                sp.wait_ge(s_arow, 16 * (c + 1))
                for t in range(2 * CH):
                    u = 2 * CH * c + t
                    if u >= NB:
                        sp.wait_ge(s_look, u - NB + 1)
                    k = (t // 2) * KP + (t % 2) * KH
                    sp.dma_start(bc[:, u % NB, :],
                                 a_rows[c, k:k + KH, :].rearrange("k n -> (k n)").unsqueeze(0)
                                 .to_broadcast([P, KH * P])).then_inc(s_bc[u % NB], 16)

            def load_attention(c, j):
                for i in range(2):
                    sp.wait_ge(s_st[i], 16 * (NG * c + QUARTER * (j + 1)) // 2)
                if c < 2:
                    sp.wait_ge(s_m, 2 * CT * (ITS - 1 + c))
                else:
                    sp.wait_ge(s_f, CT * (c - 1))
                cols = slice(QUARTER * HALF * j, QUARTER * HALF * (j + 1))
                sp.dma_start(att_flat[c % 2][:, cols].bitcast(F32), att_d[c][:, cols]).then_inc(s_back, 16)

            for q in range(CHUNKS * NG):
                sp.wait_ge(s_scc, q + 1)
                sp.dma_start(att_d[q // NG, :, (q % NG) * HALF:(q % NG + 1) * HALF],
                             spread_s[q % 2]).then_inc(s_st[q % 2], 16)
                for c, j in LOAD_AT.get(q, []):
                    load_attention(c, j)
            for c in range(CHUNKS):
                b, hf = c // NH, c % NH
                for t in range(CT):
                    sp.wait_ge(s_fo, CT * c + t + 1)
                    sp.dma_start(out[b, t * P:(t + 1) * P, hf * HALF:(hf + 1) * HALF],
                                 X[:, b, t, hf * HALF:(hf + 1) * HALF]).then_inc(s_out, 16)
            sp.wait_ge(s_out, 16 * CHUNKS * CT)

        @block.gpsimd
        def _(pool):
            pool.memset(ident[:], 0.0).then_inc(s_const, 1)
            pool.memset(neg_half[:], -0.5).then_inc(s_const, 1)
            pool.memset(mean_mat[:], 1.0 / P).then_inc(s_const, 1)
            pool.memset(minus_one[:], -1.0).then_inc(s_const, 1)
            pool.wait_ge(s_const, 4)
            pool.affine_select(out=ident[:], in_=ident[:], compare_op=ALU.not_equal, fill=1.0, base=0,
                               pattern=[[-1, P]], channel_multiplier=1).then_inc(s_const, 1)
            pool.iota(iota_r[:], pattern=[[1, KP]], base=0, channel_multiplier=0,
                      allow_small_or_imprecise_dtypes=True).then_inc(s_const, 1)
            pool.iota(part[:], pattern=[[0, 1]], base=0, channel_multiplier=1,
                      allow_small_or_imprecise_dtypes=True).then_inc(s_const, 1)
            for t in range(CH):
                pool.wait_ge(s_const, 7 + t)
                pool.memset(slot_t[t * KP:(t + 1) * KP, :], float(t)).then_inc(s_const, 1)
            pool.wait_ge(s_const, 7 + CH)
            pool.tensor_copy(ident_b[:], ident[:]).then_inc(s_const, 1)

            def low_part(k):
                n = 2 * KT + k
                pool.wait_ge(s_stage[n % NS], 16 * (n // NS + 1))
                pool.wait_ge(s_ph, KT + k + 1)
                pool.tensor_tensor(pts_l[:, k, :], stage[:, n % NS, :], pts_h[:, k, :].bitcast(F32),
                                   ALU.subtract).then_inc(s_pl1, 1)

            def add_norm(T):
                pool.wait_ge(s_nsq, 2 * (T // NT + 1))
                pool.wait_ge(s_gc, 2 * (T + 1))
                pool.tensor_tensor(score[:, T % SC, :], score[:, T % SC, :], sq_half[T // NT],
                                   ALU.add).then_inc(s_v, 1)

            def add_square(n):
                pool.wait_ge(s_sq, n + 1)
                pool.tensor_tensor(acc[0], acc[0], stage[:, n % NS, :], ALU.add).then_inc(s_add[0], 1)

            def diagonal(T):
                pool.wait_ge(s_adj, T + 1)
                diag = adj[:, T % 2, (T % NT) * P:(T % NT + 1) * P]
                pool.tensor_tensor(diag, diag, ident_b[:], ALU.add).then_inc(s_diag, 1)

            for n in (2, 4, 6):
                if n > 2:
                    pool.wait_ge(s_add[0], n // 2 - 1)
                add_square(n)
            POOL = {0: [], 1: [("d", 0)], 2: [("s", 1), ("s", 2), ("d", 1)], 3: [("s", 3), ("s", 4), ("s", 5)],
                    4: [("d", 2), ("d", 3)], 5: [("s", 6), ("s", 7)], 6: [("d", 4), ("d", 5)],
                    7: [("l", 0), ("l", 1), ("l", 2), ("l", 3)],
                    8: [("l", 4), ("l", 5), ("l", 6), ("l", 7), ("d", 6), ("d", 7)], 9: [],
                    10: [("d", 8), ("d", 9)], 11: [], 12: [], 13: [("d", 10), ("d", 11)], 14: [],
                    15: [("d", 12), ("d", 13)]}
            for T in range(TILES):
                for what, i in POOL[T]:
                    if what == "d":
                        diagonal(i)
                    elif what == "l":
                        low_part(i)
                    else:
                        pool.wait_ge(s_add[0], KT // 2 - 2 + i)
                        add_square(KT + i)
                add_norm(T)

            def p_low(n):
                hf, t = (n % (2 * CT)) // CT, n % CT
                pool.wait_ge(s_p0, n + 1)
                pool.tensor_tensor(p_l[:, t, hf * HALF:(hf + 1) * HALF], p32(n),
                                   p_h[:, t, hf * HALF:(hf + 1) * HALF].bitcast(F32),
                                   ALU.subtract).then_inc(s_p1, 1)

            def weight(q):
                c = q // NG
                pool.wait_ge(s_eq, q + 1)
                if q % NG == 0:
                    pool.wait_ge(s_attq, c + 1)
                if q >= 2:
                    pool.wait_ge(s_sc, q - 1)
                weigh(pool, q, 1)

            for n in range(2 * CT):
                p_low(n)
            for it in range(ITS):
                for s_ in range(16):
                    g = 16 * it + s_
                    if g == 1:
                        diagonal(TILES - 2)
                        diagonal(TILES - 1)
                    if g == T0:
                        pool.wait_ge(s_att, 1)
                        pool.iota(iota_a8, pattern=[[1, P], [0, GN]], base=0, channel_multiplier=0,
                                  allow_small_or_imprecise_dtypes=True).then_inc(s_iota, 1)
                        pool.iota(iota_r8, pattern=[[1, KP], [0, GN]], base=0, channel_multiplier=0,
                                  allow_small_or_imprecise_dtypes=True).then_inc(s_iota, 1)
                    if g >= S0:
                        weight(g - S0)
                    if s_ >= NT and it + 1 < ITS:
                        p_low(2 * CT * (it + 1) + s_ - NT)
            for q in range(S_END, CHUNKS * NG):
                weight(q)

        @block.scalar
        def _(act):
            def w_high(n):
                t = n % CT
                act.wait_ge(s_wps, n + 1)
                if n == CT:
                    act.wait_ge(s_wkeep, 16)
                act.copy(wT[:, 0, t, :], w_bank(n)).then_inc(s_wh, 1)

            def high_part(m):
                k, n = m % KT, m if m < KT else m + KT
                act.wait_ge(s_stage[n % NS], 16 * (n // NS + 1))
                if m >= KT:
                    act.wait_ge(s_kdone, k + 1)
                act.copy(pts_h[:, k, :], stage[:, n % NS, :]).then_inc(s_ph, 1)

            def square(n):
                if n in (0, 1, KT):
                    dst = acc[n % KT]
                else:
                    dst = stage[:, n % NS, :]
                if 1 < n < KT:
                    act.wait_ge(s_pl0, n + 1)
                elif n >= KT:
                    act.wait_ge(s_stage[n % NS], 16 * (n // NS + 1))
                act.activation(dst, stage[:, n % NS, :], ACT.Square).then_inc(s_sq, 1)

            def norm_out(b):
                act.wait_ge(s_sqmm, b + 1)
                for hf in range(NH):
                    act.copy(sq_half[b][:, hf * HALF:(hf + 1) * HALF], bank[4 + hf][:]).then_inc(s_nsq, 1)

            def gram_out(T):
                if T == NT - 1:
                    act.wait_ge(s_kdone, KT)
                else:
                    act.wait_ge(s_g, T + 1 if T < NT else T)
                if T == 2:
                    act.wait_ge(s_wps, CT)
                if T >= SC:
                    act.wait_ge(s_sel, T - SC + 1)
                for hf in range(NH):
                    act.copy(score[:, T % SC, hf * HALF:(hf + 1) * HALF], bank[2 * (T % 2) + hf][:]) \
                        .then_inc(s_gc, 1)

            def nbr_out(T):
                act.wait_ge(s_adjT, T + 1)
                act.copy(nbr[:, T // NT, :, (T % NT) * P:(T % NT + 1) * P],
                         bank[6 + T % 2][:].bitcast(BF16).rearrange("p (m n) -> p m n", m=NT)) \
                    .then_inc(s_nbr, 1)

            def adjacency(T):
                act.wait_ge(s_near, T + 1)
                if T >= 2:
                    act.wait_ge(s_adjT, T - 1)
                act.activation(adj[:, T % 2, :], score[:, T % SC, :], ACT.Relu, bias=minus_one[:, 0:1],
                               scale=2.0 / REMOVED).then_inc(s_adj, 1)

            high_part(0)
            for n in range(1, KT):
                high_part(n)
                square(n - 1)
            square(KT - 1)
            norm_out(0)
            gram_out(0)
            adjacency(0)
            gram_out(1)
            for n in range(CT):
                w_high(n)
            for n in range(KT, KT + 3):
                square(n)
            adjacency(1)
            gram_out(2)
            nbr_out(0)
            for n in range(KT + 3, KT + NS):
                square(n)
            gram_out(3)
            nbr_out(1)
            adjacency(2)
            adjacency(3)
            gram_out(4)
            for n in range(KT + NS, 2 * KT):
                square(n)
            gram_out(5)
            nbr_out(2)
            nbr_out(3)
            adjacency(4)
            adjacency(5)
            norm_out(1)
            gram_out(6)
            for n in range(CT, 2 * CT):
                w_high(n)
            for k in range(KT):
                high_part(KT + k)
            gram_out(7)
            nbr_out(4)
            nbr_out(5)
            adjacency(6)
            adjacency(7)
            gram_out(8)
            nbr_out(6)
            nbr_out(7)
            gram_out(9)
            adjacency(8)
            adjacency(9)
            gram_out(10)
            nbr_out(8)
            nbr_out(9)
            gram_out(11)
            gram_out(12)
            adjacency(10)
            adjacency(11)
            nbr_out(10)
            nbr_out(11)
            gram_out(13)
            gram_out(14)
            adjacency(12)
            adjacency(13)
            gram_out(15)
            nbr_out(12)
            nbr_out(13)

            def p_high(n):
                hf, t = (n % (2 * CT)) // CT, n % CT
                act.wait_ge(s_p32, n + 1)
                act.copy(p_h[:, t, hf * HALF:(hf + 1) * HALF], p32(n)).then_inc(s_p0, 1)

            def y_high(g):
                it, m = g // NT, g % NT
                act.wait_ge(s_wm, g + 1)
                if m == 0 and it:
                    act.wait_ge(s_m, 2 * CT * it)
                act.copy(y_h[:, m, :], bank[g % 3][:]).then_inc(s_yh, 1)

            def a_row_out(c):
                act.wait_ge(s_aT, c + 1)
                if c:
                    act.wait_ge(s_arow, 16 * c)
                act.copy(a_row[:], bank[6][:, 384:HALF]).then_inc(s_ar, 1)

            def bn_sqrt(ev, n):
                act.wait_ge(s_mlp, MLP[ev])
                act.activation(stat[:, 40:40 + n], stat[:, 34:34 + n], ACT.Sqrt).then_inc(s_act, 1)

            def bn_apply(ev, first, n):
                act.wait_ge(s_mlp, MLP[ev])
                for c in range(n):
                    act.activation(slots(first + c), slots(first + c), ACT.Identity, bias=stat[:, 58 + c:59 + c],
                                   scale=stat[:, 52 + c:53 + c]).then_inc(s_act, 1)

            def side(g):
                if g == 1:
                    adjacency(TILES - 2)
                    adjacency(TILES - 1)
                if g == 3:
                    nbr_out(TILES - 2)
                    nbr_out(TILES - 1)
                if (g - R0) % 8 == 2 and 0 <= (g - R0) // 8 < CHUNKS:
                    a_row_out((g - R0) // 8)
                if g == 16 + NT:
                    act.wait_ge(s_wm, 2 * NT)
                    act.dma_start(w_flat.bitcast(F32), w1_keep).then_inc(s_wback, 16)
                m = g - M0
                if m == 4:
                    act.wait_ge(s_mlp, MLP["sqrt"])
                    act.activation(slots(6, 2), slots(4, 2), ACT.Sqrt).then_inc(s_act, 1)
                if m == 10:
                    act.wait_ge(s_mlp, MLP["atan"])
                    act.activation(slots(6, 2), slots(8, 2), ACT.Arctan).then_inc(s_act, 1)
                if m == 25:
                    bn_sqrt("bn1s", 6)
                if m == 26:
                    bn_apply("bn1a", 0, 6)
                if m == 38:
                    bn_sqrt("bn2s", 3)
                if m == 39:
                    bn_apply("bn2a", 6, 3)
                if m == 45:
                    bn_sqrt("bn3s", 1)
                if m == 46:
                    bn_apply("bn3a", 0, 1)
                if m == 47:
                    act.wait_ge(s_mlp, MLP["exp"])
                    act.activation(slots(1), slots(0), ACT.Exp).then_inc(s_act, 1)
                if g == T0 + 1:
                    columns()
                if g in (T0 + 2, T0 + 3):
                    round_high(2 * (g - T0 - 2))
                if g >= S0:
                    spread_out(g - S0)
                if g >= 16 * ITS - AB:
                    xT_high(g - 16 * ITS + AB)

            def columns():
                act.wait_ge(s_scT, 1)
                act.copy(aT, bank[6][:]).then_inc(s_sct, 1)
                act.wait_ge(s_scT, 2)
                act.activation(rT, bank[7][:], ACT.Identity, bias=slot_t[:, 0:1]).then_inc(s_sct, 1)

            def round_high(c0):
                act.wait_ge(s_scT, 3)
                for c in (c0, c0 + 1):
                    if c:
                        act.wait_ge(s_attq, c)
                    act.copy(att_h12[:], bank[6][:, c * P:(c + 1) * P]).then_inc(s_h12, 1)

            def spread_out(q):
                act.wait_ge(s_sc, q + 1)
                if q >= 2:
                    act.wait_ge(s_st[q % 2], 16 * (q // 2))
                act.copy(spread_s[q % 2].rearrange("p (x n) -> p n x", n=GN),
                         bank[6 + q % 2][:].rearrange("p (n x) -> p n x", n=GN)).then_inc(s_scc, 1)

            def xT_high(n):
                act.wait_ge(s_xT, n + 1)
                act.copy(xT[n // AB][:, 0, n % AB, :], bank[n % 2][:]).then_inc(s_xTh, 1)

            for j in range(2 * CT):
                p_high(j)
            for it in range(ITS):
                for m in range(NT):
                    y_high(NT * it + m)
                    side(16 * it + m)
                for j in range(2 * CT):
                    if it + 1 < ITS:
                        p_high(2 * CT * (it + 1) + j)
                    side(16 * it + NT + j)

            for i in range(CHUNKS * CT):
                for n, q in enumerate(tail_groups(i)):
                    if n == 2 and i < AB:
                        xT_high(AB + i)
                    spread_out(q)

        @block.vector
        def _(dve):
            chain = [0]

            def link(ins):
                chain[0] += 1
                ins.then_inc(s_link, 1)
                dve.wait_ge(s_link, chain[0])

            def w_low(n):
                t = n % CT
                dve.wait_ge(s_wh, n + 1)
                dve.tensor_tensor(wT[:, 1, t, :], w_bank(n), wT[:, 0, t, :].bitcast(F32),
                                  ALU.subtract).then_inc(s_wl, 1)

            def pts_low(k):
                dve.wait_ge(s_ph, k + 1)
                dve.tensor_tensor(pts_l[:, k, :], stage[:, k % NS, :], pts_h[:, k, :].bitcast(F32),
                                  ALU.subtract).then_inc(s_pl0, 1)

            top_step = [0]
            after = {}

            def select_step(T, n):
                r, kind = n // 3, n % 3
                v, top = score[:, T % SC, :], vals[:, T % 2, 8 * r:8 * r + 8]
                if n == 0:
                    dve.wait_ge(s_v, T + 1)
                elif n == 3:
                    dve.wait_ge(s_near, T + 1)
                else:
                    dve.wait_ge(s_top, after[T])
                if n == 5:
                    dve.wait_ge(s_adj, T + 1)
                if kind == 0:
                    ins = dve.max(top, v)
                elif kind == 1:
                    ins = dve.max_index(idx[:, T, 8 * r:8 * r + 8], top, v)
                else:
                    ins = dve.match_replace(v, top, v, REMOVED)
                if n == 2:
                    ins.then_inc(s_near, 1)
                elif n == STEPS - 1:
                    ins.then_inc(s_sel, 1)
                else:
                    top_step[0] += 1
                    after[T] = top_step[0]
                    ins.then_inc(s_top, 1)

            STEPS = 3 * (KP // 8) - 1

            def select(tiles):
                for n in range(STEPS):
                    for T in tiles:
                        select_step(T, n)

            dve.wait_ge(s_const, 8 + CH)
            for k in range(KT):
                pts_low(k)
                if k >= 3 and k % 2:
                    dve.wait_ge(s_sq, k + 1)
                    if k > 3:
                        dve.wait_ge(s_add[1], k // 2 - 1)
                    dve.tensor_tensor(acc[1], acc[1], stage[:, k % NS, :], ALU.add).then_inc(s_add[1], 1)
            select([0])
            for n in range(CT):
                w_low(n)
            select([1])
            select([2, 3])
            select([4, 5])
            for n in range(CT, 2 * CT):
                w_low(n)
            dve.wait_ge(s_prm, 16 * (9 + 6 * B))
            link(dve.tensor_copy(tab_p[:, 0], tab[:]))
            link(dve.tensor_tensor(tab_rest[:], tab[:], tab_p[:, 0], ALU.subtract))
            link(dve.tensor_copy(tab_p[:, 1], tab_rest[:]))
            link(dve.tensor_tensor(tab_rest[:], tab_rest[:], tab_p[:, 1], ALU.subtract))
            dve.tensor_copy(tab_p[:, 2], tab_rest[:]).then_inc(s_tab, 1)
            for T in range(6, TILES - 2, 2):
                select([T, T + 1])

            def p_make(n):
                it = n // (2 * CT)
                b, hf, t = it % B, (n % (2 * CT)) // CT, n % CT
                if it < B:
                    dve.wait_ge(s_x[b], 16)
                else:
                    dve.wait_ge(s_xu, 2 * CT * (it - 1))
                if it and n % (2 * CT) == 0:
                    dve.wait_ge(s_wm, NT * it)
                if n >= 2:
                    dve.wait_ge(s_p1, n - 1)
                src = X[:, b, t, hf * HALF:(hf + 1) * HALF]
                dve.scalar_tensor_tensor(p32(n), src, SLOPE0, src, ALU.mult, ALU.max).then_inc(s_p32, 1)

            def y_low(g):
                m = g % NT
                dve.wait_ge(s_yh, g + 1)
                dve.tensor_tensor(y_l[:, m, :], bank[g % 3][:], y_h[:, m, :].bitcast(F32),
                                  ALU.subtract).then_inc(s_yl, 1)

            def x_update(g):
                it, j = g // (2 * CT), g % (2 * CT)
                b, hf, t = it % B, j // CT, j % CT
                dst = X[:, b, t, hf * HALF:(hf + 1) * HALF]
                dve.wait_ge(s_m, g + 1)
                dve.scalar_tensor_tensor(dst, bank[3 + g % 3][:], 1.0 / (K0 + 1.0), dst,
                                         ALU.mult, ALU.add).then_inc(s_xu, 1)

            def index_rows(c):
                src = idx[:, CH * c:CH * (c + 1), :].rearrange("p t k -> p (t k)")
                if c:
                    dve.wait_ge(s_aT, c)
                link(dve.tensor_scalar(i_u, src, 3, None, ALU.logical_shift_right))
                link(dve.tensor_copy(a_f, i_u))
                link(dve.tensor_scalar(i_u, src, AB - 1, None, ALU.bitwise_and))
                dve.tensor_copy(r_all[:, CH * c:CH * (c + 1), :].rearrange("p t k -> p (t k)"), i_u) \
                    .then_inc(s_af, 1)

            def onehot_a(u):
                dve.wait_ge(s_bc[u % NB], 16 * (u // NB + 1))
                dve.tensor_scalar(bc[:, u % NB, :], bc[:, u % NB, :], part[:, 0:1], None, ALU.is_equal) \
                    .then_inc(s_oh, 1)

            def pick_r(u):
                T, k0 = u // 2, (u % 2) * KH
                dve.wait_ge(s_af, T // CH + 1)
                link(dve.tensor_tensor(oh_r, r_all[:, T, k0:k0 + KH].unsqueeze(2).to_broadcast([P, KH, AB]),
                                       iota_r[:, 0:AB].unsqueeze(1).to_broadcast([P, KH, AB]), ALU.is_equal))
                dve.wait_ge(s_look, u + 1)
                dve.tensor_tensor(pick, bank[6 + u % 2][:, 0:3 * KH * AB]
                                  .rearrange("p (k j r) -> p k j r", k=KH, j=3),
                                  oh_r.unsqueeze(2).to_broadcast([P, KH, 3, AB]), ALU.mult).then_inc(s_pick, 1)
                dve.wait_ge(s_pick, u + 1)
                link(dve.tensor_reduce(near[:, :, T, k0:k0 + KH], pick.rearrange("p k j r -> p j k r"),
                                       AX_X, ALU.add))

            def tt(o, a, b_, op):
                link(dve.tensor_tensor(o, a, b_, op))

            def ts(o, a, s1, op0, s2=None, op1=None):
                if op1 is None:
                    link(dve.tensor_scalar(o, a, s1, None, op0))
                else:
                    link(dve.tensor_scalar(o, a, s1, s2, op0, op1))

            def stt(o, a, s_, b_, op0, op1):
                link(dve.scalar_tensor_tensor(o, a, s_, b_, op0, op1))

            def mix(first, src, ws, fresh=True):
                for j, a in enumerate(src):
                    for c, w in enumerate(ws(j)):
                        if j == 0 and fresh:
                            ts(slots(first + c), slots(a), w, ALU.mult)
                        else:
                            stt(slots(first + c), slots(a), w, slots(first + c), ALU.mult, ALU.add)

            def bn_partial(first, n, some, last):
                for c in some:
                    link(dve.bn_stats(small[:, 6 * c:6 * c + 6], slots(first + c)))
                for c in some:
                    link(dve.bn_aggr(small[:, 40 + 2 * c:42 + 2 * c], small[:, 6 * c:6 * c + 6]))
                if not last:
                    return
                pair = small[:, 40:40 + 2 * n].rearrange("p (c s) -> p s c", s=2)
                ts(stat[:, 0:n], pair[:, 0], 1.0, ALU.mult)
                tt(stat[:, n:2 * n], pair[:, 0], pair[:, 0], ALU.mult)
                dve.tensor_tensor(stat[:, n:2 * n], stat[:, n:2 * n], pair[:, 1], ALU.add).then_inc(s_bnin, 1)

            def bn_variance(layer, n, ev):
                dve.wait_ge(s_bnps, layer)
                ts(stat[:, 16:16 + 2 * n], bank[7][:, 480:480 + 2 * n], 1.0, ALU.mult)
                tt(stat[:, 28:28 + n], stat[:, 16:16 + n], stat[:, 16:16 + n], ALU.mult)
                tt(stat[:, 34:34 + n], stat[:, 16 + n:16 + 2 * n], stat[:, 28:28 + n], ALU.subtract)
                dve.tensor_scalar(stat[:, 34:34 + n], stat[:, 34:34 + n], EPS_BN, None,
                                  ALU.add).then_inc(s_mlp, 1)

            def bn_coefficients(n, gain, bias, ev):
                y, t, v = stat[:, 46:46 + n], stat[:, 28:28 + n], stat[:, 34:34 + n]
                dve.wait_ge(s_act, DONE[ev])
                link(dve.reciprocal(y, stat[:, 40:40 + n]))
                tt(t, y, y, ALU.mult)
                tt(t, t, v, ALU.mult)
                ts(t, t, -0.5, ALU.mult, 1.5, ALU.add)
                tt(y, y, t, ALU.mult)
                tt(stat[:, 52:52 + n], y, prm[:, gain:gain + n], ALU.mult)
                tt(t, stat[:, 16:16 + n], stat[:, 52:52 + n], ALU.mult)
                dve.tensor_tensor(stat[:, 58:58 + n], prm[:, bias:bias + n], t,
                                  ALU.subtract).then_inc(s_mlp, 1)

            def leaky(first, n, ev):
                dve.wait_ge(s_act, DONE[ev])
                h = slots(first, n)
                stt(h, h, SLOPE1, h, ALU.mult, ALU.max)

            own_k = own[:].unsqueeze(3).to_broadcast([P, 3, TILES, K1])

            def grid(a):
                return slots(a).rearrange("p (t k) -> p t k", t=TILES)

            def network(n):
                Y, Xa, S, R = slots(0, 2), slots(2, 2), slots(4), slots(5)
                A, T_ = slots(6, 2), slots(8, 2)
                if n == 0:
                    tt(grid(0), grid(0), own_k[:, 0], ALU.subtract)
                    tt(grid(1), grid(1), own_k[:, 1], ALU.subtract)
                    tt(grid(3), grid(2), own_k[:, 2], ALU.subtract)
                if n == 1:
                    tt(S, slots(3), slots(3), ALU.mult)
                    tt(R, slots(1), slots(1), ALU.mult)
                    tt(S, S, R, ALU.add)
                if n == 2:
                    tt(R, slots(0), slots(0), ALU.mult)
                    tt(R, S, R, ALU.add)
                    stt(slots(0), R, TINY, slots(0), ALU.is_ge, ALU.mult)
                if n == 3:
                    stt(slots(1), S, TINY, slots(1), ALU.is_ge, ALU.mult)
                    stt(slots(3), S, TINY, slots(3), ALU.is_ge, ALU.mult)
                if n == 4:
                    stt(slots(3), S, TINY, slots(3), ALU.is_lt, ALU.add)
                    dve.tensor_scalar(slots(4, 2), slots(4, 2), TINY, None, ALU.max).then_inc(s_mlp, 1)
                if n == 5:
                    dve.wait_ge(s_act, DONE["sqrt"])
                    link(dve.reciprocal(T_, A))
                    tt(T_, T_, slots(4, 2), ALU.mult)
                if n == 6:
                    tt(T_, T_, A, ALU.add)
                    ts(slots(2), slots(8), 0.5, ALU.mult)
                    ts(slots(10), slots(9), 0.5, ALU.mult)
                if n == 7:
                    stt(slots(4, 2), Y, -1.0, Y, ALU.mult, ALU.max)
                    stt(A, Xa, -1.0, Xa, ALU.mult, ALU.max)
                if n == 8:
                    tt(T_, slots(4, 2), A, ALU.min)
                    tt(A, slots(4, 2), A, ALU.max)
                if n == 9:
                    tt(slots(4, 2), slots(4, 2), A, ALU.is_ge)
                    link(dve.reciprocal(A, A))
                if n == 10:
                    dve.tensor_tensor(T_, T_, A, ALU.mult).then_inc(s_mlp, 1)
                    w = prm[:, 0:36].rearrange("p (c j) -> p c j", c=6)
                    link(dve.tensor_reduce(small[:, 0:6], w[:, :, 3:6], AX_X, ALU.add))
                    ts(small[:, 0:6], small[:, 0:6], -1.0 / 3.0, ALU.mult)
                    tt(w_eff[:], w[:, :, 0:3], w[:, :, 3:6], ALU.add)
                    tt(w_eff[:], w_eff[:], small[:, 0:6].unsqueeze(2).to_broadcast([P, 6, 3]), ALU.add)
                if n == 11:
                    dve.wait_ge(s_act, DONE["atan"])
                    ts(T_, A, -2.0, ALU.mult, PI / 2, ALU.add)
                    tt(T_, T_, slots(4, 2), ALU.mult)
                if n == 12:
                    tt(A, A, T_, ALU.add)
                    ts(T_, A, -2.0, ALU.mult, PI, ALU.add)
                if n == 13:
                    stt(T_, Xa, 0.0, T_, ALU.is_lt, ALU.mult)
                    tt(A, A, T_, ALU.add)
                if n == 14:
                    ts(T_, Y, 0.0, ALU.is_ge, 2.0, ALU.mult)
                    stt(A, T_, -1.0, A, ALU.add, ALU.mult)
                if 15 <= n < 21:
                    c = n - 15
                    mix(c, (10, 6, 7), lambda j: [w_eff[:, c, j:j + 1]])
                if n == 21:
                    bn_partial(0, 6, range(3), False)
                if n == 22:
                    bn_partial(0, 6, range(3, 6), True)
                if n == 25:
                    bn_variance(1, 6, "bn1s")
                if n == 26:
                    bn_coefficients(6, 36, 42, "bn1s")
                if n == 27:
                    leaky(0, 3, "bn1a")
                if n == 28:
                    leaky(3, 3, "bn1a")
                if 29 <= n < 35:
                    c, hf = (n - 29) // 2, (n - 29) % 2
                    mix(6 + c, range(3 * hf, 3 * hf + 3),
                        lambda j: [prm[:, 48 + 6 * c + 3 * hf + j:49 + 6 * c + 3 * hf + j]], hf == 0)
                if n == 35:
                    bn_partial(6, 3, range(3), True)
                if n == 38:
                    bn_variance(2, 3, "bn2s")
                if n == 39:
                    bn_coefficients(3, 66, 69, "bn2s")
                if n == 40:
                    leaky(6, 3, "bn2a")
                if n == 41:
                    mix(0, (6, 7, 8), lambda j: [prm[:, 72 + j:73 + j]])
                if n == 42:
                    bn_partial(0, 1, range(1), True)
                if n == 45:
                    bn_variance(3, 1, "bn3s")
                if n == 46:
                    bn_coefficients(1, 75, 76, "bn3s")
                if n == 47:
                    leaky(0, 1, "bn3a")
                    link(dve.tensor_reduce(small[:, 0:TILES], grid(0), AX_X, ALU.max))
                    dve.tensor_tensor(grid(0), grid(0), small[:, 0:TILES].unsqueeze(2)
                                      .to_broadcast([P, TILES, K1]), ALU.subtract).then_inc(s_mlp, 1)
                if n == 48:
                    dve.wait_ge(s_act, DONE["exp"])
                    link(dve.tensor_reduce(small[:, 16:16 + TILES], grid(1), AX_X, ALU.add))
                    link(dve.reciprocal(small[:, 32:32 + TILES], small[:, 16:16 + TILES]))
                    link(dve.memset(att32[:, :, K1:KP], 0.0))
                    tt(att32[:, :, 0:K1], grid(1), small[:, 32:32 + TILES].unsqueeze(2)
                       .to_broadcast([P, TILES, K1]), ALU.mult)

            def index_columns():
                src = idx[:].rearrange("p t k -> p (t k)")
                link(dve.tensor_scalar(i_all, src, 3, None, ALU.logical_shift_right))
                link(dve.tensor_copy(a_all, i_all))
                link(dve.tensor_scalar(i_all, src, AB - 1, None, ALU.bitwise_and))
                dve.tensor_scalar(r4_all, i_all, float(CH), None, ALU.mult).then_inc(s_att, 1)

            def att_parts(c):
                cols = slice(c * P, (c + 1) * P)
                dve.wait_ge(s_h12, c + 1)
                h = att_h12[:].bitcast(F32)
                link(dve.tensor_copy(att_q[:, 0, 0, cols], h))
                link(dve.tensor_tensor(att_q[:, 1, 0, cols], h, att_q[:, 0, 0, cols], ALU.subtract))
                link(dve.tensor_tensor(l_tmp, bank[6][:, cols], h, ALU.subtract))
                link(dve.tensor_copy(att_q[:, 0, 1, cols], l_tmp))
                dve.tensor_tensor(att_q[:, 1, 1, cols], l_tmp, att_q[:, 0, 1, cols],
                                  ALU.subtract).then_inc(s_attq, 1)

            def onehots(q):
                n0 = (q // NG) * P + (q % NG) * GN
                if q == 0:
                    dve.wait_ge(s_sct, 2)
                    dve.wait_ge(s_iota, 2)
                    dve.wait_ge(s_attq, CHUNKS)
                if q >= 2:
                    dve.wait_ge(s_sc, q - 1)
                    dve.wait_ge(s_mv[1], q - 1)
                dve.tensor_tensor(eq[q % 2], rT[:, n0:n0 + GN].unsqueeze(1).to_broadcast([P, KP, GN]),
                                  iota_r8, ALU.is_equal).then_inc(s_eq, 1)
                dve.tensor_tensor(oa[q % 2], aT[:, n0:n0 + GN].unsqueeze(1).to_broadcast([P, P, GN]),
                                  iota_a8, ALU.is_equal).then_inc(s_oa, 1)
                dve.wait_ge(s_eq, q + 1)
                weigh(dve, q, 0)

            def xT_low(n):
                dve.wait_ge(s_xTh, n + 1)
                dve.tensor_tensor(xT[n // AB][:, 1, n % AB, :], bank[n % 2][:],
                                  xT[n // AB][:, 0, n % AB, :].bitcast(F32), ALU.subtract).then_inc(s_xTl, 1)

            def side(g):
                if g < STEPS - 2:
                    for T in (TILES - 2, TILES - 1):
                        select_step(T, g + 2)
                if (g - R0) % 8 == 0 and 0 <= (g - R0) // 8 < CHUNKS:
                    index_rows((g - R0) // 8)
                if G0 <= g < G0 + 2 * TILES:
                    onehot_a(g - G0)
                if G0 + 2 <= g < G0 + 2 + 2 * TILES:
                    pick_r(g - G0 - 2)
                if M0 <= g < M0 + 49:
                    network(g - M0)
                if g == M0 + 49:
                    index_columns()
                if g == T0 + 2:
                    att_parts(0)
                    att_parts(1)
                if g == T0 + 3:
                    att_parts(2)
                    att_parts(3)
                if g >= S0:
                    onehots(g - S0)
                if g > 16 * ITS - AB:
                    xT_low(g - 16 * ITS + AB - 1)

            for j in range(2 * CT):
                p_make(j)
                if j in (1, 3):
                    for T in (TILES - 2, TILES - 1):
                        select_step(T, j // 2)
            for it in range(ITS):
                for m in range(NT):
                    side(16 * it + m)
                    y_low(NT * it + m)
                for j in range(2 * CT):
                    side(16 * it + NT + j)
                    x_update(2 * CT * it + j)
                    if it + 1 < ITS:
                        p_make(2 * CT * (it + 1) + j)

            def result(i):
                c, t = i // CT, i % CT
                b, hf = c // NH, c % NH
                dve.wait_ge(s_f, i + 1)
                dst = X[:, b, t, hf * HALF:(hf + 1) * HALF].rearrange("p (t q n) -> p q t n", t=CH, n=GN)
                dve.tensor_tensor(dst, bank[4 + t % 2][:].rearrange("p (q t n) -> p q t n", q=NG, t=CH),
                                  dst, ALU.add).then_inc(s_fo, 1)

            xT_low(AB - 1)
            for i in range(CHUNKS * CT):
                for n, q in enumerate(tail_groups(i)):
                    onehots(q)
                    if n == 1 and i:
                        result(i - 1)
                    if n == 3 and i < AB:
                        xT_low(AB + i)
                if i and not tail_groups(i):
                    result(i - 1)
            result(CHUNKS * CT - 1)

        @block.tensor
        def _(pe):
            def w_turn(n):
                i, t = 1 - n // CT, n % CT
                pe.wait_ge(s_w, 16 * (n // CT + 1))
                if n == CT:
                    pe.wait_ge(s_wl, CT)
                    pe.wait_ge(s_nbr, 4)
                if n % CT == 2:
                    pe.wait_ge(s_nsq, 2 * (n // CT + 1))
                for o in range(CT):
                    mm = pe.transpose(w_bank(n)[:, o * P:(o + 1) * P],
                                      w_raw[i][:, o, t * P:(t + 1) * P], ident[:])
                mm.then_inc(s_wps, 1)

            def norms(b):
                if b == 0:
                    for i in range(2):
                        pe.wait_ge(s_add[i], KT // 2 - 1)
                else:
                    pe.wait_ge(s_add[0], KT // 2 - 1 + KT - 1)
                    pe.wait_ge(s_wl, CT)
                sums = acc if b == 0 else acc[:1]
                for hf in range(NH):
                    for i, a in enumerate(sums):
                        mm = pe.matmul(bank[4 + hf][:], neg_half[:], a[:, hf * HALF:(hf + 1) * HALF],
                                       start=(i == 0), stop=(i == len(sums) - 1))
                mm.then_inc(s_sqmm, 1)

            def gram(T):
                b, t = T // NT, T % NT
                if T >= 2:
                    pe.wait_ge(s_gc, 2 * (T - 1))
                for k in range(KT):
                    if t == 0:
                        pe.wait_ge((s_pl0, s_pl1)[b], k + 1)
                    rows = slice(t * P, (t + 1) * P)
                    for hf in range(NH):
                        cols = slice(hf * HALF, (hf + 1) * HALF)
                        o = bank[2 * (T % 2) + hf][:]
                        pe.matmul(o, pts_h[:, k, rows], pts_h[:, k, cols], start=(k == 0), stop=False)
                        pe.matmul(o, pts_h[:, k, rows], pts_l[:, k, cols], start=False, stop=False)
                        mm = pe.matmul(o, pts_l[:, k, rows], pts_h[:, k, cols], start=False,
                                       stop=(k == KT - 1))
                    if T == NT - 1:
                        mm.then_inc(s_kdone, 1)
                if T != NT - 1:
                    mm.then_inc(s_g, 1)

            def adj_turn(T):
                pe.wait_ge(s_diag, T + 1)
                if T in (0, 4):
                    pe.wait_ge(s_wl, CT if T == 0 else 2 * CT)
                if T >= 2:
                    pe.wait_ge(s_nbr, T - 1)
                for m in range(NT):
                    mm = pe.transpose(bank[6 + T % 2][:].bitcast(BF16)[:, m * P:(m + 1) * P],
                                      adj[:, T % 2, m * P:(m + 1) * P], ident_b[:])
                mm.then_inc(s_adjT, 1)

            pe.wait_ge(s_const, 8 + CH)
            PE_ORDER = [("g", 0), ("n", 0), ("g", 1), ("w", 0), ("g", 2), ("a", 0), ("g", 3), ("a", 1),
                        ("g", 4), ("g", 5), ("a", 2), ("a", 3), ("n", 1), ("g", 6), ("w", 1), ("g", 7),
                        ("a", 4), ("a", 5), ("g", 8), ("a", 6), ("a", 7), ("g", 9), ("g", 10), ("a", 8), ("a", 9), ("g", 11),
                        ("g", 12), ("a", 10), ("a", 11), ("g", 13), ("g", 14), ("g", 15), ("a", 12), ("a", 13)]
            for what, i in PE_ORDER:
                if what == "g":
                    gram(i)
                elif what == "n":
                    norms(i)
                elif what == "a":
                    adj_turn(i)
                else:
                    for n in range(CT * i, CT * (i + 1)):
                        w_turn(n)

            def wp(g):
                it, m = g // NT, g % NT
                if m in (0, NT // 2):
                    pe.wait_ge(s_p1, 2 * CT * it + (CT if m == 0 else 2 * CT))
                if g == 2 * NT:
                    pe.wait_ge(s_wback, 16)
                if g >= 3:
                    pe.wait_ge(s_yl, g - 2)
                elif g == 0:
                    pe.wait_ge(s_gc, 2 * TILES)
                cols = slice(m * P, (m + 1) * P)
                for t in range(CT):
                    pe.matmul(bank[g % 3][:], p_h[:, t, cols], wT[:, 0, t, :], start=(t == 0), stop=False)
                    pe.matmul(bank[g % 3][:], p_h[:, t, cols], wT[:, 1, t, :], start=False, stop=False)
                    mm = pe.matmul(bank[g % 3][:], p_l[:, t, cols], wT[:, 0, t, :], start=False,
                                   stop=(t == CT - 1))
                mm.then_inc(s_wm, 1)

            def aggregate(g):
                it, j = g // (2 * CT), g % (2 * CT)
                b, hf, t = it % B, j // CT, j % CT
                if it < B and j == 0:
                    pe.wait_ge(s_nbr, NT * (it + 1))
                if g >= 3:
                    pe.wait_ge(s_xu, g - 2)
                for m in range(NT):
                    if j == 0:
                        pe.wait_ge(s_yl, NT * it + m + 1)
                    for part_, y in enumerate((y_h, y_l)):
                        mm = pe.matmul(bank[3 + g % 3][:], y[:, m, t * P:(t + 1) * P],
                                       nbr[:, b, m, hf * HALF:(hf + 1) * HALF],
                                       start=(m == 0 and part_ == 0), stop=(m == NT - 1 and part_ == 1))
                mm.then_inc(s_m, 1)

            def turn_a(c):
                pe.wait_ge(s_af, c + 1)
                if c:
                    pe.wait_ge(s_ar, c)
                    pe.wait_ge(s_pick, 8 * c + R0 - G0 + 1)
                else:
                    pe.wait_ge(s_nbr, TILES)
                pe.transpose(bank[6][:, 384:HALF], a_f, ident[:]).then_inc(s_aT, 1)

            def lookup(u):
                pe.wait_ge(s_oh, u + 1)
                if u >= 2:
                    pe.wait_ge(s_pick, u - 1)
                pe.wait_ge(s_ar, min((u + G0 - R0 - 2) // 8 + 1, CHUNKS))
                b = u // (2 * NT)
                for k in range(KH):
                    for i in range(3):
                        mm = pe.matmul(bank[6 + u % 2][:, k * 3 * AB:(k + 1) * 3 * AB],
                                       bc[:, u % NB, k * P:(k + 1) * P],
                                       tab_p[:, i, b].rearrange("p j r -> p (j r)"),
                                       start=(i == 0), stop=(i == 2))
                mm.then_inc(s_look, 1)

            def bn_sum(layer, n):
                pe.wait_ge(s_bnin, layer)
                pe.matmul(bank[7][:, 480:480 + 2 * n], mean_mat[:], stat[:, 0:2 * n],
                          start=True, stop=True).then_inc(s_bnps, 1)

            def side(g):
                if g == 2:
                    adj_turn(TILES - 2)
                    adj_turn(TILES - 1)
                if G0 < g <= G0 + 2 * TILES:
                    lookup(g - G0 - 1)
                if (g - R0) % 8 == 2 and 0 <= (g - R0) // 8 < CHUNKS:
                    turn_a((g - R0) // 8)
                m = g - M0
                if m == 24:
                    bn_sum(1, 6)
                if m == 37:
                    bn_sum(2, 3)
                if m == 44:
                    bn_sum(3, 1)
                if g == T0 + 1:
                    turn_att()
                if g > S0:
                    spread(g - S0 - 1)
                if g == 16 * ITS - 1:
                    spread(g - S0)
                if g >= 16 * ITS - AB:
                    turn_x(g - 16 * ITS + AB)

            def turn_att():
                pe.wait_ge(s_att, 1)
                for c in range(CHUNKS):
                    mm = pe.transpose(bank[6][:, c * P:(c + 1) * P], a_all[:, c * P:(c + 1) * P], ident[:])
                mm.then_inc(s_scT, 1)
                for c in range(CHUNKS):
                    mm = pe.transpose(bank[7][:, c * P:(c + 1) * P], r4_all[:, c * P:(c + 1) * P], ident[:])
                mm.then_inc(s_scT, 1)
                pe.wait_ge(s_sct, 1)
                for c in range(CHUNKS):
                    mm = pe.transpose(bank[6][:, c * P:(c + 1) * P],
                                      att32[:, CH * c:CH * (c + 1), :].rearrange("p t k -> p (t k)"), ident[:])
                mm.then_inc(s_scT, 1)

            def spread(q):
                pe.wait_ge(s_oa, q + 1)
                pe.wait_ge(s_mv[0], q + 1)
                pe.wait_ge(s_mv[1], q + 1)
                if q == 0:
                    pe.wait_ge(s_attq, CHUNKS)
                if q >= 2:
                    pe.wait_ge(s_scc, q - 1)
                for n in range(GN):
                    for i in range(2):
                        mm = pe.matmul(bank[6 + q % 2][:, n * 2 * KP:(n + 1) * 2 * KP], oa[q % 2][:, :, n],
                                       mv[q % 2][:, i, :, :, n].rearrange("p h r -> p (h r)"),
                                       start=(i == 0), stop=(i == 1))
                mm.then_inc(s_sc, 1)

            def turn_x(n):
                if n == 0:
                    pe.wait_ge(s_yl, NT * ITS)
                    pe.wait_ge(s_xu, 2 * CT * (ITS - 1))
                if n == AB:
                    pe.wait_ge(s_xu, 2 * CT * ITS)
                if n >= 2:
                    pe.wait_ge(s_xTl, n - 1)
                b, r = n // AB, n % AB
                for t in range(CT):
                    mm = pe.transpose(bank[n % 2][:, t * P:(t + 1) * P], X[:, b, t, r:N:AB], ident[:])
                mm.then_inc(s_xT, 1)

            for it in range(ITS):
                for m in range(NT):
                    wp(NT * it + m)
                    side(16 * it + m)
                for j in range(2 * CT):
                    aggregate(2 * CT * it + j)
                    side(16 * it + NT + j)

            def attend(i):
                c, t = i // CT, i % CT
                b = c // NH
                if t == 0:
                    pe.wait_ge(s_back, 16 * 4 * (c + 1))
                    pe.wait_ge(s_xTl, AB * (b + 1))
                if i >= 2:
                    pe.wait_ge(s_fo, i - 1)
                else:
                    pe.wait_ge(s_xu, 2 * CT * ITS)
                beside = list(tail_groups(i))
                for r in range(AB):
                    if r % 2 and r // 2 < len(beside):
                        spread(beside[r // 2])
                    if r == 3 and i < AB:
                        turn_x(AB + i)
                    o = bank[4 + t % 2][:]
                    lhs = [xT[b][:, h, r, t * P:(t + 1) * P] for h in range(2)]
                    rhs = [att_T[c % 2][:, h, r] for h in range(2)]
                    pe.matmul(o, lhs[0], rhs[0], start=(r == 0), stop=False)
                    pe.matmul(o, lhs[0], rhs[1], start=False, stop=False)
                    mm = pe.matmul(o, lhs[1], rhs[0], start=False, stop=(r == AB - 1))
                mm.then_inc(s_f, 1)

            for i in range(CHUNKS * CT):
                attend(i)



_INS = ["x", "ctx_4096", "fside_BxSxS_0", "L1_xattn_W1", "L1_xattn_g1", "L1_xattn_b1", "L1_xattn_W2",
        "L1_xattn_g2", "L1_xattn_b2", "L1_xattn_W3", "L1_xattn_g3", "L1_xattn_b3"]


def kernel(**inputs):
    import concourse.bacc as bacc
    from concourse.bass_utils import run_bass_kernel_spmd

    nc = bacc.Bacc("TRN2", target_bir_lowering=False, num_devices=1)
    arrays, args = {}, []
    for name in _INS:
        a = np.ascontiguousarray(inputs[name])
        arrays[f"in_{name}"] = a
        args.append(nc.dram_tensor(f"in_{name}", a.shape, mybir.dt.from_np(a.dtype), kind="ExternalInput").ap())
    shape = arrays["in_x"].shape
    out = nc.dram_tensor("out_dram", shape, F32, kind="ExternalOutput").ap()
    build(nc, *args, out)
    r = run_bass_kernel_spmd(nc, [arrays], core_ids=[0])
    return r.results[0]["out_dram"]
```

```python
from contextlib import ExitStack

import numpy as np
import concourse.bass as bass
from concourse import mybir

F32 = mybir.dt.float32
F32R = mybir.dt.float32r
BF16 = mybir.dt.bfloat16
U32 = mybir.dt.uint32
ALU = mybir.AluOpType
ACT = mybir.ActivationFunctionType
AX_X = mybir.AxisListType.X

P = 128
HALF = 512
K0 = 8
K1 = 30
KP = 32
BLOCKS = 4
SLOPE0 = 0.01
SLOPE1 = 0.2
EPS_BN = 1e-5
TINY = 1e-20
REMOVED = -1.0e38
PI = float(np.pi)


def build(nc, x, ctx, fside, W1, g1, b1, W2, g2, b2, W3, g3, b3, out):
    B, C, N = x.shape
    D = ctx.shape[1]
    CT = C // P
    KT = D // P
    NT = N // P
    TILES = B * NT
    NH = N // HALF
    AB = N // P
    CH = 4
    CHUNKS = TILES // CH
    ITS = B * BLOCKS
    GN = 8
    NG = P // GN
    NS = 6
    U = TILES * K1

    with ExitStack() as st:
        def sb(name, shape, dt):
            return st.enter_context(nc.sbuf_tensor(name, shape, dt))

        def sem(name):
            return st.enter_context(nc.semaphore(name))

        pts_h = sb("pts_h", [P, KT, N], F32R)
        pts_l = sb("pts_l", [P, KT, N], F32R)
        nbr = sb("nbr", [P, B, NT, N], F32R)
        X = sb("X", [P, B, CT, N], F32)
        wT = sb("wT", [P, 2, CT, C], F32R)
        scratch = sb("scratch", [P, 11 * U + 2 * HALF], F32)
        ident = sb("ident", [P, P], F32)
        ident_b = sb("ident_b", [P, P], BF16)
        neg_half = sb("neg_half", [P, P], F32)
        mean_mat = sb("mean_mat", [P, P], F32)
        iota_r = sb("iota_r", [P, KP], F32)
        part = sb("part", [P, 1], F32)
        minus_one = sb("minus_one", [P, 1], F32)
        slot_t = sb("slot_t", [P, 1], F32)
        att_h12 = sb("att_h12", [P, P], F32R)
        vals = sb("vals", [P, 2, KP], F32)
        idx = sb("idx", [P, TILES, KP], U32)
        own = sb("own", [P, 3, TILES], F32)
        tab = sb("tab", [P, B, 3, AB], F32)
        tab_rest = sb("tab_rest", [P, B, 3, AB], F32)
        tab_p = sb("tab_p", [P, 3, B, 3, AB], BF16)
        a_row = sb("a_row", [P, P], BF16)
        prm = sb("prm", [P, 77], F32)
        w_eff = sb("w_eff", [P, 6, 3], F32)
        stat = sb("stat", [P, 64], F32)
        small = sb("small", [P, 64], F32)

        a_rows = nc.dram_tensor("a_rows", [CHUNKS, P, P], BF16, kind="Internal").ap()
        att_d = nc.dram_tensor("att_d", [CHUNKS, P, NG * HALF], F32, kind="Internal").ap()
        w1_keep = nc.dram_tensor("w1_keep", [P, 2 * CT * C], F32, kind="Internal").ap()

        bank = [st.enter_context(nc.psum_tensor(f"bank{i}", [P, HALF], F32)) for i in range(8)]

        x_flat = X[:].rearrange("p b c n -> p (b c n)")
        stage = x_flat[:, 0:NS * N].rearrange("p (s n) -> p s n", s=NS)
        sq_half = [x_flat[:, (NS + b) * N:(NS + b + 1) * N] for b in range(B)]
        SC = 4
        score = scratch[:, 0:SC * N].rearrange("p (s n) -> p s n", s=SC)
        adj = scratch[:, SC * N:(SC + 1) * N].bitcast(BF16).rearrange("p (s n) -> p s n", s=2)
        acc = [scratch[:, (SC + 1) * N:(SC + 2) * N], sq_half[1]]
        w_raw = [x_flat[:, 2 * N:4 * N].rearrange("p (t c) -> p t c", t=CT),
                 scratch[:, 2 * N:4 * N].rearrange("p (t c) -> p t c", t=CT)]
        p_h, p_l = pts_h[:, 0:CT, :], pts_h[:, CT:2 * CT, :]
        y_h = pts_l[:, 0:CT, :].rearrange("p c n -> p (c n)").rearrange("p (m o) -> p m o", m=NT)
        y_l = pts_l[:, CT:2 * CT, :].rearrange("p c n -> p (c n)").rearrange("p (m o) -> p m o", m=NT)
        NB = 3
        KH = K1 // 2
        near = scratch[:, 0:3 * U].rearrange("p (j t k) -> p j t k", j=3, t=TILES)
        oh_r = scratch[:, 1440:1500].bitcast(BF16).rearrange("p (k r) -> p k r", k=KH)
        r_all = scratch[:, 1500:1756].bitcast(BF16).rearrange("p (t k) -> p t k", t=TILES)
        i_u = scratch[:, 1756:1884].bitcast(U32)
        a_f = scratch[:, 1884:2012]
        pick = scratch[:, 2012:2372].rearrange("p (k j r) -> p k j r", k=KH, j=3)
        bc = scratch[:, 2372:5252].bitcast(BF16).rearrange("p (s f) -> p s f", s=NB)
        att32 = scratch[:, 2400:2912].rearrange("p (t k) -> p t k", t=TILES)
        a_all = scratch[:, 2912:3424]
        r4_all = scratch[:, 3424:3936]
        i_all = scratch[:, 3936:4448].bitcast(U32)
        l_tmp = scratch[:, 4864:4992]
        aT = scratch[:, 0:256].bitcast(BF16)
        rT = scratch[:, 256:512].bitcast(BF16)
        att_q = scratch[:, 512:1536].bitcast(BF16).rearrange("p (i h n) -> p i h n", i=2, h=2)
        oa = [scratch[:, 1536 + 512 * i:2048 + 512 * i].bitcast(BF16).rearrange("p (a n) -> p a n", n=GN)
              for i in range(2)]
        eq = [scratch[:, 2560 + 128 * i:2688 + 128 * i].bitcast(BF16).rearrange("p (r n) -> p r n", n=GN)
              for i in range(2)]
        mv = [scratch[:, 2816 + 512 * i:3328 + 512 * i].bitcast(BF16)
              .rearrange("p (i h r n) -> p i h r n", n=GN, i=2, h=2) for i in range(2)]
        iota_a8 = idx[:].rearrange("p t k -> p (t k)").bitcast(BF16).rearrange("p (a n) -> p a n", n=GN)
        iota_r8 = scratch[:, 4992:5120].bitcast(BF16).rearrange("p (r n) -> p r n", n=GN)
        spread_s = [scratch[:, 3840 + 512 * i:4352 + 512 * i] for i in range(2)]
        w_flat = wT[:].rearrange("p h t c -> p (h t c)")
        att_flat = [nbr[:, i].rearrange("p m n -> p (m n)") for i in range(2)]
        att_T = [a.rearrange("p (q h r x) -> p h r q x", q=NG, h=2, r=AB) for a in att_flat]
        xT = [t[:].rearrange("p k n -> p (k n)").rearrange("p (h r c) -> p h r c", h=2, r=AB)
              for t in (pts_h, pts_l)]

        def p32(n):
            if n < 6:
                return x_flat[:, (NS - 2) * N + n * HALF:(NS - 2) * N + (n + 1) * HALF]
            return scratch[:, 11 * U + (n % 2) * HALF:11 * U + (n % 2 + 1) * HALF]

        def slots(a, n=1):
            return scratch[:, a * U:(a + n) * U]

        s_w = sem("w_loaded")
        s_stage = [sem(f"stage_loaded{i}") for i in range(NS)]
        s_prm = sem("params_loaded")
        s_const = sem("consts_ready")
        s_wps = sem("w_transposed")
        s_wh = sem("w_high_ready")
        s_wl = sem("w_low_ready")
        s_wkeep = sem("w1_kept")
        s_wback = sem("w1_back")
        s_ph = sem("pts_high_ready")
        s_pl0 = sem("pts0_low_ready")
        s_pl1 = sem("pts1_low_ready")
        s_pl2 = sem("pts1_last_low_ready")
        s_sq = sem("squares_ready")
        s_sqmm = sem("squares_used")
        s_nsq = sem("sq_half_ready")
        s_kdone = sem("pts_tile_used")
        s_g = sem("gram_ready")
        s_gc = sem("gram_copied")
        s_v = sem("scores_ready")
        s_add = [sem(f"squares_added{i}") for i in range(2)]
        s_top = sem("topk_step")
        s_near = sem("nearest_removed")
        s_sel = sem("selection_done")
        s_adj = sem("adj_ready")
        s_diag = sem("adj_diagonal_ready")
        s_adjT = sem("adj_transposed")
        s_nbr = sem("nbr_ready")
        s_x = [sem(f"x{b}_loaded") for b in range(B)]
        s_p32 = sem("p_ready")
        s_p0 = sem("p_high_ready")
        s_p1 = sem("p_low_ready")
        s_wm = sem("wp_done")
        s_yh = sem("y_high_ready")
        s_yl = sem("y_low_ready")
        s_m = sem("agg_done")
        s_xu = sem("x_updated")
        s_link = sem("dve_link")
        s_af = sem("a_index_ready")
        s_aT = sem("a_index_transposed")
        s_ar = sem("a_row_ready")
        s_arow = sem("a_rows_stored")
        s_bc = [sem(f"a_broadcast{i}") for i in range(NB)]
        s_oh = sem("onehot_ready")
        s_look = sem("lookup_done")
        s_pick = sem("lookup_read")
        s_tab = sem("table_ready")
        s_mlp = sem("mlp_to_act")
        s_act = sem("act_to_mlp")
        s_bnin = sem("bn_partial_ready")
        s_bnps = sem("bn_summed")
        s_att = sem("att_ready")
        s_scT = sem("att_transposed")
        s_sct = sem("att_columns_copied")
        s_h12 = sem("att_high_rounded")
        s_attq = sem("att_parts_ready")
        s_st = [sem(f"spread_stored{i}") for i in range(2)]
        s_back = [sem(f"attention{c}_loaded") for c in range(CHUNKS)]
        s_oa = sem("a_onehot_ready")
        s_eq = sem("r_onehot_ready")
        s_mv = [sem(f"weighted_onehot{i}_ready") for i in range(2)]
        s_iota = sem("repeated_iotas_ready")
        s_sc = sem("spread_done")
        s_scc = sem("spread_copied")
        s_xT = sem("xT_done")
        s_xTh = sem("xT_high_ready")
        s_xTl = sem("xT_low_ready")
        s_f = sem("attended")
        s_fo = sem("result_ready")
        s_out = sem("out_stored")

        MLP = {e: n + 1 for n, e in enumerate(
            ("sqrt", "atan", "bn1s", "bn1a", "bn2s", "bn2a", "bn3s", "bn3a", "exp"))}
        DONE = {"sqrt": 1, "atan": 2, "bn1s": 3, "bn1a": 9, "bn2s": 10, "bn2a": 13, "bn3s": 14, "bn3a": 15,
                "exp": 16}
        G0 = 20
        R0 = 14
        SEL0 = 7
        M0 = G0 + 2 * TILES + 3
        NET = [0, 1, 2, 3, 4, (5, 0), (5, 1), (5, 2), 6, 7, 8, (9, 0), (9, 1), (9, 2), *range(10, 49)]
        T0 = M0 + len(NET) + 1
        S0 = T0 + 6
        S_END = 2 * (16 * ITS - S0)
        TAIL = 4

        QUARTER = NG // 4
        FREE_AT = [max(1, 2 * (16 * (ITS - 1) - S0 + 1)), S_END + 1, S_END + 4 * TAIL + 2, S_END + 8 * TAIL + 1]
        LOAD_AT = {}
        for c in range(CHUNKS):
            for j in range(4):
                q = max(NG * c + QUARTER * (j + 1) + 1, FREE_AT[c] + 2 * j)
                LOAD_AT.setdefault(min(q, CHUNKS * NG - 1), []).append((c, j))

        block = st.enter_context(nc.Block())

        def tail_groups(i):
            return range(min(S_END + TAIL * i, CHUNKS * NG), min(S_END + TAIL * (i + 1), CHUNKS * NG))

        def w_bank(n):
            return bank[(6, 7, 4, 5)[n % 4]][:]

        def weigh(engine, q, i):
            n0 = (q // NG) * P + (q % NG) * GN
            engine.tensor_tensor(mv[q % 2][:, i],
                                 eq[q % 2].unsqueeze(1).to_broadcast([P, 2, KP, GN]),
                                 att_q[:, i, :, n0:n0 + GN].unsqueeze(2).to_broadcast([P, 2, KP, GN]),
                                 ALU.mult).then_inc(s_mv[i], 1)

        @block.sync
        def _(sp):
            def load_stage(n):
                e = n - NS
                if e in (0, 1, KT):
                    sp.wait_ge(s_sq, e + 1)
                elif 0 <= e < KT:
                    sp.wait_ge(s_add[e % 2], e // 2)
                elif KT < e < 2 * KT:
                    sp.wait_ge(s_add[0], KT // 2 - 1 + e - KT)
                if 0 <= e < KT:
                    sp.wait_ge(s_pl0, e + 1)
                if e >= 2 * KT:
                    sp.wait_ge(s_pl1, e - 2 * KT + 1)
                b, k = (0 if n < KT else 1), n % KT
                sp.dma_start(stage[:, n % NS, :], ctx[b, k * P:(k + 1) * P, :]).then_inc(s_stage[n % NS], 16)

            for n in range(KT):
                load_stage(n)
            sp.dma_start(w_raw[1], fside[1].rearrange("(t p) c -> p t c", p=P)).then_inc(s_w, 16)
            for n in range(KT, KT + NS):
                load_stage(n)
            off = 0
            for w in (W1, g1, b1, W2, g2, b2, W3, g3, b3):
                n = int(np.prod(w.shape))
                flat = w.rearrange("a b -> (a b)") if len(w.shape) == 2 else w
                sp.dma_start(prm[:, off:off + n], flat.unsqueeze(0).to_broadcast([P, n])).then_inc(s_prm, 16)
                off += n
            for b in range(B):
                for j in range(3):
                    sp.dma_start(tab[:, b, j, :], ctx[b, 2 - j, :].rearrange("(a r) -> a r", r=AB)) \
                        .then_inc(s_prm, 16)
                    sp.dma_start(own[:, j, b * NT:(b + 1) * NT],
                                 ctx[b, 2 - j, :].rearrange("(t p) -> p t", p=P),
                                 allow_slow_non_contiguous=True).then_inc(s_prm, 16)
            sp.wait_ge(s_wh, CT)
            sp.wait_ge(s_wl, CT)
            sp.dma_start(w1_keep, w_flat.bitcast(F32)).then_inc(s_wkeep, 16)
            for n in range(KT + NS, 3 * NS + 2):
                load_stage(n)
            sp.wait_ge(s_add[0], KT // 2 - 1 + KT - 1)
            sp.dma_start(w_raw[0], fside[0].rearrange("(t p) c -> p t c", p=P)).then_inc(s_w, 16)
            sp.wait_ge(s_wps, 2 * CT)
            for n in range(3 * NS + 2, 3 * KT):
                load_stage(n)
            sp.wait_ge(s_pl1, KT - 2)
            sp.wait_ge(s_pl2, 2)
            sp.dma_start(X[:, 0], x[0].rearrange("(t p) n -> p t n", p=P)).then_inc(s_x[0], 16)
            sp.wait_ge(s_v, TILES - 1)
            sp.wait_ge(s_p1, 2 * CT)
            sp.dma_start(X[:, 1], x[1].rearrange("(t p) n -> p t n", p=P)).then_inc(s_x[1], 16)
            sp.wait_ge(s_adjT, TILES)
            sp.wait_ge(s_sel, TILES)
            for c in range(CHUNKS):
                sp.wait_ge(s_ar, c + 1)
                sp.dma_start(a_rows[c], a_row[:]).then_inc(s_arow, 16)
                sp.wait_ge(s_arow, 16 * (c + 1))
                for t in range(2 * CH):
                    u = 2 * CH * c + t
                    if u >= NB:
                        sp.wait_ge(s_look, u - NB + 1)
                    k = (t // 2) * KP + (t % 2) * KH
                    sp.dma_start(bc[:, u % NB, :],
                                 a_rows[c, k:k + KH, :].rearrange("k n -> (k n)").unsqueeze(0)
                                 .to_broadcast([P, KH * P])).then_inc(s_bc[u % NB], 16)

            def load_attention(c, j):
                for i in range(2):
                    sp.wait_ge(s_st[i], 16 * (NG * c + QUARTER * (j + 1)) // 2)
                if c < 2:
                    sp.wait_ge(s_m, 2 * CT * (ITS - 1 + c))
                else:
                    sp.wait_ge(s_f, CT * (c - 1))
                cols = slice(QUARTER * HALF * j, QUARTER * HALF * (j + 1))
                sp.dma_start(att_flat[c % 2][:, cols].bitcast(F32), att_d[c][:, cols]).then_inc(s_back[c], 16)

            for q in range(CHUNKS * NG):
                sp.wait_ge(s_scc, q + 1)
                sp.dma_start(att_d[q // NG, :, (q % NG) * HALF:(q % NG + 1) * HALF],
                             spread_s[q % 2]).then_inc(s_st[q % 2], 16)
                for c, j in LOAD_AT.get(q, []):
                    load_attention(c, j)
            for c in range(CHUNKS):
                b, hf = c // NH, c % NH
                for t in range(CT):
                    sp.wait_ge(s_fo, CT * c + t + 1)
                    sp.dma_start(out[b, t * P:(t + 1) * P, hf * HALF:(hf + 1) * HALF],
                                 X[:, b, t, hf * HALF:(hf + 1) * HALF]).then_inc(s_out, 16)
            sp.wait_ge(s_out, 16 * CHUNKS * CT)

        @block.gpsimd
        def _(pool):
            pool.memset(ident[:], 0.0).then_inc(s_const, 1)
            pool.memset(neg_half[:], -0.5).then_inc(s_const, 1)
            pool.memset(mean_mat[:], 1.0 / P).then_inc(s_const, 1)
            pool.memset(minus_one[:], -1.0).then_inc(s_const, 1)
            pool.wait_ge(s_const, 4)
            pool.affine_select(out=ident[:], in_=ident[:], compare_op=ALU.not_equal, fill=1.0, base=0,
                               pattern=[[-1, P]], channel_multiplier=1).then_inc(s_const, 1)
            pool.iota(iota_r[:], pattern=[[1, KP]], base=0, channel_multiplier=0,
                      allow_small_or_imprecise_dtypes=True).then_inc(s_const, 1)
            pool.iota(part[:], pattern=[[0, 1]], base=0, channel_multiplier=1,
                      allow_small_or_imprecise_dtypes=True).then_inc(s_const, 1)
            for t in range(CH):
                pool.wait_ge(s_const, 7 + t)
                pool.memset(slot_t[t * KP:(t + 1) * KP, :], float(t)).then_inc(s_const, 1)
            pool.wait_ge(s_const, 7 + CH)
            pool.tensor_copy(ident_b[:], ident[:]).then_inc(s_const, 1)

            def low_part(k):
                n = 2 * KT + k
                pool.wait_ge(s_stage[n % NS], 16 * (n // NS + 1))
                pool.wait_ge(s_ph, KT + k + 1)
                pool.tensor_tensor(pts_l[:, k, :], stage[:, n % NS, :], pts_h[:, k, :].bitcast(F32),
                                   ALU.subtract).then_inc(s_pl1, 1)

            def add_norm(T):
                pool.wait_ge(s_nsq, 2 * (T // NT + 1))
                pool.wait_ge(s_gc, 2 * (T + 1))
                pool.tensor_tensor(score[:, T % SC, :], score[:, T % SC, :], sq_half[T // NT],
                                   ALU.add).then_inc(s_v, 1)

            def add_square(n):
                pool.wait_ge(s_sq, n + 1)
                done = n // 2 - 1 if n < KT else KT // 2 - 2 + n - KT
                if done:
                    pool.wait_ge(s_add[0], done)
                pool.tensor_tensor(acc[0], acc[0], stage[:, n % NS, :], ALU.add).then_inc(s_add[0], 1)

            def diagonal(T):
                pool.wait_ge(s_adj, T + 1)
                diag = adj[:, T % 2, (T % NT) * P:(T % NT + 1) * P]
                pool.tensor_tensor(diag, diag, ident_b[:], ALU.add).then_inc(s_diag, 1)

            for n in (2, 4, 6):
                add_square(n)
            diagonal(0)
            add_norm(1)
            for k in range(1, 3):
                add_square(KT + k)
            diagonal(1)
            add_norm(2)
            for k in range(3, 6):
                add_square(KT + k)
            add_norm(3)
            for k in range(2, 4):
                diagonal(k)
            for k in range(6, 8):
                add_square(KT + k)
            add_norm(4)
            add_norm(5)
            for k in range(4, 6):
                diagonal(k)
            add_norm(6)
            for k in range(0, 4):
                low_part(k)
            add_norm(7)
            for k in range(4, KT - 2):
                low_part(k)
            for k in range(6, 8):
                diagonal(k)
            add_norm(8)
            add_norm(9)
            for k in range(8, 10):
                diagonal(k)
            add_norm(10)
            add_norm(11)
            add_norm(12)
            for k in range(10, 12):
                diagonal(k)
            add_norm(13)
            add_norm(14)
            for k in range(12, 14):
                diagonal(k)
            add_norm(15)

            def p_low(n):
                hf, t = (n % (2 * CT)) // CT, n % CT
                pool.wait_ge(s_p0, n + 1)
                pool.tensor_tensor(p_l[:, t, hf * HALF:(hf + 1) * HALF], p32(n),
                                   p_h[:, t, hf * HALF:(hf + 1) * HALF].bitcast(F32),
                                   ALU.subtract).then_inc(s_p1, 1)

            def weight(q):
                c = q // NG
                pool.wait_ge(s_eq, q + 1)
                if q % NG == 0:
                    pool.wait_ge(s_attq, c + 1)
                if q >= 2:
                    pool.wait_ge(s_sc, q - 1)
                weigh(pool, q, 1)

            for it in range(ITS):
                for s_ in range(16):
                    g = 16 * it + s_
                    if g == SEL0 + 3:
                        diagonal(TILES - 2)
                        diagonal(TILES - 1)
                    if g == T0:
                        pool.wait_ge(s_att, 1)
                        pool.iota(iota_a8, pattern=[[1, P], [0, GN]], base=0, channel_multiplier=0,
                                  allow_small_or_imprecise_dtypes=True).then_inc(s_iota, 1)
                        pool.iota(iota_r8, pattern=[[1, KP], [0, GN]], base=0, channel_multiplier=0,
                                  allow_small_or_imprecise_dtypes=True).then_inc(s_iota, 1)
                    if g >= S0:
                        weight(2 * (g - S0))
                    if s_ >= NT and it + 1 < ITS:
                        p_low(2 * CT * (it + 1) + s_ - NT)
                    if g >= S0:
                        weight(2 * (g - S0) + 1)
            for q in range(S_END, CHUNKS * NG):
                weight(q)

        @block.scalar
        def _(act):
            def w_high(n):
                t = n % CT
                act.wait_ge(s_wps, n + 1)
                if n == CT:
                    act.wait_ge(s_wkeep, 16)
                act.copy(wT[:, 0, t, :], w_bank(n)).then_inc(s_wh, 1)

            def high_part(m):
                k, n = m % KT, m if m < KT else m + KT
                act.wait_ge(s_stage[n % NS], 16 * (n // NS + 1))
                if m >= KT:
                    act.wait_ge(s_kdone, k + 1)
                act.copy(pts_h[:, k, :], stage[:, n % NS, :]).then_inc(s_ph, 1)

            def square(n):
                if n in (0, 1, KT):
                    dst = acc[n % KT]
                else:
                    dst = stage[:, n % NS, :]
                if 1 < n < KT:
                    act.wait_ge(s_pl0, n + 1)
                elif n >= KT:
                    act.wait_ge(s_stage[n % NS], 16 * (n // NS + 1))
                act.activation(dst, stage[:, n % NS, :], ACT.Square).then_inc(s_sq, 1)

            def norm_out(b):
                for hf in range(NH):
                    act.wait_ge(s_sqmm, NH * b + hf + 1)
                    act.copy(sq_half[b][:, hf * HALF:(hf + 1) * HALF], bank[4 + hf][:]).then_inc(s_nsq, 1)

            def gram_out(T):
                if T == NT - 1:
                    act.wait_ge(s_kdone, KT)
                else:
                    act.wait_ge(s_g, T + 1 if T < NT else T)
                if T == 2:
                    act.wait_ge(s_wps, CT)
                if T >= SC:
                    act.wait_ge(s_sel, T - SC + 1)
                for hf in range(NH):
                    act.copy(score[:, T % SC, hf * HALF:(hf + 1) * HALF], bank[2 * (T % 2) + hf][:]) \
                        .then_inc(s_gc, 1)

            def nbr_out(T):
                act.wait_ge(s_adjT, T + 1)
                act.copy(nbr[:, T // NT, :, (T % NT) * P:(T % NT + 1) * P],
                         bank[6 + T % 2][:].bitcast(BF16).rearrange("p (m n) -> p m n", m=NT)) \
                    .then_inc(s_nbr, 1)

            def adjacency(T):
                act.wait_ge(s_near, T + 1)
                if T >= 2:
                    act.wait_ge(s_adjT, T - 1)
                act.activation(adj[:, T % 2, :], score[:, T % SC, :], ACT.Relu, bias=minus_one[:, 0:1],
                               scale=2.0 / REMOVED).then_inc(s_adj, 1)

            high_part(0)
            for n in range(1, KT):
                high_part(n)
                square(n - 1)
            square(KT - 1)
            gram_out(0)
            norm_out(0)
            adjacency(0)
            gram_out(1)
            for n in range(CT):
                w_high(n)
            for n in range(KT, KT + 3):
                square(n)
            adjacency(1)
            gram_out(2)
            nbr_out(0)
            for n in range(KT + 3, KT + NS):
                square(n)
            gram_out(3)
            nbr_out(1)
            adjacency(2)
            adjacency(3)
            for n in range(KT + NS, 2 * KT):
                square(n)
            gram_out(4)
            gram_out(5)
            nbr_out(2)
            nbr_out(3)
            norm_out(1)
            adjacency(4)
            adjacency(5)
            gram_out(6)
            for n in range(CT, 2 * CT):
                w_high(n)
            for k in range(KT):
                high_part(KT + k)
            gram_out(7)
            nbr_out(4)
            nbr_out(5)
            adjacency(6)
            adjacency(7)
            gram_out(8)
            nbr_out(6)
            nbr_out(7)
            gram_out(9)
            adjacency(8)
            adjacency(9)
            gram_out(10)
            nbr_out(8)
            nbr_out(9)
            gram_out(11)
            gram_out(12)
            adjacency(10)
            adjacency(11)
            gram_out(13)
            nbr_out(10)
            nbr_out(11)
            gram_out(14)
            adjacency(12)
            adjacency(13)
            def p_high(n):
                hf, t = (n % (2 * CT)) // CT, n % CT
                act.wait_ge(s_p32, n + 1)
                act.copy(p_h[:, t, hf * HALF:(hf + 1) * HALF], p32(n)).then_inc(s_p0, 1)

            def y_high(g):
                it, m = g // NT, g % NT
                act.wait_ge(s_wm, g + 1)
                if m == 0 and it:
                    act.wait_ge(s_m, 2 * CT * it)
                act.copy(y_h[:, m, :], bank[g % 3][:]).then_inc(s_yh, 1)

            def a_row_out(c):
                act.wait_ge(s_aT, c + 1)
                if c:
                    act.wait_ge(s_arow, 16 * c)
                act.copy(a_row[:], bank[6][:, 384:HALF]).then_inc(s_ar, 1)

            def bn_sqrt(ev, n):
                act.wait_ge(s_mlp, MLP[ev])
                act.activation(stat[:, 40:40 + n], stat[:, 34:34 + n], ACT.Sqrt).then_inc(s_act, 1)

            def bn_apply(ev, first, n):
                act.wait_ge(s_mlp, MLP[ev])
                for c in range(n):
                    act.activation(slots(first + c), slots(first + c), ACT.Identity, bias=stat[:, 58 + c:59 + c],
                                   scale=stat[:, 52 + c:53 + c]).then_inc(s_act, 1)

            def side(g):
                if g == SEL0 + 3:
                    adjacency(TILES - 2)
                    adjacency(TILES - 1)
                if g == SEL0 + 5:
                    nbr_out(TILES - 2)
                    nbr_out(TILES - 1)
                if (g - R0) % 8 == 2 and 0 <= (g - R0) // 8 < CHUNKS:
                    a_row_out((g - R0) // 8)
                if g == 16 + NT:
                    act.wait_ge(s_wm, 2 * NT)
                    act.dma_start(w_flat.bitcast(F32), w1_keep).then_inc(s_wback, 16)
                m = NET[g - M0] if M0 <= g < M0 + len(NET) else None
                if m == 4:
                    act.wait_ge(s_mlp, MLP["sqrt"])
                    act.activation(slots(6, 2), slots(4, 2), ACT.Sqrt).then_inc(s_act, 1)
                if m == 10:
                    act.wait_ge(s_mlp, MLP["atan"])
                    act.activation(slots(6, 2), slots(8, 2), ACT.Arctan).then_inc(s_act, 1)
                if m == 25:
                    bn_sqrt("bn1s", 6)
                if m == 26:
                    bn_apply("bn1a", 0, 6)
                if m == 38:
                    bn_sqrt("bn2s", 3)
                if m == 39:
                    bn_apply("bn2a", 6, 3)
                if m == 45:
                    bn_sqrt("bn3s", 1)
                if m == 46:
                    bn_apply("bn3a", 0, 1)
                if m == 47:
                    act.wait_ge(s_mlp, MLP["exp"])
                    act.activation(slots(1), slots(0), ACT.Exp).then_inc(s_act, 1)
                if g == T0 + 1:
                    columns()
                if T0 + 2 <= g < T0 + 2 + CHUNKS:
                    round_high(g - T0 - 2)
                if g > S0:
                    spread_out(2 * (g - S0) - 1)
                if g >= 16 * ITS - AB:
                    xT_high(g - 16 * ITS + AB)

            def columns():
                act.wait_ge(s_scT, 1)
                act.copy(aT, bank[6][:]).then_inc(s_sct, 1)
                act.wait_ge(s_scT, 2)
                act.activation(rT, bank[7][:], ACT.Identity, bias=slot_t[:, 0:1]).then_inc(s_sct, 1)

            def round_high(c):
                act.wait_ge(s_scT, 3)
                if c:
                    act.wait_ge(s_attq, c)
                act.copy(att_h12[:], bank[6][:, c * P:(c + 1) * P]).then_inc(s_h12, 1)

            def spread_out(q):
                act.wait_ge(s_sc, q + 1)
                if q >= 2:
                    act.wait_ge(s_st[q % 2], 16 * (q // 2))
                act.copy(spread_s[q % 2].rearrange("p (x n) -> p n x", n=GN),
                         bank[6 + q % 2][:].rearrange("p (n x) -> p n x", n=GN)).then_inc(s_scc, 1)

            def xT_high(n):
                act.wait_ge(s_xT, n + 1)
                act.copy(xT[n // AB][:, 0, n % AB, :], bank[n % 2][:]).then_inc(s_xTh, 1)

            act.wait_ge(s_g, TILES - 1)
            for j in range(CT):
                p_high(j)
            gram_out(15)
            for j in range(CT, 2 * CT):
                p_high(j)
            nbr_out(12)
            nbr_out(13)
            for it in range(ITS):
                for m in range(NT):
                    if 16 * it + m > S0:
                        spread_out(2 * (16 * it + m - S0) - 2)
                    y_high(NT * it + m)
                    side(16 * it + m)
                for j in range(2 * CT):
                    if 16 * it + NT + j > S0:
                        spread_out(2 * (16 * it + NT + j - S0) - 2)
                    if it + 1 < ITS:
                        p_high(2 * CT * (it + 1) + j)
                    side(16 * it + NT + j)

            spread_out(S_END - 2)
            spread_out(S_END - 1)
            for i in range(CHUNKS * CT):
                if i < AB and len(tail_groups(i)) <= 2:
                    xT_high(AB + i)
                for n, q in enumerate(tail_groups(i)):
                    if n == 2 and i < AB:
                        xT_high(AB + i)
                    spread_out(q)

        @block.vector
        def _(dve):
            chain = [0]

            def link(ins):
                chain[0] += 1
                ins.then_inc(s_link, 1)
                dve.wait_ge(s_link, chain[0])

            def w_low(n):
                t = n % CT
                dve.wait_ge(s_wh, n + 1)
                dve.tensor_tensor(wT[:, 1, t, :], w_bank(n), wT[:, 0, t, :].bitcast(F32),
                                  ALU.subtract).then_inc(s_wl, 1)

            def pts_low(k):
                dve.wait_ge(s_ph, k + 1)
                dve.tensor_tensor(pts_l[:, k, :], stage[:, k % NS, :], pts_h[:, k, :].bitcast(F32),
                                  ALU.subtract).then_inc(s_pl0, 1)

            top_step = [0]
            after = {}

            def select_step(T, n):
                r, kind = n // 3, n % 3
                v, top = score[:, T % SC, :], vals[:, T % 2, 8 * r:8 * r + 8]
                if n == 0:
                    if T:
                        dve.wait_ge(s_v, T)
                elif n == 3:
                    dve.wait_ge(s_near, T + 1)
                else:
                    dve.wait_ge(s_top, after[T])
                if n == 5:
                    dve.wait_ge(s_adj, T + 1)
                if kind == 0:
                    ins = dve.max(top, v)
                elif kind == 1:
                    ins = dve.max_index(idx[:, T, 8 * r:8 * r + 8], top, v)
                else:
                    ins = dve.match_replace(v, top, v, REMOVED)
                if n == 2:
                    ins.then_inc(s_near, 1)
                elif n == STEPS - 1:
                    ins.then_inc(s_sel, 1)
                else:
                    top_step[0] += 1
                    after[T] = top_step[0]
                    ins.then_inc(s_top, 1)

            STEPS = 3 * (KP // 8) - 1

            def select(tiles):
                for n in range(STEPS):
                    for T in tiles:
                        select_step(T, n)

            dve.wait_ge(s_const, 8 + CH)
            for k in range(KT):
                pts_low(k)
                if k >= 3 and k % 2:
                    dve.wait_ge(s_sq, k + 1)
                    if k > 3:
                        dve.wait_ge(s_add[1], k // 2 - 1)
                    dve.tensor_tensor(acc[1], acc[1], stage[:, k % NS, :], ALU.add).then_inc(s_add[1], 1)
            for hf in range(NH):
                cols = slice(hf * HALF, (hf + 1) * HALF)
                dve.wait_ge(s_gc, 2)
                dve.wait_ge(s_nsq, hf + 1)
                link(dve.tensor_tensor(score[:, 0, cols], score[:, 0, cols], sq_half[0][:, cols], ALU.add))
            select([0])
            for n in range(CT):
                w_low(n)
            select([1])
            select([2, 3])
            for n in range(STEPS):
                if n == 8:
                    for i in range(CT, 2 * CT):
                        w_low(i)
                for T in (4, 5):
                    select_step(T, n)
            dve.wait_ge(s_prm, 16 * (9 + 6 * B))
            link(dve.tensor_copy(tab_p[:, 0], tab[:]))
            link(dve.tensor_tensor(tab_rest[:], tab[:], tab_p[:, 0], ALU.subtract))
            link(dve.tensor_copy(tab_p[:, 1], tab_rest[:]))
            link(dve.tensor_tensor(tab_rest[:], tab_rest[:], tab_p[:, 1], ALU.subtract))
            dve.tensor_copy(tab_p[:, 2], tab_rest[:]).then_inc(s_tab, 1)
            for k in (KT - 2, KT - 1):
                n = 2 * KT + k
                dve.wait_ge(s_stage[n % NS], 16 * (n // NS + 1))
                dve.wait_ge(s_ph, KT + k + 1)
                dve.tensor_tensor(pts_l[:, k, :], stage[:, n % NS, :], pts_h[:, k, :].bitcast(F32),
                                  ALU.subtract).then_inc(s_pl2, 1)
            for T in range(6, TILES - CH, 2):
                select([T, T + 1])
            for n in range(4):
                for T in (TILES - 4, TILES - 3):
                    select_step(T, n)

            def p_make(n):
                it = n // (2 * CT)
                b, hf, t = it % B, (n % (2 * CT)) // CT, n % CT
                if it < B:
                    dve.wait_ge(s_x[b], 16)
                else:
                    dve.wait_ge(s_xu, 2 * CT * (it - 1))
                if it and n % (2 * CT) == 0:
                    dve.wait_ge(s_wm, NT * it)
                if n >= 2 * CT:
                    dve.wait_ge(s_p1, n - 1)
                src = X[:, b, t, hf * HALF:(hf + 1) * HALF]
                dve.scalar_tensor_tensor(p32(n), src, SLOPE0, src, ALU.mult, ALU.max).then_inc(s_p32, 1)

            def y_low(g):
                m = g % NT
                dve.wait_ge(s_yh, g + 1)
                dve.tensor_tensor(y_l[:, m, :], bank[g % 3][:], y_h[:, m, :].bitcast(F32),
                                  ALU.subtract).then_inc(s_yl, 1)

            def x_update(g):
                it, j = g // (2 * CT), g % (2 * CT)
                b, hf, t = it % B, j // CT, j % CT
                dst = X[:, b, t, hf * HALF:(hf + 1) * HALF]
                dve.wait_ge(s_m, g + 1)
                dve.scalar_tensor_tensor(dst, bank[3 + g % 3][:], 1.0 / (K0 + 1.0), dst,
                                         ALU.mult, ALU.add).then_inc(s_xu, 1)

            def index_rows(c):
                src = idx[:, CH * c:CH * (c + 1), :].rearrange("p t k -> p (t k)")
                if c:
                    dve.wait_ge(s_aT, c)
                link(dve.tensor_scalar(i_u, src, 3, None, ALU.logical_shift_right))
                link(dve.tensor_copy(a_f, i_u))
                link(dve.tensor_scalar(i_u, src, AB - 1, None, ALU.bitwise_and))
                dve.tensor_copy(r_all[:, CH * c:CH * (c + 1), :].rearrange("p t k -> p (t k)"), i_u) \
                    .then_inc(s_af, 1)

            def onehot_a(u):
                dve.wait_ge(s_bc[u % NB], 16 * (u // NB + 1))
                dve.tensor_scalar(bc[:, u % NB, :], bc[:, u % NB, :], part[:, 0:1], None, ALU.is_equal) \
                    .then_inc(s_oh, 1)

            def pick_r(u):
                T, k0 = u // 2, (u % 2) * KH
                dve.wait_ge(s_af, T // CH + 1)
                link(dve.tensor_tensor(oh_r, r_all[:, T, k0:k0 + KH].unsqueeze(2).to_broadcast([P, KH, AB]),
                                       iota_r[:, 0:AB].unsqueeze(1).to_broadcast([P, KH, AB]), ALU.is_equal))
                dve.wait_ge(s_look, u + 1)
                dve.tensor_tensor(pick, bank[6 + u % 2][:, 0:3 * KH * AB]
                                  .rearrange("p (k j r) -> p k j r", k=KH, j=3),
                                  oh_r.unsqueeze(2).to_broadcast([P, KH, 3, AB]), ALU.mult).then_inc(s_pick, 1)
                dve.wait_ge(s_pick, u + 1)
                link(dve.tensor_reduce(near[:, :, T, k0:k0 + KH], pick.rearrange("p k j r -> p j k r"),
                                       AX_X, ALU.add))

            def tt(o, a, b_, op):
                link(dve.tensor_tensor(o, a, b_, op))

            def ts(o, a, s1, op0, s2=None, op1=None):
                if op1 is None:
                    link(dve.tensor_scalar(o, a, s1, None, op0))
                else:
                    link(dve.tensor_scalar(o, a, s1, s2, op0, op1))

            def stt(o, a, s_, b_, op0, op1):
                link(dve.scalar_tensor_tensor(o, a, s_, b_, op0, op1))

            def mix(first, src, ws, fresh=True):
                for j, a in enumerate(src):
                    for c, w in enumerate(ws(j)):
                        if j == 0 and fresh:
                            ts(slots(first + c), slots(a), w, ALU.mult)
                        else:
                            stt(slots(first + c), slots(a), w, slots(first + c), ALU.mult, ALU.add)

            def bn_partial(first, n, some, last):
                for c in some:
                    link(dve.bn_stats(small[:, 6 * c:6 * c + 6], slots(first + c)))
                for c in some:
                    link(dve.bn_aggr(small[:, 40 + 2 * c:42 + 2 * c], small[:, 6 * c:6 * c + 6]))
                if not last:
                    return
                pair = small[:, 40:40 + 2 * n].rearrange("p (c s) -> p s c", s=2)
                ts(stat[:, 0:n], pair[:, 0], 1.0, ALU.mult)
                tt(stat[:, n:2 * n], pair[:, 0], pair[:, 0], ALU.mult)
                dve.tensor_tensor(stat[:, n:2 * n], stat[:, n:2 * n], pair[:, 1], ALU.add).then_inc(s_bnin, 1)

            def bn_variance(layer, n):
                dve.wait_ge(s_bnps, layer)
                ts(stat[:, 16:16 + 2 * n], bank[7][:, 480:480 + 2 * n], 1.0, ALU.mult)
                tt(stat[:, 28:28 + n], stat[:, 16:16 + n], stat[:, 16:16 + n], ALU.mult)
                tt(stat[:, 34:34 + n], stat[:, 16 + n:16 + 2 * n], stat[:, 28:28 + n], ALU.subtract)
                dve.tensor_scalar(stat[:, 34:34 + n], stat[:, 34:34 + n], EPS_BN, None,
                                  ALU.add).then_inc(s_mlp, 1)

            def bn_coefficients(n, gain, bias, ev):
                y, t, v = stat[:, 46:46 + n], stat[:, 28:28 + n], stat[:, 34:34 + n]
                dve.wait_ge(s_act, DONE[ev])
                link(dve.reciprocal(y, stat[:, 40:40 + n]))
                tt(t, y, y, ALU.mult)
                tt(t, t, v, ALU.mult)
                ts(t, t, -0.5, ALU.mult, 1.5, ALU.add)
                tt(y, y, t, ALU.mult)
                tt(stat[:, 52:52 + n], y, prm[:, gain:gain + n], ALU.mult)
                tt(t, stat[:, 16:16 + n], stat[:, 52:52 + n], ALU.mult)
                dve.tensor_tensor(stat[:, 58:58 + n], prm[:, bias:bias + n], t,
                                  ALU.subtract).then_inc(s_mlp, 1)

            def leaky(first, n, ev):
                dve.wait_ge(s_act, DONE[ev])
                h = slots(first, n)
                stt(h, h, SLOPE1, h, ALU.mult, ALU.max)

            own_k = own[:].unsqueeze(3).to_broadcast([P, 3, TILES, K1])

            def grid(a):
                return slots(a).rearrange("p (t k) -> p t k", t=TILES)

            def network(n):
                Y, Xa, S, R = slots(0, 2), slots(2, 2), slots(4), slots(5)
                A, T_ = slots(6, 2), slots(8, 2)
                if n == 0:
                    tt(grid(0), grid(0), own_k[:, 0], ALU.subtract)
                    tt(grid(1), grid(1), own_k[:, 1], ALU.subtract)
                    tt(grid(3), grid(2), own_k[:, 2], ALU.subtract)
                if n == 1:
                    tt(S, slots(3), slots(3), ALU.mult)
                    tt(R, slots(1), slots(1), ALU.mult)
                    tt(S, S, R, ALU.add)
                if n == 2:
                    tt(R, slots(0), slots(0), ALU.mult)
                    tt(R, S, R, ALU.add)
                    stt(slots(0), R, TINY, slots(0), ALU.is_ge, ALU.mult)
                if n == 3:
                    stt(slots(1), S, TINY, slots(1), ALU.is_ge, ALU.mult)
                    stt(slots(3), S, TINY, slots(3), ALU.is_ge, ALU.mult)
                if n == 4:
                    stt(slots(3), S, TINY, slots(3), ALU.is_lt, ALU.add)
                    dve.tensor_scalar(slots(4, 2), slots(4, 2), TINY, None, ALU.max).then_inc(s_mlp, 1)
                if n in ((5, 0), (5, 1), (5, 2)):
                    dve.wait_ge(s_act, DONE["sqrt"])
                    cut = slice(n[1] * 2 * U // 3, (n[1] + 1) * 2 * U // 3)
                    link(dve.reciprocal(T_[:, cut], A[:, cut]))
                if n == 6:
                    tt(T_, T_, slots(4, 2), ALU.mult)
                    tt(T_, T_, A, ALU.add)
                    ts(slots(2), slots(8), 0.5, ALU.mult)
                    ts(slots(10), slots(9), 0.5, ALU.mult)
                if n == 7:
                    stt(slots(4, 2), Y, -1.0, Y, ALU.mult, ALU.max)
                    stt(A, Xa, -1.0, Xa, ALU.mult, ALU.max)
                if n == 8:
                    tt(T_, slots(4, 2), A, ALU.min)
                    tt(A, slots(4, 2), A, ALU.max)
                if n == (9, 0):
                    tt(slots(4, 2), slots(4, 2), A, ALU.is_ge)
                if n in ((9, 0), (9, 1), (9, 2)):
                    cut = slice(n[1] * 2 * U // 3, (n[1] + 1) * 2 * U // 3)
                    link(dve.reciprocal(A[:, cut], A[:, cut]))
                if n == 10:
                    dve.tensor_tensor(T_, T_, A, ALU.mult).then_inc(s_mlp, 1)
                    w = prm[:, 0:36].rearrange("p (c j) -> p c j", c=6)
                    link(dve.tensor_reduce(small[:, 0:6], w[:, :, 3:6], AX_X, ALU.add))
                    ts(small[:, 0:6], small[:, 0:6], -1.0 / 3.0, ALU.mult)
                    tt(w_eff[:], w[:, :, 0:3], w[:, :, 3:6], ALU.add)
                    tt(w_eff[:], w_eff[:], small[:, 0:6].unsqueeze(2).to_broadcast([P, 6, 3]), ALU.add)
                if n == 11:
                    dve.wait_ge(s_act, DONE["atan"])
                    ts(T_, A, -2.0, ALU.mult, PI / 2, ALU.add)
                    tt(T_, T_, slots(4, 2), ALU.mult)
                if n == 12:
                    tt(A, A, T_, ALU.add)
                    ts(T_, A, -2.0, ALU.mult, PI, ALU.add)
                if n == 13:
                    stt(T_, Xa, 0.0, T_, ALU.is_lt, ALU.mult)
                    tt(A, A, T_, ALU.add)
                if n == 14:
                    ts(T_, Y, 0.0, ALU.is_ge, 2.0, ALU.mult)
                    stt(A, T_, -1.0, A, ALU.add, ALU.mult)
                if n in range(15, 21):
                    c = n - 15
                    mix(c, (10, 6, 7), lambda j: [w_eff[:, c, j:j + 1]])
                if n == 21:
                    bn_partial(0, 6, range(3), False)
                if n == 22:
                    bn_partial(0, 6, range(3, 6), True)
                if n == 25:
                    bn_variance(1, 6)
                if n == 26:
                    bn_coefficients(6, 36, 42, "bn1s")
                if n == 27:
                    leaky(0, 3, "bn1a")
                if n == 28:
                    leaky(3, 3, "bn1a")
                if n in range(29, 35):
                    c, hf = (n - 29) // 2, (n - 29) % 2
                    mix(6 + c, range(3 * hf, 3 * hf + 3),
                        lambda j: [prm[:, 48 + 6 * c + 3 * hf + j:49 + 6 * c + 3 * hf + j]], hf == 0)
                if n == 35:
                    bn_partial(6, 3, range(3), True)
                if n == 38:
                    bn_variance(2, 3)
                if n == 39:
                    bn_coefficients(3, 66, 69, "bn2s")
                if n == 40:
                    leaky(6, 3, "bn2a")
                if n == 41:
                    mix(0, (6, 7, 8), lambda j: [prm[:, 72 + j:73 + j]])
                if n == 42:
                    bn_partial(0, 1, range(1), True)
                if n == 45:
                    bn_variance(3, 1)
                if n == 46:
                    bn_coefficients(1, 75, 76, "bn3s")
                if n == 47:
                    leaky(0, 1, "bn3a")
                    link(dve.tensor_reduce(small[:, 0:TILES], grid(0), AX_X, ALU.max))
                    dve.tensor_tensor(grid(0), grid(0), small[:, 0:TILES].unsqueeze(2)
                                      .to_broadcast([P, TILES, K1]), ALU.subtract).then_inc(s_mlp, 1)
                if n == 48:
                    dve.wait_ge(s_act, DONE["exp"])
                    link(dve.tensor_reduce(small[:, 16:16 + TILES], grid(1), AX_X, ALU.add))
                    link(dve.reciprocal(small[:, 32:32 + TILES], small[:, 16:16 + TILES]))
                    link(dve.memset(att32[:, :, K1:KP], 0.0))
                    tt(att32[:, :, 0:K1], grid(1), small[:, 32:32 + TILES].unsqueeze(2)
                       .to_broadcast([P, TILES, K1]), ALU.mult)

            def index_columns():
                src = idx[:].rearrange("p t k -> p (t k)")
                link(dve.tensor_scalar(i_all, src, 3, None, ALU.logical_shift_right))
                link(dve.tensor_copy(a_all, i_all))
                link(dve.tensor_scalar(i_all, src, AB - 1, None, ALU.bitwise_and))
                dve.tensor_scalar(r4_all, i_all, float(CH), None, ALU.mult).then_inc(s_att, 1)

            def att_parts(c):
                cols = slice(c * P, (c + 1) * P)
                dve.wait_ge(s_h12, c + 1)
                h = att_h12[:].bitcast(F32)
                link(dve.tensor_copy(att_q[:, 0, 0, cols], h))
                link(dve.tensor_tensor(att_q[:, 1, 0, cols], h, att_q[:, 0, 0, cols], ALU.subtract))
                link(dve.tensor_tensor(l_tmp, bank[6][:, cols], h, ALU.subtract))
                link(dve.tensor_copy(att_q[:, 0, 1, cols], l_tmp))
                dve.tensor_tensor(att_q[:, 1, 1, cols], l_tmp, att_q[:, 0, 1, cols],
                                  ALU.subtract).then_inc(s_attq, 1)

            def onehots(q):
                n0 = (q // NG) * P + (q % NG) * GN
                if q == 0:
                    dve.wait_ge(s_sct, 2)
                    dve.wait_ge(s_iota, 2)
                    dve.wait_ge(s_attq, CHUNKS)
                if q >= 2:
                    dve.wait_ge(s_sc, q - 1)
                    dve.wait_ge(s_mv[1], q - 1)
                dve.tensor_tensor(eq[q % 2], rT[:, n0:n0 + GN].unsqueeze(1).to_broadcast([P, KP, GN]),
                                  iota_r8, ALU.is_equal).then_inc(s_eq, 1)
                dve.tensor_tensor(oa[q % 2], aT[:, n0:n0 + GN].unsqueeze(1).to_broadcast([P, P, GN]),
                                  iota_a8, ALU.is_equal).then_inc(s_oa, 1)
                dve.wait_ge(s_eq, q + 1)
                weigh(dve, q, 0)

            def xT_low(n):
                dve.wait_ge(s_xTh, n + 1)
                dve.tensor_tensor(xT[n // AB][:, 1, n % AB, :], bank[n % 2][:],
                                  xT[n // AB][:, 0, n % AB, :].bitcast(F32), ALU.subtract).then_inc(s_xTl, 1)

            def side(g):
                if g < SEL0:
                    for T in (TILES - 4, TILES - 3):
                        select_step(T, g + STEPS - SEL0)
                elif g < SEL0 + STEPS:
                    for T in (TILES - 2, TILES - 1):
                        select_step(T, g - SEL0)
                if (g - R0) % 8 == 0 and 0 <= (g - R0) // 8 < CHUNKS:
                    index_rows((g - R0) // 8)
                if G0 <= g < G0 + 2 * TILES:
                    onehot_a(g - G0)
                if G0 + 2 <= g < G0 + 2 + 2 * TILES:
                    pick_r(g - G0 - 2)
                if M0 <= g < M0 + len(NET):
                    network(NET[g - M0])
                if g == M0 + len(NET):
                    index_columns()
                if T0 + 3 <= g < T0 + 3 + CHUNKS:
                    att_parts(g - T0 - 3)
                if g >= S0:
                    onehots(2 * (g - S0))
                if g > 16 * ITS - AB:
                    xT_low(g - 16 * ITS + AB - 1)

            for hf in range(NH):
                cols = slice(hf * HALF, (hf + 1) * HALF)
                for t in range(CT):
                    p_make(CT * hf + t)
                for t in range(CT):
                    dve.wait_ge(s_p0, CT * hf + t + 1)
                    dve.tensor_tensor(p_l[:, t, cols], p32(CT * hf + t), p_h[:, t, cols].bitcast(F32),
                                      ALU.subtract).then_inc(s_p1, 1)
            for it in range(ITS):
                for m in range(NT):
                    side(16 * it + m)
                    y_low(NT * it + m)
                    if 16 * it + m >= S0:
                        onehots(2 * (16 * it + m - S0) + 1)
                for j in range(2 * CT):
                    side(16 * it + NT + j)
                    x_update(2 * CT * it + j)
                    if it + 1 < ITS:
                        p_make(2 * CT * (it + 1) + j)
                    if 16 * it + NT + j >= S0:
                        onehots(2 * (16 * it + NT + j - S0) + 1)

            def result(i):
                c, t = i // CT, i % CT
                b, hf = c // NH, c % NH
                dve.wait_ge(s_f, i + 1)
                dst = X[:, b, t, hf * HALF:(hf + 1) * HALF].rearrange("p (t q n) -> p q t n", t=CH, n=GN)
                dve.tensor_tensor(dst, bank[4 + t % 2][:].rearrange("p (q t n) -> p q t n", q=NG, t=CH),
                                  dst, ALU.add).then_inc(s_fo, 1)

            xT_low(AB - 1)
            for i in range(CHUNKS * CT):
                for n, q in enumerate(tail_groups(i)):
                    onehots(q)
                    if n == 1 and i:
                        result(i - 1)
                    if n == 3 and i < AB:
                        xT_low(AB + i)
                if i and len(tail_groups(i)) <= 1:
                    result(i - 1)
                if i < AB and len(tail_groups(i)) <= 3:
                    xT_low(AB + i)
            result(CHUNKS * CT - 1)

        @block.tensor
        def _(pe):
            def w_turn(n):
                i, t = 1 - n // CT, n % CT
                pe.wait_ge(s_w, 16 * (n // CT + 1))
                if n == CT:
                    pe.wait_ge(s_wl, CT)
                    pe.wait_ge(s_nbr, 4)
                if n % CT == 2:
                    pe.wait_ge(s_nsq, 2 * (n // CT + 1))
                for o in range(CT):
                    mm = pe.transpose(w_bank(n)[:, o * P:(o + 1) * P],
                                      w_raw[i][:, o, t * P:(t + 1) * P], ident[:])
                mm.then_inc(s_wps, 1)

            def norms(b):
                if b == 0:
                    for i in range(2):
                        pe.wait_ge(s_add[i], KT // 2 - 1)
                else:
                    pe.wait_ge(s_add[0], KT // 2 - 1 + KT - 1)
                    pe.wait_ge(s_wl, CT)
                sums = acc if b == 0 else acc[:1]
                for hf in range(NH):
                    for i, a in enumerate(sums):
                        mm = pe.matmul(bank[4 + hf][:], neg_half[:], a[:, hf * HALF:(hf + 1) * HALF],
                                       start=(i == 0), stop=(i == len(sums) - 1))
                    mm.then_inc(s_sqmm, 1)

            def gram(T):
                b, t = T // NT, T % NT
                if T >= 2:
                    pe.wait_ge(s_gc, 2 * (T - 1))
                for k in range(KT):
                    if t == 0:
                        if b and k >= KT - 2:
                            pe.wait_ge(s_pl2, k - KT + 3)
                        else:
                            pe.wait_ge((s_pl0, s_pl1)[b], k + 1)
                    rows = slice(t * P, (t + 1) * P)
                    for hf in range(NH):
                        cols = slice(hf * HALF, (hf + 1) * HALF)
                        o = bank[2 * (T % 2) + hf][:]
                        pe.matmul(o, pts_h[:, k, rows], pts_h[:, k, cols], start=(k == 0), stop=False)
                        pe.matmul(o, pts_h[:, k, rows], pts_l[:, k, cols], start=False, stop=False)
                        mm = pe.matmul(o, pts_l[:, k, rows], pts_h[:, k, cols], start=False,
                                       stop=(k == KT - 1))
                    if T == NT - 1:
                        mm.then_inc(s_kdone, 1)
                if T != NT - 1:
                    mm.then_inc(s_g, 1)

            def adj_turn(T):
                pe.wait_ge(s_diag, T + 1)
                if T in (0, 4):
                    pe.wait_ge(s_wl, CT if T == 0 else 2 * CT)
                if T >= 2:
                    pe.wait_ge(s_nbr, T - 1)
                for m in range(NT):
                    mm = pe.transpose(bank[6 + T % 2][:].bitcast(BF16)[:, m * P:(m + 1) * P],
                                      adj[:, T % 2, m * P:(m + 1) * P], ident_b[:])
                mm.then_inc(s_adjT, 1)

            pe.wait_ge(s_const, 8 + CH)
            gram(0)
            norms(0)
            gram(1)
            for n in range(CT):
                w_turn(n)
            gram(2)
            adj_turn(0)
            gram(3)
            adj_turn(1)
            gram(4)
            gram(5)
            adj_turn(2)
            adj_turn(3)
            norms(1)
            gram(6)
            for n in range(CT, 2 * CT):
                w_turn(n)
            gram(7)
            adj_turn(4)
            adj_turn(5)
            gram(8)
            adj_turn(6)
            adj_turn(7)
            gram(9)
            gram(10)
            adj_turn(8)
            adj_turn(9)
            gram(11)
            gram(12)
            gram(13)
            adj_turn(10)
            adj_turn(11)
            gram(14)
            gram(15)
            adj_turn(12)
            adj_turn(13)

            def wp(g):
                it, m = g // NT, g % NT
                if m in (0, NT // 2):
                    pe.wait_ge(s_p1, 2 * CT * it + (CT if m == 0 else 2 * CT))
                if g == 2 * NT:
                    pe.wait_ge(s_wback, 16)
                if g >= 3:
                    pe.wait_ge(s_yl, g - 2)
                else:
                    pe.wait_ge(s_gc, 2 * TILES - (2 if g < 2 else 0))
                cols = slice(m * P, (m + 1) * P)
                for t in range(CT):
                    pe.matmul(bank[g % 3][:], p_h[:, t, cols], wT[:, 0, t, :], start=(t == 0), stop=False)
                    pe.matmul(bank[g % 3][:], p_h[:, t, cols], wT[:, 1, t, :], start=False, stop=False)
                    mm = pe.matmul(bank[g % 3][:], p_l[:, t, cols], wT[:, 0, t, :], start=False,
                                   stop=(t == CT - 1))
                mm.then_inc(s_wm, 1)

            def aggregate(g):
                it, j = g // (2 * CT), g % (2 * CT)
                b, hf, t = it % B, j // CT, j % CT
                if it < B and j == 0:
                    pe.wait_ge(s_nbr, NT * (it + 1))
                if g >= 3:
                    pe.wait_ge(s_xu, g - 2)
                for m in range(NT):
                    if j == 0:
                        pe.wait_ge(s_yl, NT * it + m + 1)
                    for part_, y in enumerate((y_h, y_l)):
                        mm = pe.matmul(bank[3 + g % 3][:], y[:, m, t * P:(t + 1) * P],
                                       nbr[:, b, m, hf * HALF:(hf + 1) * HALF],
                                       start=(m == 0 and part_ == 0), stop=(m == NT - 1 and part_ == 1))
                mm.then_inc(s_m, 1)

            def turn_a(c):
                pe.wait_ge(s_af, c + 1)
                if c:
                    pe.wait_ge(s_ar, c)
                    pe.wait_ge(s_pick, 8 * c + R0 - G0 + 1)
                else:
                    pe.wait_ge(s_nbr, TILES)
                pe.transpose(bank[6][:, 384:HALF], a_f, ident[:]).then_inc(s_aT, 1)

            def lookup(u):
                pe.wait_ge(s_oh, u + 1)
                if u == 0:
                    pe.wait_ge(s_tab, 1)
                if u >= 2:
                    pe.wait_ge(s_pick, u - 1)
                pe.wait_ge(s_ar, min((u + G0 - R0 - 2) // 8 + 1, CHUNKS))
                b = u // (2 * NT)
                for k in range(KH):
                    for i in range(3):
                        mm = pe.matmul(bank[6 + u % 2][:, k * 3 * AB:(k + 1) * 3 * AB],
                                       bc[:, u % NB, k * P:(k + 1) * P],
                                       tab_p[:, i, b].rearrange("p j r -> p (j r)"),
                                       start=(i == 0), stop=(i == 2))
                mm.then_inc(s_look, 1)

            def bn_sum(layer, n):
                pe.wait_ge(s_bnin, layer)
                pe.matmul(bank[7][:, 480:480 + 2 * n], mean_mat[:], stat[:, 0:2 * n],
                          start=True, stop=True).then_inc(s_bnps, 1)

            def side(g):
                if g == SEL0 + 4:
                    adj_turn(TILES - 2)
                    adj_turn(TILES - 1)
                if G0 < g <= G0 + 2 * TILES:
                    lookup(g - G0 - 1)
                if (g - R0) % 8 == 2 and 0 <= (g - R0) // 8 < CHUNKS:
                    turn_a((g - R0) // 8)
                m = NET[g - M0] if M0 <= g < M0 + len(NET) else None
                if m == 24:
                    bn_sum(1, 6)
                if m == 37:
                    bn_sum(2, 3)
                if m == 44:
                    bn_sum(3, 1)
                if g == T0 + 1:
                    turn_att()
                if g > S0:
                    spread(2 * (g - S0) - 1)
                if g >= 16 * ITS - AB:
                    turn_x(g - 16 * ITS + AB)

            def turn_att():
                pe.wait_ge(s_att, 1)
                for c in range(CHUNKS):
                    mm = pe.transpose(bank[6][:, c * P:(c + 1) * P], a_all[:, c * P:(c + 1) * P], ident[:])
                mm.then_inc(s_scT, 1)
                for c in range(CHUNKS):
                    mm = pe.transpose(bank[7][:, c * P:(c + 1) * P], r4_all[:, c * P:(c + 1) * P], ident[:])
                mm.then_inc(s_scT, 1)
                pe.wait_ge(s_sct, 1)
                for c in range(CHUNKS):
                    mm = pe.transpose(bank[6][:, c * P:(c + 1) * P],
                                      att32[:, CH * c:CH * (c + 1), :].rearrange("p t k -> p (t k)"), ident[:])
                mm.then_inc(s_scT, 1)

            def spread(q):
                pe.wait_ge(s_oa, q + 1)
                pe.wait_ge(s_mv[0], q + 1)
                pe.wait_ge(s_mv[1], q + 1)
                if q == 0:
                    pe.wait_ge(s_attq, CHUNKS)
                if q >= 2:
                    pe.wait_ge(s_scc, q - 1)
                for n in range(GN):
                    for i in range(2):
                        mm = pe.matmul(bank[6 + q % 2][:, n * 2 * KP:(n + 1) * 2 * KP], oa[q % 2][:, :, n],
                                       mv[q % 2][:, i, :, :, n].rearrange("p h r -> p (h r)"),
                                       start=(i == 0), stop=(i == 1))
                mm.then_inc(s_sc, 1)

            def turn_x(n):
                if n == 0:
                    pe.wait_ge(s_yl, NT * ITS)
                    pe.wait_ge(s_xu, 2 * CT * (ITS - 1))
                if n == AB:
                    pe.wait_ge(s_xu, 2 * CT * ITS)
                if n >= 2:
                    pe.wait_ge(s_xTl, n - 1)
                b, r = n // AB, n % AB
                for t in range(CT):
                    mm = pe.transpose(bank[n % 2][:, t * P:(t + 1) * P], X[:, b, t, r:N:AB], ident[:])
                mm.then_inc(s_xT, 1)

            for it in range(ITS):
                for m in range(NT):
                    if 16 * it + m > S0:
                        spread(2 * (16 * it + m - S0) - 2)
                    wp(NT * it + m)
                    side(16 * it + m)
                for j in range(2 * CT):
                    if 16 * it + NT + j > S0:
                        spread(2 * (16 * it + NT + j - S0) - 2)
                    aggregate(2 * CT * it + j)
                    side(16 * it + NT + j)

            def attend(i):
                c, t = i // CT, i % CT
                b = c // NH
                if t == 0:
                    pe.wait_ge(s_back[c], 16 * 4)
                    pe.wait_ge(s_xTl, AB * (b + 1))
                if i >= 2:
                    pe.wait_ge(s_fo, i - 1)
                else:
                    pe.wait_ge(s_xu, 2 * CT * ITS)
                beside = list(tail_groups(i))
                for r in range(AB):
                    if r % 2 and r // 2 < len(beside):
                        spread(beside[r // 2])
                    if r == 3 and i < AB:
                        turn_x(AB + i)
                    o = bank[4 + t % 2][:]
                    lhs = [xT[b][:, h, r, t * P:(t + 1) * P] for h in range(2)]
                    rhs = [att_T[c % 2][:, h, r] for h in range(2)]
                    pe.matmul(o, lhs[0], rhs[0], start=(r == 0), stop=False)
                    pe.matmul(o, lhs[0], rhs[1], start=False, stop=False)
                    mm = pe.matmul(o, lhs[1], rhs[0], start=False, stop=(r == AB - 1))
                mm.then_inc(s_f, 1)

            spread(S_END - 2)
            spread(S_END - 1)
            for i in range(CHUNKS * CT):
                attend(i)



_INS = ["x", "ctx_4096", "fside_BxSxS_0", "L1_xattn_W1", "L1_xattn_g1", "L1_xattn_b1", "L1_xattn_W2",
        "L1_xattn_g2", "L1_xattn_b2", "L1_xattn_W3", "L1_xattn_g3", "L1_xattn_b3"]


def kernel(**inputs):
    import concourse.bacc as bacc
    from concourse.bass_utils import run_bass_kernel_spmd

    nc = bacc.Bacc("TRN2", target_bir_lowering=False, num_devices=1)
    arrays, args = {}, []
    for name in _INS:
        a = np.ascontiguousarray(inputs[name])
        arrays[f"in_{name}"] = a
        args.append(nc.dram_tensor(f"in_{name}", a.shape, mybir.dt.from_np(a.dtype), kind="ExternalInput").ap())
    shape = arrays["in_x"].shape
    out = nc.dram_tensor("out_dram", shape, F32, kind="ExternalOutput").ap()
    build(nc, *args, out)
    r = run_bass_kernel_spmd(nc, [arrays], core_ids=[0])
    return r.results[0]["out_dram"]
```
